# Optimizing a Trainium2 kernel written in Bass

```python
import numpy as np
import jax
import jax.numpy as jnp

def _softmax(x, axis=-1):
    return jax.nn.softmax(x, axis=axis)

def _gelu(x):
    return jax.nn.gelu(x, approximate=True)

def _silu(x):
    return jax.nn.silu(x)

def _sigmoid(x):
    return jax.nn.sigmoid(x)

def _layernorm(x, axis=-1, eps=1e-05):
    m = jnp.mean(x, axis=axis, keepdims=True)
    v = jnp.var(x, axis=axis, keepdims=True)
    return (x - m) / jnp.sqrt(v + eps)

def _scatter_add(tgt, idx, src, axis=0):
    return tgt.at[idx].add(src)

def _segment_sum(src, seg, n):
    return jax.ops.segment_sum(src, seg, n)
kernel_name = 'mk_flamingo_gated_d2_seqx_r8_8a1083'

def setup_inputs(seed: int=0):
    np.random.seed(seed)
    _w = jnp.asarray

    def _rec_inputs():
        import jax
        import jax.numpy as jnp
        _rk = jax.random.key(seed)
        x = -0.000125 + 0.9999 * jax.random.normal(jax.random.fold_in(_rk, 1), (8, 128, 256), jnp.float32)
        _lenS = 128 - jax.random.randint(jax.random.fold_in(_rk, 7), (8,), 0, max(1, 128 // 4) + 1, jnp.int32)
        _lenS2 = 128 - jax.random.randint(jax.random.fold_in(_rk, 8), (8,), 0, max(1, 128 // 4) + 1, jnp.int32)
        _ctx_2048P = jax.random.normal(jax.random.fold_in(_rk, 11), (8, 16, 256), jnp.float32)
        _ctx_2048c = jax.random.dirichlet(jax.random.fold_in(_rk, 511), 0.3 * jnp.ones((16,), jnp.float32), (8, 128))
        _ctx_2048t = jnp.einsum('bsk,bkd->bsd', _ctx_2048c, _ctx_2048P)
        _ctx_2048t = _ctx_2048t * jax.lax.rsqrt(jnp.mean(jnp.square(_ctx_2048t)) + 1e-12) * 0.953939
        ctx_2048 = 1.72703e-05 + 1.00003 * (_ctx_2048t + 0.3 * jax.random.normal(jax.random.fold_in(_rk, 611), (8, 128, 256), jnp.float32))
        _validS = jnp.arange(128)[None, :] < _lenS[:, None]
        _validS2 = jnp.arange(128)[None, :] < _lenS2[:, None]
        _causal = jnp.tril(jnp.ones((128, 128), dtype=bool))
        mask_BxS2_bk0 = jnp.logical_not(jnp.broadcast_to(_validS2[:, :], (8, 128)))
        _g = jax.random.normal(jax.random.fold_in(_rk, 9001), (2, 2), jnp.float32)
        _g = jnp.sign(_g) * jnp.maximum(jnp.abs(_g), 1.0) + (_g == 0) * 1.0
        g_xattn = _g[0]
        g_ffn = _g[1]
        return (x, ctx_2048, mask_BxS2_bk0, g_xattn, g_ffn)
    x, ctx_2048, mask_BxS2_bk0, g_xattn, g_ffn = _rec_inputs()

    def _L0_xattn_setup():
        import jax, jax.numpy as jnp
        import numpy as np
        DIM = 256
        NH = 16
        HD = DIM // NH
        EPS = 1e-06
        IMG_LEN = 257

        def rms_norm(x, w, eps=EPS):
            xf = x.astype(jnp.float32)
            y = xf * jax.lax.rsqrt(jnp.mean(xf * xf, axis=-1, keepdims=True) + eps)
            return y.astype(x.dtype) * w

        def linear(x, w, b):
            return jnp.einsum('blc,oc->blo', x, w) + b

        def attention(q, k, v):
            scale = 1.0 / jnp.sqrt(jnp.asarray(HD, q.dtype))
            scores = jnp.einsum('bqhd,bkhd->bhqk', q, k) * scale
            probs = jax.nn.softmax(scores, axis=-1)
            return jnp.einsum('bhqk,bkhd->bqhd', probs, v)
        key = jax.random.key(seed)
        ks = jax.random.split(key, 12)
        B, L = (2, 1024)
        s = 0.02
        inp = {'x': jax.random.normal(ks[0], (B, L, DIM), jnp.float32), 'context': jax.random.normal(ks[1], (B, 769, DIM), jnp.float32), 'q_w': jax.random.normal(ks[2], (DIM, DIM), jnp.float32) * s, 'q_b': jnp.zeros((DIM,), jnp.float32), 'k_w': jax.random.normal(ks[3], (DIM, DIM), jnp.float32) * s, 'k_b': jnp.zeros((DIM,), jnp.float32), 'v_w': jax.random.normal(ks[4], (DIM, DIM), jnp.float32) * s, 'v_b': jnp.zeros((DIM,), jnp.float32), 'k_img_w': jax.random.normal(ks[5], (DIM, DIM), jnp.float32) * s, 'k_img_b': jnp.zeros((DIM,), jnp.float32), 'v_img_w': jax.random.normal(ks[6], (DIM, DIM), jnp.float32) * s, 'v_img_b': jnp.zeros((DIM,), jnp.float32), 'o_w': jax.random.normal(ks[7], (DIM, DIM), jnp.float32) * s, 'o_b': jnp.zeros((DIM,), jnp.float32), 'norm_q_w': jnp.ones((DIM,), jnp.float32), 'norm_k_w': jnp.ones((DIM,), jnp.float32), 'norm_k_img_w': jnp.ones((DIM,), jnp.float32)}
        return inp
    _L0_xattn_all = _L0_xattn_setup()
    _L0_xattn_in = {k: v for k, v in _L0_xattn_all.items() if k in ('q_w', 'q_b', 'k_w', 'k_b', 'v_w', 'v_b', 'k_img_w', 'k_img_b', 'v_img_w', 'v_img_b', 'o_w', 'o_b', 'norm_q_w', 'norm_k_w', 'norm_k_img_w')}
    del _L0_xattn_all

    def _L0_ffn_setup():
        import jax, jax.numpy as jnp
        import numpy as np
        HIDDEN = 256
        INTER = 1024
        BATCH, LOCAL_SEQ = (2, 512)
        key = jax.random.key(seed)
        k1, k2, k3 = jax.random.split(key, 3)
        h_shard = jax.random.normal(k1, (BATCH, LOCAL_SEQ, HIDDEN), dtype=jnp.float32)
        w_gate_up = jax.random.normal(k2, (2 * INTER, HIDDEN), dtype=jnp.float32) * 0.02
        w_down = jax.random.normal(k3, (HIDDEN, INTER), dtype=jnp.float32) * 0.02
        return {'h_shard': h_shard, 'w_gate_up': w_gate_up, 'w_down': w_down}
    _L0_ffn_all = _L0_ffn_setup()
    _L0_ffn_in = {k: v for k, v in _L0_ffn_all.items() if k in ('w_gate_up', 'w_down')}
    del _L0_ffn_all

    def _L1_xattn_setup():
        import jax, jax.numpy as jnp
        import numpy as np
        key = jax.random.key(seed)
        k1, k2, k3 = jax.random.split(key, 3)
        B, S, D, M = (8, 256, 256, 128)
        hidden_states = jax.random.normal(k1, (B, S, D), dtype=jnp.float32)
        memory_tokens = jax.random.normal(k2, (B, M, D), dtype=jnp.float32)
        memory_mask = jax.random.randint(k3, (B, M), 0, 2).astype(jnp.bool_)
        return {'hidden_states': hidden_states, 'memory_tokens': memory_tokens, 'memory_mask': memory_mask}
    _L1_xattn_all = _L1_xattn_setup()
    _L1_xattn_in = {k: v for k, v in _L1_xattn_all.items() if k in ()}
    del _L1_xattn_all

    def _L1_ffn_setup():
        import jax, jax.numpy as jnp
        import numpy as np
        N_BLOCKS = 16
        BLOCK_SIZE = 64
        TOP_K = N_BLOCKS // 4
        key = jax.random.key(seed)
        k1, k2, k3, k4, k5 = jax.random.split(key, 5)
        in_f, out_f = (256, 1024)
        x = jax.random.normal(k1, (2, 512, in_f), dtype=jnp.float32)
        Wr = jax.random.normal(k2, (N_BLOCKS, in_f), dtype=jnp.float32) * in_f ** (-0.5)
        br = jnp.zeros((N_BLOCKS,), dtype=jnp.float32)
        W1 = jax.random.normal(k3, (out_f, in_f), dtype=jnp.float32) * in_f ** (-0.5)
        W2 = jax.random.normal(k4, (in_f, out_f), dtype=jnp.float32) * out_f ** (-0.5)
        return {'x': x, 'Wr': Wr, 'br': br, 'W1': W1, 'W2': W2}
    _L1_ffn_all = _L1_ffn_setup()
    _L1_ffn_in = {k: v for k, v in _L1_ffn_all.items() if k in ('Wr', 'br', 'W1', 'W2')}
    del _L1_ffn_all
    return {'x': x, 'ctx_2048': ctx_2048, 'mask_BxS2_bk0': mask_BxS2_bk0, 'g_xattn': g_xattn, 'g_ffn': g_ffn, 'L0_xattn_q_w': _L0_xattn_in['q_w'], 'L0_xattn_q_b': _L0_xattn_in['q_b'], 'L0_xattn_k_w': _L0_xattn_in['k_w'], 'L0_xattn_k_b': _L0_xattn_in['k_b'], 'L0_xattn_v_w': _L0_xattn_in['v_w'], 'L0_xattn_v_b': _L0_xattn_in['v_b'], 'L0_xattn_k_img_w': _L0_xattn_in['k_img_w'], 'L0_xattn_k_img_b': _L0_xattn_in['k_img_b'], 'L0_xattn_v_img_w': _L0_xattn_in['v_img_w'], 'L0_xattn_v_img_b': _L0_xattn_in['v_img_b'], 'L0_xattn_o_w': _L0_xattn_in['o_w'], 'L0_xattn_o_b': _L0_xattn_in['o_b'], 'L0_xattn_norm_q_w': _L0_xattn_in['norm_q_w'], 'L0_xattn_norm_k_w': _L0_xattn_in['norm_k_w'], 'L0_xattn_norm_k_img_w': _L0_xattn_in['norm_k_img_w'], 'L0_ffn_w_gate_up': _L0_ffn_in['w_gate_up'], 'L0_ffn_w_down': _L0_ffn_in['w_down'], 'L1_ffn_Wr': _L1_ffn_in['Wr'], 'L1_ffn_br': _L1_ffn_in['br'], 'L1_ffn_W1': _L1_ffn_in['W1'], 'L1_ffn_W2': _L1_ffn_in['W2']}

def reference(x, ctx_2048, mask_BxS2_bk0, g_xattn, g_ffn, L0_xattn_q_w, L0_xattn_q_b, L0_xattn_k_w, L0_xattn_k_b, L0_xattn_v_w, L0_xattn_v_b, L0_xattn_k_img_w, L0_xattn_k_img_b, L0_xattn_v_img_w, L0_xattn_v_img_b, L0_xattn_o_w, L0_xattn_o_b, L0_xattn_norm_q_w, L0_xattn_norm_k_w, L0_xattn_norm_k_img_w, L0_ffn_w_gate_up, L0_ffn_w_down, L1_ffn_Wr, L1_ffn_br, L1_ffn_W1, L1_ffn_W2):
    import jax
    import jax.numpy as jnp

    def _L0_xattn_ref(x, context, q_w, q_b, k_w, k_b, v_w, v_b, k_img_w, k_img_b, v_img_w, v_img_b, o_w, o_b, norm_q_w, norm_k_w, norm_k_img_w):
        import jax, jax.numpy as jnp
        import numpy as np
        DIM = 256
        NH = 16
        HD = DIM // NH
        EPS = 1e-06
        IMG_LEN = 257

        def rms_norm(x, w, eps=EPS):
            xf = x.astype(jnp.float32)
            y = xf * jax.lax.rsqrt(jnp.mean(xf * xf, axis=-1, keepdims=True) + eps)
            return y.astype(x.dtype) * w

        def linear(x, w, b):
            return jnp.einsum('blc,oc->blo', x, w) + b

        def attention(q, k, v):
            scale = 1.0 / jnp.sqrt(jnp.asarray(HD, q.dtype))
            scores = jnp.einsum('bqhd,bkhd->bhqk', q, k) * scale
            probs = jax.nn.softmax(scores, axis=-1)
            return jnp.einsum('bhqk,bkhd->bqhd', probs, v)
        B, L, _ = x.shape
        ctx_img = context[:, :IMG_LEN]
        ctx_txt = context[:, IMG_LEN:]
        q = rms_norm(linear(x, q_w, q_b), norm_q_w).reshape(B, L, NH, HD)
        k = rms_norm(linear(ctx_txt, k_w, k_b), norm_k_w).reshape(B, -1, NH, HD)
        v = linear(ctx_txt, v_w, v_b).reshape(B, -1, NH, HD)
        k_img = rms_norm(linear(ctx_img, k_img_w, k_img_b), norm_k_img_w).reshape(B, -1, NH, HD)
        v_img = linear(ctx_img, v_img_w, v_img_b).reshape(B, -1, NH, HD)
        img_x = attention(q, k_img, v_img)
        txt_x = attention(q, k, v)
        out = (txt_x + img_x).reshape(B, L, DIM)
        return linear(out, o_w, o_b)

    def _L0_ffn_ref(h_shard, w_gate_up, w_down):
        import jax, jax.numpy as jnp
        import numpy as np
        HIDDEN = 256
        INTER = 1024
        BATCH, LOCAL_SEQ = (2, 512)
        batch, local_seq, hidden = h_shard.shape
        gate_up = jnp.einsum('bsh,oh->bso', h_shard, w_gate_up)
        gate, up = jnp.split(gate_up, 2, axis=-1)
        h = jax.nn.silu(gate) * up
        out = jnp.einsum('bsi,hi->bsh', h, w_down)
        return out

    def _L1_xattn_ref(hidden_states, memory_tokens, memory_mask):
        import jax, jax.numpy as jnp
        import numpy as np
        B, S, D = hidden_states.shape
        scale = 1.0 / jnp.sqrt(jnp.asarray(D, hidden_states.dtype))
        scores = jnp.einsum('bsd,bmd->bsm', hidden_states, memory_tokens) * scale
        neg_inf = jnp.asarray(-1e+30, scores.dtype)
        scores = jnp.where(memory_mask[:, None, :], scores, neg_inf)
        attn = jax.nn.softmax(scores, axis=-1)
        readout = jnp.einsum('bsm,bmd->bsd', attn, memory_tokens)
        valid_b = jnp.any(memory_mask, axis=-1)
        out = jnp.where(valid_b[:, None, None], readout, jnp.zeros_like(readout))
        return out

    def _L1_ffn_ref(x, Wr, br, W1, W2):
        import jax, jax.numpy as jnp
        import numpy as np
        N_BLOCKS = 16
        BLOCK_SIZE = 64
        TOP_K = N_BLOCKS // 4
        x_shape = x.shape
        in_f = x_shape[-1]
        xf = x.reshape(-1, in_f)
        n = xf.shape[0]
        prob = jax.nn.softmax(xf @ Wr.T + br, axis=-1)
        _, idx = jax.lax.top_k(prob, TOP_K)
        mask = jnp.zeros((n, N_BLOCKS), dtype=xf.dtype)
        mask = mask.at[jnp.arange(n)[:, None], idx].set(1.0)
        W1b = W1.reshape(N_BLOCKS, BLOCK_SIZE, in_f)
        h = jnp.einsum('nf,ibf->nib', xf, W1b)
        h = jax.nn.gelu(h, approximate=False) * mask[:, :, None]
        W2b = W2.reshape(in_f, N_BLOCKS, BLOCK_SIZE)
        y = jnp.einsum('nib,fib->nf', h, W2b)
        return y.reshape(x_shape)
    x = x + jnp.tanh(g_xattn[0]) * _L0_xattn_ref(_layernorm(x, axis=-1), ctx_2048, L0_xattn_q_w, L0_xattn_q_b, L0_xattn_k_w, L0_xattn_k_b, L0_xattn_v_w, L0_xattn_v_b, L0_xattn_k_img_w, L0_xattn_k_img_b, L0_xattn_v_img_w, L0_xattn_v_img_b, L0_xattn_o_w, L0_xattn_o_b, L0_xattn_norm_q_w, L0_xattn_norm_k_w, L0_xattn_norm_k_img_w)
    x = x + jnp.tanh(g_ffn[0]) * _L0_ffn_ref(_layernorm(x, axis=-1), L0_ffn_w_gate_up, L0_ffn_w_down)
    x = x + jnp.tanh(g_xattn[1]) * _L1_xattn_ref(_layernorm(x, axis=-1), ctx_2048, mask_BxS2_bk0)
    x = x + jnp.tanh(g_ffn[1]) * _L1_ffn_ref(_layernorm(x, axis=-1), L1_ffn_Wr, L1_ffn_br, L1_ffn_W1, L1_ffn_W2)
    return x

_drawn_inputs = setup_inputs


def setup_inputs(seed=0):
    import zlib

    import numpy as np

    out = dict(_drawn_inputs(seed))
    spreads = {'g_ffn': (-1.0, 0.6),
     'L0_xattn_q_b': (0.0, 2.0),
     'L0_xattn_k_b': (0.0, 0.1),
     'L0_xattn_v_b': (0.0, 0.1),
     'L0_xattn_k_img_b': (0.0, 0.8),
     'L0_xattn_v_img_b': (0.0, 0.1),
     'L0_xattn_o_b': (0.0, 0.1),
     'L0_xattn_norm_q_w': (1.0, 0.6),
     'L0_xattn_norm_k_w': (1.0, 0.2),
     'L0_xattn_norm_k_img_w': (1.0, 0.6),
     'L1_ffn_br': (0.0, 0.1)}
    factors = {'L0_xattn_q_w': 8.708}
    for name, (base, spread) in spreads.items():
        noise = np.random.default_rng([zlib.crc32(name.encode()), seed]).standard_normal(out[name].shape)
        drawn = base * np.exp(spread * noise) if base else spread * noise
        out[name] = jnp.asarray(drawn.astype(out[name].dtype))
    for name, factor in factors.items():
        out[name] = (out[name] * factor).astype(out[name].dtype)
    return out
```

```python
import concourse.bass as bass
from concourse import mybir
from contextlib import ExitStack


def build(nc, x_d, ctx_d, ctxT_d, mask_d, gx_d, gf_d, wq_d, qb_d, wkv_d, kb_d, vb_d, wo_d, ob_d,
          nq_d, nk_d, wgu_d, wd_d, wr_d, br_d, w1_d, w2_d, out_d):
    f32, f32r, f16, bf16, u8 = (mybir.dt.float32, mybir.dt.float32r, mybir.dt.float16,
                                mybir.dt.bfloat16, mybir.dt.uint8)
    ALU, ACT, AX = mybir.AluOpType, mybir.ActivationFunctionType, mybir.AxisListType

    P = 128
    NT = x_d.shape[0]
    D = x_d.shape[2]
    KC = D // P
    NP = NT // 2
    PW = 2 * D
    T2 = 2 * P
    NH, HD = 16, 16
    HP = 32
    INTER = wd_d.shape[1] // D * P
    NC = INTER // P
    NB, TOPK, BLK = 16, 4, 64
    MASKED = -1e30 * D ** 0.5
    UNPICKED = -1e30
    EXP_LOW = -87.3365
    PAD = -1e30

    ctx = ExitStack()
    with ctx:
        def sb(name, shape, dt=f32):
            return ctx.enter_context(nc.sbuf_tensor(name, shape, dt))

        def sem(name):
            return ctx.enter_context(nc.semaphore(name))

        xs = sb("xs", [P, NT * D])
        cs = sb("cs", [P, NT * D])
        csT = sb("csT", [P, NT * D])
        PIECE, RING = 512, 3
        raw = [sb(f"raw{i}", [P, PIECE]) for i in range(RING)]
        NQ, NKV = KC * D, KC * 2 * D
        wgu_hi, wgu_lo = sb("wgu_hi", [P, KC * 2 * INTER], f32r), sb("wgu_lo", [P, KC * 2 * INTER], f32r)
        wd_hi, wd_lo = sb("wd_hi", [P, NC * D], f32r), sb("wd_lo", [P, NC * D], f32r)
        wr_hi, wr_lo = sb("wr_hi", [P, KC * P], f32r), sb("wr_lo", [P, KC * P], f32r)
        W2O = KC * INTER
        qb, kb, vb = sb("qb", [P, D]), sb("kb", [P, D]), sb("vb", [P, D])
        ob2 = sb("ob2", [P, PW])
        nqk = sb("nqk", [P, 2 * D])
        wn = sb("wn", [P, D])
        wn_max, wn_inv, sc_exp = sb("wn_max", [P, 1]), sb("wn_inv", [P, 1]), sb("sc_exp", [P, 1])
        br_col = sb("br_col", [HP, 1])
        graw, gate = sb("graw", [P, 4]), sb("gate", [P, 4])
        gf0_half = sb("gf0_half", [P, 1])
        mask_words = sb("mask_words", [P, NT * P // 4], mybir.dt.uint32)
        mask_all = mask_words[:].bitcast(u8)
        valid = sb("valid", [P, NT])
        neg_half = sb("neg_half", [P, 4])
        ident = sb("ident", [P, P])
        ident16, identb = sb("ident16", [P, P], f16), sb("identb", [P, P], bf16)
        pick_row = sb("pick_row", [P, 8 * P], f16)
        spread = sb("spread", [P, NC * P], bf16)

        bn_a, var_a, vare_a, rstd_a = sb("bn_a", [P, 12]), sb("var_a", [P, 4]), sb("vare_a", [P, 2]), sb("rstd_a", [P, 2])
        ssq, msq, rms = sb("ssq", [P, 4]), sb("msq", [P, 4]), sb("rms", [P, 4])
        mx = sb("mx", [P, 2 * NH])
        nm16 = sb("nm16", [P, 2 * P], f16)
        mT = sb("mT", [P, 2 * P], f16)
        rden = sb("rden", [P, 2 * NH])
        x1 = sb("x1", [P, PW])
        bn_f, var_f, vare_f, rstd_f = sb("bn_f", [P, 12]), sb("var_f", [P, 4]), sb("vare_f", [P, 2]), sb("rstd_f", [P, 2])
        xn_f = sb("xn_f", [P, PW])
        fT_hi, fT_lo = sb("fT_hi", [P, PW], f32r), sb("fT_lo", [P, PW], f32r)
        th, uu = sb("th", [P, 2 * T2]), sb("uu", [P, 2 * T2])
        HB = 4
        HF = 2
        hf = sb("hf", [P, HF * T2])
        h_hi, h_lo = sb("h_hi", [P, HB * T2], f32r), sb("h_lo", [P, HB * T2], f32r)
        x2 = x1
        bn_l, var_l, vare_l, rstd_l = sb("bn_l", [P, 12]), sb("var_l", [P, 4]), sb("vare_l", [P, 2]), sb("rstd_l", [P, 2])
        xn_l = xn_f
        lT = sb("lT", [P, 2 * KC * P])
        mask2 = sb("mask2", [P, T2], u8)
        sc = sb("sc", [P, T2])
        nmx, nmx_s, den = sb("nmx", [P, 2]), sb("nmx_s", [P, 2]), sb("den", [P, 2])
        pl, plT = sb("pl", [P, T2]), sb("plT", [P, T2])
        rec, coef = sb("rec", [P, 2]), sb("coef", [P, 2])
        bn_b, var_b, vare_b, rstd_b = sb("bn_b", [P, 12]), sb("var_b", [P, 4]), sb("vare_b", [P, 2]), sb("rstd_b", [P, 2])
        t8, rep = sb("t8", [P, 16]), sb("rep", [P, 16])
        lgv, mr = sb("lgv", [P, 2 * 24]), sb("mr", [P, 2 * 24])
        pen = sb("pen", [P, T2], bf16)
        with ExitStack() as place:
            def sa(name, shape, dt=f32):
                return place.enter_context(nc.sbuf_tensor(name, shape, dt))
            whi_a, wlo_a = sa("whi_a", [P, KC * 4 * D], f32r), sa("wlo_a", [P, KC * 4 * D], f32r)
            xn_a = sa("xn_a", [P, PW])
            attn = xn_a
            aT_hi, aT_lo = sa("aT_hi", [P, PW], f32r), sa("aT_lo", [P, PW], f32r)
            oT_hi, oT_lo = aT_hi, aT_lo
            c_hi, c_lo = sa("c_hi", [P, PW], f32r), sa("c_lo", [P, PW], f32r)
            q_pre, k_pre = sa("q_pre", [P, 2 * D]), sa("k_pre", [P, 2 * D])
            qn, kn = q_pre, k_pre
            junk = sa("junk", [P, D])
            v_aug = sa("v_aug", [P, 2 * NH * HP])
            q16, k16 = sa("q16", [P, 2 * 4 * D], f16), sa("k16", [P, 2 * 4 * D], f16)
            QT, KT = sa("QT", [P, 2 * 8 * P], f16), sa("KT", [P, 2 * 8 * P], f16)
            PTs = sa("PTs", [P, 2 * 8 * P])
            PT = [PTs[:, 0:8 * P], PTs[:, 8 * P:]]
            raw_qkvo = PTs
            po = sa("po", [P, 2 * 4 * P])
        with ExitStack() as place:
            w12_hi, w12_lo = sa("w12_hi", [P, KC * INTER + NC * D], f32r), sa("w12_lo", [P, KC * INTER + NC * D], f32r)
            xn_b = sa("xn_b", [P, PW])
            bT_hi, bT_lo = sa("bT_hi", [P, NP * PW], f32r), sa("bT_lo", [P, NP * PW], f32r)
            lgT = sa("lgT", [HP, T2])
            penT = sa("penT", [P, NP * T2], bf16)

        def bank(name, cols=512):
            return ctx.enter_context(nc.psum_tensor(name, [P, cols], f32))
        G = [bank("G0"), bank("G1")]
        DN = bank("DN")
        W = [bank("W0", 1024), bank("W1", 1024)]
        M = bank("M")

        S = {n: sem(n) for n in """
            x_in ctx_in ctxT_in wqkvo_in rows_in mask_in stores
            consts rows_ready gates_ready ident_ready patterns_ready wa_split piece_split
            a_stats a_var a_vare a_rstd a_xn a_T a_hi a_lo c_hi_done c_split
            qkv_done q_pre_done k_pre_done v_done ss_done msq_done rms_done qn_done kn_done q16_hi k16_hi q16_lo k16_lo
            qkT_done QT_done KT_done s_done max_done nm_hi nm_done mT_ps mT_done st_done PT_done pv_done po_done
            oTok_done rden_done attn_done oT_ps oT_hi_done oT_lo_done o_done ob_done x1_done
            f_stats f_var f_vare f_rstd f_xn f_T f_hi f_lo gu_done th_done uu_done hf_done h_hi_done h_lo_done dn_part x2_done
            l_stats l_var l_vare l_rstd l_xn l_T lT_done l_sc mask_sel sc_filled l_sel l_max l_maxs lp_done rec_done coef_done plT_ps plT_done ro_done x3_done
            b_stats b_var b_vare b_rstd b_xn b_T b_hi b_lo rt_ps lg_done lgT_ps t8_done lgv_done rep_done mr_done pen_done penT_ps penT_done
            up_done bf_done bh_hi bh_lo bdn_part x4_done wn_mul wn_abs wn_rec""".split()}

        raw_in = [sem(f"raw_in{i}") for i in range(RING)]
        PIECES = [(wgu_d, i, wgu_hi, wgu_lo, i, PIECE) for i in range(0, KC * 2 * INTER, PIECE)]
        PIECES += [(wd_d, i, wd_hi, wd_lo, i, PIECE) for i in range(0, NC * D, PIECE)]
        PIECES += [(wr_d, 0, wr_hi, wr_lo, 0, KC * P)]
        EARLY = len(PIECES)
        PIECES += [(w1_d, i, w12_hi, w12_lo, i, PIECE) for i in range(0, W2O, PIECE)]
        PIECES += [(w2_d, i, w12_hi, w12_lo, W2O + i, PIECE) for i in range(0, NC * D, PIECE)]

        block = ctx.enter_context(nc.Block())

        BODY = [("A.ln", 0), ("A.T", 0), ("F.ln", 0), ("F.T", 0), ("A.qkv", 0), ("F.up", 0), ("A.qkv", 1), ("F.up", 1),
                ("A.qkT", 0), ("F.up", 2), ("F.dn", 0), ("A.qkT", 1), ("F.up", 3), ("F.dn", 1),
                ("A.s", 0), ("A.s", 1), ("F.up", 4), ("F.dn", 2), ("A.s", 2), ("F.up", 5), ("F.dn", 3), ("A.s", 3), ("A.mT", 0),
                ("F.up", 6), ("F.dn", 4), ("A.mT", 1), ("A.st", 0), ("F.up", 7), ("F.dn", 5), ("A.st", 1), ("F.dn", 6), ("F.dn", 7),
                ("A.pv", 0), ("L.ln", 0), ("A.st", 2), ("L.T", 0), ("A.st", 3), ("L.T", 1), ("L.sc", 0), ("A.oT", 0), ("L.sc", 1), ("A.pv", 1),
                ("L.pT", 0), ("A.oT", 1), ("L.pT", 1), ("L.ro", 0), ("A.aT", 0), ("L.ro", 1), ("A.o", 0), ("L.end", 0)]
        ONLY_A = [s for s in BODY if s[0][0] == "A"]
        REST = [s for s in BODY if s[0][0] != "A"]
        ROUTE = [("R.ln", 0), ("R.T", 0), ("R.rt", 0), ("R.lT", 0), ("R.pT", 0)]
        MIX = [("B.up", 0), ("B.up", 1), ("R.ln", 0), ("B.up", 2), ("B.dn", 0), ("R.T", 0), ("B.up", 3), ("B.dn", 1),
               ("B.up", 4), ("R.rt", 0), ("B.dn", 2), ("B.up", 5), ("R.lT", 0), ("B.dn", 3), ("B.up", 6), ("B.dn", 4), ("B.up", 7),
               ("R.pT", 0), ("B.dn", 5), ("B.dn", 6), ("B.dn", 7)]
        ONLY_B = [s for s in MIX if s[0][0] == "B"]

        def run(eng, steps):
            def go(order, a, r):
                for name, i in order:
                    if name in steps:
                        steps[name](a if name[0] == "A" else r, i)
            go(ONLY_A, 0, None)
            with eng.Fori(1, NP) as p:
                go(BODY, p, p - 1)
            go(REST, None, NP - 1)

            def go_b(order, r, nxt):
                for name, i in order:
                    if name in steps:
                        steps[name](nxt if name[0] == "R" else r, i)
            go_b(ROUTE, None, 0)
            with eng.Fori(0, NP - 1) as r:
                go_b(MIX, r, r + 1)
            go_b(ONLY_B, NP - 1, None)

        def wait_apart(eng, name, value):
            v = value if isinstance(value, int) else eng.snap(value)
            eng.wait_ge(S["consts"], 1)
            eng.wait_ge(S[name], v)

        def parts(which, j, s):
            v = (q16, k16)[which][:, j * 4 * D:(j + 1) * 4 * D].rearrange("p (h a b c) -> p h a b c", a=2, b=2, c=HD)
            return v[:, :, :, s, :] if which else v[:, :, s, :, :]

        def twice(src):
            return src.rearrange("p (h c) -> p h c", c=HD).unsqueeze(2).to_broadcast([P, NH, 2, HD])

        def pair(t, w=PW):
            return bass.ds(t * w, w)

        @block.sync
        def _(sp):
            sp.dma_start(xs[:].rearrange("p (t d) -> p t d", t=NT), x_d.rearrange("t p d -> p t d")).then_inc(S["x_in"], 16)
            sp.dma_start(csT[:], ctxT_d).then_inc(S["ctxT_in"], 16)
            sp.dma_start(raw_qkvo[:, 0:NQ], wq_d).then_inc(S["wqkvo_in"], 16)
            sp.dma_start(raw_qkvo[:, NQ:NQ + NKV], wkv_d).then_inc(S["wqkvo_in"], 16)
            sp.dma_start(raw_qkvo[:, NQ + NKV:], wo_d).then_inc(S["wqkvo_in"], 16)
            for n, (src, col, _, _, _, cols) in enumerate(PIECES):
                if n == EARLY:
                    sp.dma_start(cs[:].rearrange("p (t d) -> p t d", t=NT), ctx_d.rearrange("t p d -> p t d")).then_inc(S["ctx_in"], 16)
                if n >= RING:
                    sp.wait_ge(S["piece_split"], 2 * (n - RING + 1))
                sp.dma_start(raw[n % RING][:, 0:cols], src[:, col:col + cols]).then_inc(raw_in[n % RING], 16)
            with sp.Fori(0, NP) as r:
                sp.wait_ge(S["x4_done"], r + 1)
                sp.dma_start(out_d[bass.ds(r * 2, 2), :, :].rearrange("t p d -> p t d"),
                             xs[:, pair(r)].rearrange("p (t d) -> p t d", t=2)).then_inc(S["stores"], 16)
            sp.wait_ge(S["stores"], 16 * NP)

        @block.gpsimd
        def _(pool):
            nc.gpsimd.memset(neg_half[:], -0.5).then_inc(S["consts"], 1)
            nc.gpsimd.memset(v_aug[:], 0.0).then_inc(S["consts"], 1)
            nc.gpsimd.memset(nm16[:], 0.0).then_inc(S["consts"], 1)
            nc.gpsimd.memset(pen[:], 0.0).then_inc(S["consts"], 1)
            nc.gpsimd.memset(rep[:], PAD).then_inc(S["consts"], 1)
            nc.gpsimd.memset(lgv[:], PAD).then_inc(S["consts"], 1)
            for m in (ident, ident16, identb, pick_row, spread):
                nc.gpsimd.memset(m[:], 0.0).then_inc(S["consts"], 1)
            pool.wait_ge(S["consts"], 11)
            nc.gpsimd.memset(v_aug[:].rearrange("p (h c) -> p h c", c=HP)[:, :, HD:HD + 1], 1.0).then_inc(S["ident_ready"], 1)
            for m in (ident, ident16, identb):
                nc.gpsimd.affine_select(out=m[:], in_=m[:], compare_op=ALU.not_equal, fill=1.0, base=0,
                                        pattern=[[-1, P]], channel_multiplier=1).then_inc(S["ident_ready"], 1)
            done = 0
            for base in (0, 8, 64, 72):
                if done:
                    pool.wait_ge(S["patterns_ready"], done)
                v = pick_row[:].rearrange("p (i k) -> p i k", k=P)
                nc.gpsimd.affine_select(out=v, in_=v, compare_op=ALU.not_equal, fill=1.0, base=-base,
                                        pattern=[[-1, 8], [0, P]], channel_multiplier=1).then_inc(S["patterns_ready"], 1)
                done += 1
            v = spread[:].rearrange("p (c b m) -> p (c b) m", b=2, m=BLK)
            nc.gpsimd.affine_select(out=v, in_=v, compare_op=ALU.not_equal, fill=1.0, base=0,
                                    pattern=[[-1, NB], [0, BLK]], channel_multiplier=1).then_inc(S["patterns_ready"], 1)

            def split_piece(n):
                _, _, hi, lo, col, cols = PIECES[n]
                r, h = raw[n % RING][:, 0:cols], hi[:, col:col + cols]
                pool.wait_ge(raw_in[n % RING], 16 * (n // RING + 1))
                nc.gpsimd.tensor_scalar(h, r, 1.0, 0.0, ALU.mult, ALU.add).then_inc(S["piece_split"], 1)
                pool.wait_ge(S["piece_split"], 2 * n + 1)
                nc.gpsimd.tensor_tensor(lo[:, col:col + cols], r, h.bitcast(f32), ALU.subtract).then_inc(S["piece_split"], 1)

            def ln(kind, vare, out):
                def step(t, _):
                    pool.wait_ge(S[f"{kind}_vare"], 2 * t + 2)
                    nc.gpsimd.tensor_tensor(out[:], vare[:], neg_half[:, 0:2], ALU.pow).then_inc(S[f"{kind}_rstd"], 1)
                    if kind == "a":
                        ctx_split(t)
                return step

            def ctx_split(t):
                pool.wait_ge(S["c_hi_done"], t + 1)
                nc.gpsimd.tensor_tensor(c_lo[:], csT[:, pair(t)], c_hi[:].bitcast(f32), ALU.subtract).then_inc(S["c_split"], 1)

            def a_qkv(t, j):
                n = 2 * t + j + 1
                pool.wait_ge(S["msq_done"], n)
                nc.gpsimd.tensor_tensor(rms[:, 2 * j:2 * j + 2], msq[:, 2 * j:2 * j + 2], neg_half[:, 0:2],
                                        ALU.pow).then_inc(S["rms_done"], 1)

            def f_up(t, c):
                pool.wait_ge(S["h_hi_done"], NC * t + c + 1)
                b, f = c % HB * T2, c % HF * T2
                nc.gpsimd.tensor_tensor(h_lo[:, b:b + T2], hf[:, f:f + T2], h_hi[:, b:b + T2].bitcast(f32),
                                        ALU.subtract).then_inc(S["h_lo_done"], 1)

            def l_ln(t, _):
                nc.gpsimd.tensor_copy(mask2[:], mask_all[:, pair(t, T2)]).then_inc(S["mask_sel"], 1)
                nc.gpsimd.memset(sc[:], MASKED).then_inc(S["sc_filled"], 1)
                ln("l", vare_l, rstd_l)(t, 0)

            def b_up(t, c):
                pool.wait_ge(S["bh_hi"], NC * t + c + 1)
                b, f = c % HB * T2, c % HF * T2
                nc.gpsimd.tensor_tensor(h_lo[:, b:b + T2], hf[:, f:f + T2], h_hi[:, b:b + T2].bitcast(f32),
                                        ALU.subtract).then_inc(S["bh_lo"], 1)

            def a_qkv_first(t, j):
                a_qkv(t, j)
                if isinstance(t, int) and j == 1:
                    for n in range(EARLY):
                        split_piece(n)

            def f_up_last(t, c):
                f_up(t, c)
                if isinstance(t, int):
                    split_piece(EARLY + c)

            steps = {"A.ln": ln("a", vare_a, rstd_a), "A.qkv": a_qkv_first, "F.ln": ln("f", vare_f, rstd_f),
                     "F.up": f_up_last, "L.ln": l_ln, "R.ln": ln("b", vare_b, rstd_b), "B.up": b_up}
            pool.wait_ge(S["mask_in"], 16)
            run(pool, steps)

        @block.scalar
        def _(act):
            def row(dst, src):
                act.dma_start(dst, src.partition_broadcast(P)).then_inc(S["rows_in"], 16)

            row(qb[:], qb_d)
            row(kb[:], kb_d)
            row(vb[:], vb_d)
            row(nqk[:, 0:D], nq_d)
            row(nqk[:, D:], nk_d)
            row(ob2[:, 0:D], ob_d)
            row(ob2[:, D:], ob_d)
            row(graw[:, 0:2], gx_d)
            row(graw[:, 2:4], gf_d)
            act.dma_start(br_col[:], br_d).then_inc(S["rows_in"], 16)
            act.dma_start(mask_words[:], mask_d.partition_broadcast(P)).then_inc(S["mask_in"], 16)
            act.wait_ge(S["rows_in"], 160)
            nc.scalar.activation(gate[:], graw[:], ACT.Tanh).then_inc(S["gates_ready"], 1)

            def copy(out, in_, s):
                nc.scalar.activation(out, in_, ACT.Copy).then_inc(S[s], 1)

            def a_T(t, _):
                act.wait_ge(S["a_T"], t + 1)
                copy(aT_hi[:], M[:], "a_hi")

            def a_qkv(t, j):
                n = 2 * t + j + 1
                d = slice(j * D, j * D + D)
                for i, (s, src) in enumerate((("q_pre_done", q_pre), ("k_pre_done", k_pre))):
                    act.wait_ge(S[s], n)
                    nc.scalar.activation(junk[:], src[:, d], ACT.Square, scale=D ** -0.5,
                                         accum_out=ssq[:, 2 * j + i:2 * j + i + 1]).then_inc(S["ss_done"], 1)
                    act.wait_ge(S["ss_done"], 2 * (n - 1) + i + 1)
                for i, (s, src, done) in enumerate((("qn_done", qn, "q16_hi"), ("kn_done", kn, "k16_hi"))):
                    act.wait_ge(S[s], n)
                    copy(parts(i, j, 0), twice(src[:, d]), done)

            def a_qkT(t, j):
                act.wait_ge(S["qkT_done"], 2 * t + j + 1)
                copy(QT[:, j * 1024:(j + 1) * 1024], W[j][:, 0:512].bitcast(f16), "QT_done")

            def a_mT(t, j):
                act.wait_ge(S["mT_ps"], 2 * t + j + 1)
                copy(mT[:, j * P:(j + 1) * P], M[:, 0:P // 2].bitcast(f16), "mT_done")

            def a_st(t, i):
                j, half = i // 2, i % 2
                act.wait_ge(S["st_done"], 4 * t + i + 1)
                if j == 1:
                    act.wait_ge(S["pv_done"], 2 * t + 1)
                nc.scalar.activation(PT[half], W[half][:], ACT.Exp, scale=sc_exp[:]).then_inc(S["PT_done"], 1)

            def a_pv(t, j):
                act.wait_ge(S["pv_done"], 2 * t + j + 1)
                copy(po[:, j * 512:(j + 1) * 512], M[:], "po_done")

            def a_aT(t, _):
                act.wait_ge(S["oT_ps"], t + 1)
                copy(oT_hi[:], M[:], "oT_hi_done")

            def f_T(t, _):
                act.wait_ge(S["f_T"], t + 1)
                copy(fT_hi[:], M[:], "f_hi")

            def f_up(t, c):
                k, b, g, f = NC * t + c + 1, c % HB * T2, c % 2 * T2, c % HF * T2
                act.wait_ge(S["gu_done"], k)
                nc.scalar.activation(th[:, g:g + T2], G[c % 2][:, 0:T2], ACT.Tanh, scale=0.5).then_inc(S["th_done"], 1)
                act.wait_ge(S["hf_done"], k)
                if c >= HB:
                    act.wait_ge(S["dn_part"], NC * t + c - HB + 1)
                copy(h_hi[:, b:b + T2], hf[:, f:f + T2], "h_hi_done")

            def l_T(t, j):
                act.wait_ge(S["l_T"], 2 * t + j + 1)
                copy(lT[:, j * D:(j + 1) * D], G[j][:, 0:D], "lT_done")

            def l_sc(t, j):
                n = 2 * t + j + 1
                act.wait_ge(S["l_maxs"], n)
                nc.scalar.activation(pl[:, j * P:(j + 1) * P], sc[:, j * P:(j + 1) * P], ACT.Exp, scale=D ** -0.5,
                                     bias=nmx_s[:, j:j + 1], accum_out=den[:, j:j + 1]).then_inc(S["lp_done"], 1)

            def l_pT(t, j):
                act.wait_ge(S["plT_ps"], 2 * t + j + 1)
                copy(plT[:, j * P:(j + 1) * P], G[j][:, 384:512], "plT_done")

            def r_T(t, _):
                act.wait_ge(S["b_T"], t + 1)
                copy(bT_hi[:, pair(t)], M[:], "b_hi")

            def b_up(t, c):
                f = c % HF * T2
                act.wait_ge(S["up_done"], NC * t + c + 1)
                if c >= HF:
                    act.wait_ge(S["bh_lo"], NC * t + c - HF + 1)
                nc.scalar.activation(hf[:, f:f + T2], G[c % 2][:, 0:T2], ACT.Gelu).then_inc(S["bf_done"], 1)

            run(act, {"A.T": a_T, "A.qkv": a_qkv, "A.qkT": a_qkT, "A.mT": a_mT, "A.st": a_st, "A.pv": a_pv, "A.aT": a_aT,
                      "F.T": f_T, "F.up": f_up, "L.T": l_T, "L.sc": l_sc, "L.pT": l_pT, "R.T": r_T, "B.up": b_up})

        @block.vector
        def _(dve):
            V = nc.vector
            dve.wait_ge(S["rows_in"], 160)
            V.tensor_tensor(wn[:], nqk[:, 0:D], nqk[:, D:], ALU.mult).then_inc(S["wn_mul"], 1)
            dve.wait_ge(S["wn_mul"], 1)
            V.tensor_reduce(wn_max[:], wn[:], AX.X, ALU.max, apply_absolute_value=True).then_inc(S["wn_abs"], 1)
            dve.wait_ge(S["wn_abs"], 1)
            V.tensor_scalar(wn_max[:], wn_max[:], 1e-30, None, ALU.max).then_inc(S["wn_abs"], 1)
            dve.wait_ge(S["wn_abs"], 2)
            V.reciprocal(wn_inv[:], wn_max[:]).then_inc(S["wn_rec"], 1)
            V.tensor_scalar(sc_exp[:], wn_max[:], HD ** -0.5, None, ALU.mult).then_inc(S["rows_ready"], 1)
            dve.wait_ge(S["wn_rec"], 1)
            V.tensor_scalar(wn[:], wn[:], wn_inv[:], None, ALU.mult).then_inc(S["rows_ready"], 1)
            dve.wait_ge(S["gates_ready"], 1)
            V.tensor_scalar(gf0_half[:], gate[:, 2:3], 0.5, None, ALU.mult).then_inc(S["rows_ready"], 1)
            dve.wait_ge(S["mask_in"], 16)
            V.tensor_reduce(valid[:], mask_all.rearrange("p (t k) -> p t k", k=P), AX.X, ALU.max).then_inc(S["rows_ready"], 1)
            dve.wait_ge(S["wqkvo_in"], 48)
            V.tensor_copy(whi_a[:], raw_qkvo[:]).then_inc(S["wa_split"], 1)
            dve.wait_ge(S["wa_split"], 1)
            V.tensor_tensor(wlo_a[:], raw_qkvo[:], whi_a[:].bitcast(f32), ALU.subtract).then_inc(S["wa_split"], 1)
            dve.wait_ge(S["rows_ready"], 4)
            dve.wait_ge(S["x_in"], 16)
            dve.wait_ge(S["ident_ready"], 4)

            def ln(t, kind, src, bn, var, vare, rs, xn):
                def plus_eps(j):
                    dve.wait_ge(S[f"{kind}_var"], 2 * t + j + 1)
                    V.tensor_scalar(vare[:, j:j + 1], var[:, 2 * j + 1:2 * j + 2], 1e-5, None, ALU.add).then_inc(S[f"{kind}_vare"], 1)

                V.bn_stats(bn[:, 0:6], src(0)).then_inc(S[f"{kind}_stats"], 1)
                dve.wait_ge(S[f"{kind}_stats"], 2 * t + 1)
                V.bn_stats(bn[:, 6:12], src(1)).then_inc(S[f"{kind}_stats"], 1)
                V.bn_aggr(var[:, 0:2], bn[:, 0:6]).then_inc(S[f"{kind}_var"], 1)
                dve.wait_ge(S[f"{kind}_stats"], 2 * t + 2)
                plus_eps(0)
                V.bn_aggr(var[:, 2:4], bn[:, 6:12]).then_inc(S[f"{kind}_var"], 1)
                plus_eps(1)
                if kind == "a":
                    V.tensor_copy(c_hi[:], csT[:, pair(t)]).then_inc(S["c_hi_done"], 1)
                dve.wait_ge(S[f"{kind}_rstd"], t + 1)
                for j in range(2):
                    V.tensor_scalar(xn[:, j * D:(j + 1) * D], src(j), var[:, 2 * j:2 * j + 1], rs[:, j:j + 1],
                                    ALU.subtract, ALU.mult).then_inc(S[f"{kind}_xn"], 1)

            def low(out, ps, hi, s):
                V.tensor_tensor(out, ps, hi.bitcast(f32), ALU.subtract).then_inc(S[s], 1)

            def a_ln(t, _):
                if isinstance(t, int):
                    dve.wait_ge(S["ctxT_in"], 16)
                ln(t, "a", lambda j: xs[:, bass.ds(t * PW + j * D, D)], bn_a, var_a, vare_a, rstd_a, xn_a)

            def a_T(t, _):
                dve.wait_ge(S["a_hi"], t + 1)
                low(aT_lo[:], M[:], aT_hi[:], "a_lo")

            def a_qkv(t, j):
                n = 2 * t + j + 1
                d = slice(j * D, j * D + D)
                dve.wait_ge(S["qkv_done"], n)
                V.tensor_tensor(q_pre[:, d], W[j][:, 512:512 + D], qb[:], ALU.add).then_inc(S["q_pre_done"], 1)
                V.tensor_tensor(k_pre[:, d], W[j][:, 0:D], kb[:], ALU.add).then_inc(S["k_pre_done"], 1)
                v = v_aug[:, j * NH * HP:(j + 1) * NH * HP].rearrange("p (h c) -> p h c", c=HP)
                V.tensor_tensor(v[:, :, 0:HD], W[j][:, D:2 * D].rearrange("p (h c) -> p h c", c=HD),
                                vb[:].rearrange("p (h c) -> p h c", c=HD), ALU.add).then_inc(S["v_done"], 1)
                dve.wait_ge(S["ss_done"], 2 * n)
                V.tensor_scalar(msq[:, 2 * j:2 * j + 2], ssq[:, 2 * j:2 * j + 2], 1e-6, None, ALU.add).then_inc(S["msq_done"], 1)
                dve.wait_ge(S["rms_done"], n)
                V.scalar_tensor_tensor(qn[:, d], q_pre[:, d], rms[:, 2 * j:2 * j + 1], wn[:], ALU.mult, ALU.mult).then_inc(S["qn_done"], 1)
                V.tensor_scalar(kn[:, d], k_pre[:, d], rms[:, 2 * j + 1:2 * j + 2], None, ALU.mult).then_inc(S["kn_done"], 1)
                for i, (src, hi_s, lo_s) in enumerate(((qn, "q16_hi", "q16_lo"), (kn, "k16_hi", "k16_lo"))):
                    dve.wait_ge(S[hi_s], n)
                    V.tensor_tensor(parts(i, j, 1), twice(src[:, d]), parts(i, j, 0), ALU.subtract).then_inc(S[lo_s], 1)

            def a_qkT(t, j):
                dve.wait_ge(S["qkT_done"], 2 * t + j + 1)
                V.tensor_copy(KT[:, j * 1024:(j + 1) * 1024], W[j][:, 512:1024].bitcast(f16)).then_inc(S["KT_done"], 1)

            def a_s(t, i):
                j, half = i // 2, i % 2
                dve.wait_ge(S["s_done"], 4 * t + i + 1)
                o = mx[:, j * NH:(j + 1) * NH].rearrange("p (r i) -> p r i", r=2)[:, :, 4 * half:4 * half + 4]
                V.tensor_reduce(o, W[half][:].rearrange("p (r i k) -> p r i k", r=2, k=P), AX.X, ALU.max).then_inc(S["max_done"], 1)
                if half == 1:
                    n = 2 * t + j + 1
                    dve.wait_ge(S["max_done"], 2 * n)
                    m = mx[:, j * NH:(j + 1) * NH].rearrange("p (r i) -> p r i", r=2)
                    o = nm16[:, j * P:(j + 1) * P].rearrange("p (r s) -> p r s", r=2)
                    V.tensor_scalar(o[:, :, 0:8], m, -1.0, None, ALU.mult).then_inc(S["nm_hi"], 1)
                    dve.wait_ge(S["nm_hi"], n)
                    V.scalar_tensor_tensor(o[:, :, 8:16], m, -1.0, o[:, :, 0:8], ALU.mult, ALU.subtract).then_inc(S["nm_done"], 1)

            def a_oT(t, j):
                n = 2 * t + j + 1
                dve.wait_ge(S["oTok_done"], n)
                o = W[j][:, 0:512].rearrange("p (h c) -> p h c", c=HP)
                V.reciprocal(rden[:, j * NH:(j + 1) * NH], o[:, :, HD]).then_inc(S["rden_done"], 1)
                dve.wait_ge(S["rden_done"], n)
                V.tensor_tensor(attn[:, j * D:(j + 1) * D].rearrange("p (h c) -> p h c", c=HD), o[:, :, 0:HD],
                                rden[:, j * NH:(j + 1) * NH].unsqueeze(2).to_broadcast([P, NH, HD]),
                                ALU.mult).then_inc(S["attn_done"], 1)

            def a_aT(t, _):
                dve.wait_ge(S["oT_hi_done"], t + 1)
                low(oT_lo[:], M[:], oT_hi[:], "oT_lo_done")

            def a_o(t, _):
                dve.wait_ge(S["o_done"], t + 1)
                if not isinstance(t, int):
                    dve.wait_ge(S["x3_done"], 2 * t)
                V.tensor_tensor(x1[:], M[:], ob2[:], ALU.add).then_inc(S["ob_done"], 1)
                dve.wait_ge(S["ob_done"], t + 1)
                V.scalar_tensor_tensor(x1[:], x1[:], gate[:, 0:1], xs[:, pair(t)], ALU.mult, ALU.add).then_inc(S["x1_done"], 1)

            def f_ln(t, _):
                dve.wait_ge(S["x1_done"], t + 1)
                ln(t, "f", lambda j: x1[:, j * D:(j + 1) * D], bn_f, var_f, vare_f, rstd_f, xn_f)

            def f_T(t, _):
                dve.wait_ge(S["f_hi"], t + 1)
                low(fT_lo[:], M[:], fT_hi[:], "f_lo")

            def f_up(t, c):
                k, b, g, f = NC * t + c + 1, c % HB * T2, c % 2 * T2, c % HF * T2
                dve.wait_ge(S["th_done"], k)
                V.scalar_tensor_tensor(uu[:, g:g + T2], th[:, g:g + T2], 1.0, G[c % 2][:, 0:T2], ALU.add, ALU.mult).then_inc(S["uu_done"], 1)
                dve.wait_ge(S["uu_done"], k)
                if c >= HF:
                    dve.wait_ge(S["h_lo_done"], NC * t + c - HF + 1)
                V.tensor_tensor(hf[:, f:f + T2], G[c % 2][:, T2:2 * T2], uu[:, g:g + T2], ALU.mult).then_inc(S["hf_done"], 1)

            def f_dn(t, c):
                if c == NC - 1:
                    dve.wait_ge(S["dn_part"], NC * t + NC)
                    V.scalar_tensor_tensor(x2[:], DN[:], gf0_half[:], x1[:], ALU.mult, ALU.add).then_inc(S["x2_done"], 1)

            def l_ln(t, _):
                dve.wait_ge(S["x2_done"], t + 1)
                ln(t, "l", lambda j: x2[:, j * D:(j + 1) * D], bn_l, var_l, vare_l, rstd_l, xn_l)

            def l_sc(t, j):
                n = 2 * t + j + 1
                k = slice(j * P, (j + 1) * P)
                wait_apart(dve, "l_sc", n)
                if j == 0:
                    dve.wait_ge(S["mask_sel"], t + 1)
                    dve.wait_ge(S["sc_filled"], t + 1)
                V.copy_predicated(sc[:, k], mask2[:, k], G[j][:, D:D + P]).then_inc(S["l_sel"], 1)
                dve.wait_ge(S["l_sel"], n)
                V.reduce_max(nmx[:, j:j + 1], sc[:, k], AX.X).then_inc(S["l_max"], 1)
                dve.wait_ge(S["l_max"], n)
                V.tensor_scalar(nmx_s[:, j:j + 1], nmx[:, j:j + 1], -(D ** -0.5), None, ALU.mult).then_inc(S["l_maxs"], 1)

            def l_ro(t, j):
                n = 2 * t + j + 1
                if j == 0:
                    for i in range(2):
                        dve.wait_ge(S["lp_done"], 2 * t + i + 1)
                        V.reciprocal(rec[:, i:i + 1], den[:, i:i + 1]).then_inc(S["rec_done"], 1)
                    for i in range(2):
                        dve.wait_ge(S["rec_done"], 2 * t + i + 1)
                        V.scalar_tensor_tensor(coef[:, i:i + 1], rec[:, i:i + 1], gate[:, 1:2], valid[:, bass.ds(t * 2 + i, 1)],
                                               ALU.mult, ALU.mult).then_inc(S["coef_done"], 1)
                dve.wait_ge(S["ro_done"], n)
                dve.wait_ge(S["coef_done"], n)
                V.scalar_tensor_tensor(xs[:, bass.ds(t * PW + j * D, D)], G[j][:, 0:D], coef[:, j:j + 1], x2[:, j * D:(j + 1) * D],
                                       ALU.mult, ALU.add).then_inc(S["x3_done"], 1)

            def r_ln(t, _):
                dve.wait_ge(S["x3_done"], 2 * t + 2)
                ln(t, "b", lambda j: xs[:, bass.ds(t * PW + j * D, D)], bn_b, var_b, vare_b, rstd_b, xn_b)

            def r_T(t, _):
                dve.wait_ge(S["b_hi"], t + 1)
                low(bT_lo[:, pair(t)], M[:], bT_hi[:, pair(t)], "b_lo")

            def r_rt(t, _):
                dve.wait_ge(S["rt_ps"], t + 1)
                V.tensor_scalar(lgT[:], W[0][0:HP, 0:T2], br_col[:], None, ALU.add).then_inc(S["lg_done"], 1)

            def r_lT(t, _):
                wait_apart(dve, "lgT_ps", t + 1)
                for j in range(2):
                    V.max(t8[:, 8 * j:8 * j + 8], W[0][:, 512 + HP * j:512 + HP * j + NB]).then_inc(S["t8_done"], 1)
                for j in range(2):
                    dve.wait_ge(S["t8_done"], 2 * t + j + 1)
                    V.tensor_scalar(lgv[:, 24 * j:24 * j + NB], W[0][:, 512 + HP * j:512 + HP * j + NB], t8[:, 8 * j:8 * j + 1], EXP_LOW,
                                    ALU.subtract, ALU.max).then_inc(S["lgv_done"], 1)
                    V.tensor_scalar(rep[:, 8 * j:8 * j + TOPK], t8[:, 8 * j:8 * j + TOPK], t8[:, 8 * j:8 * j + 1], EXP_LOW,
                                    ALU.subtract, ALU.max).then_inc(S["rep_done"], 1)
                for j in range(2):
                    wait_apart(dve, "lgv_done", 2 * t + j + 1)
                    dve.wait_ge(S["rep_done"], 2 * t + j + 1)
                    V.match_replace(mr[:, 24 * j:24 * j + 24], rep[:, 8 * j:8 * j + 8], lgv[:, 24 * j:24 * j + 24], 1.0).then_inc(S["mr_done"], 1)
                for j in range(2):
                    dve.wait_ge(S["mr_done"], 2 * t + j + 1)
                    V.tensor_scalar(pen[:, j * P:j * P + NB], mr[:, 24 * j:24 * j + NB], 0.5, UNPICKED, ALU.is_lt, ALU.mult).then_inc(S["pen_done"], 1)

            def r_pT(t, _):
                dve.wait_ge(S["penT_ps"], t + 1)
                V.tensor_copy(penT[:, pair(t, T2)], W[1][:, 0:P].bitcast(bf16)).then_inc(S["penT_done"], 1)

            def b_up(t, c):
                b, f = c % HB * T2, c % HF * T2
                dve.wait_ge(S["bf_done"], NC * t + c + 1)
                if c >= HB:
                    dve.wait_ge(S["bdn_part"], NC * t + c - HB + 1)
                V.tensor_copy(h_hi[:, b:b + T2], hf[:, f:f + T2]).then_inc(S["bh_hi"], 1)

            def b_dn(t, c):
                if c == NC - 1:
                    dve.wait_ge(S["bdn_part"], NC * t + NC)
                    V.scalar_tensor_tensor(xs[:, pair(t)], DN[:], gate[:, 3:4], xs[:, pair(t)], ALU.mult, ALU.add).then_inc(S["x4_done"], 1)

            run(dve, {"A.ln": a_ln, "A.T": a_T, "A.qkv": a_qkv, "A.qkT": a_qkT, "A.s": a_s, "A.oT": a_oT, "A.aT": a_aT, "A.o": a_o,
                      "F.ln": f_ln, "F.T": f_T, "F.up": f_up, "F.dn": f_dn, "L.ln": l_ln, "L.sc": l_sc, "L.ro": l_ro,
                      "R.ln": r_ln, "R.T": r_T, "R.rt": r_rt, "R.lT": r_lT, "R.pT": r_pT, "B.up": b_up, "B.dn": b_dn})

        @block.tensor
        def _(pe):
            MM, TR = nc.tensor.matmul, nc.tensor.transpose

            def split_mm(out, terms, first=True, last=True):
                n = 3 * len(terms)
                i = 0
                for (lh, ll), (rh, rl) in terms:
                    for a, b in ((lh, rh), (lh, rl), (ll, rh)):
                        ins = MM(out, a, b, start=first and i == 0, stop=last and i == n - 1, skip_group_check=True)
                        i += 1
                return ins

            def transpose_pair(src):
                for j in range(2):
                    for kc in range(KC):
                        ins = TR(M[:, kc * T2 + j * P:kc * T2 + (j + 1) * P], src[:, j * D + kc * P:j * D + (kc + 1) * P], ident[:])
                return ins

            def cols(hi, lo, a, n):
                return hi[:, a:a + n], lo[:, a:a + n]

            def a_T(t, _):
                if isinstance(t, int):
                    pe.wait_ge(S["ident_ready"], 4)
                    pe.wait_ge(S["patterns_ready"], 5)
                pe.wait_ge(S["a_xn"], 2 * t + 2)
                transpose_pair(xn_a).then_inc(S["a_T"], 1)

            def a_qkv(t, j):
                if j == 0:
                    pe.wait_ge(S["a_lo"], t + 1)
                    pe.wait_ge(S["c_split"], t + 1)
                    if isinstance(t, int):
                        pe.wait_ge(S["wa_split"], 2)
                split_mm(W[j][:, 0:512], [(cols(c_hi, c_lo, j * D + kc * P, P), cols(whi_a, wlo_a, NQ + kc * 2 * D, 2 * D))
                                          for kc in range(KC)])
                split_mm(W[j][:, 512:512 + D], [(cols(aT_hi, aT_lo, kc * T2 + j * P, P), cols(whi_a, wlo_a, kc * D, D))
                                                for kc in range(KC)]).then_inc(S["qkv_done"], 1)

            def a_qkT(t, j):
                n = 2 * t + j + 1
                pe.wait_ge(S["q16_lo"], n)
                pe.wait_ge(S["k16_lo"], n)
                o = W[j][:].bitcast(f16)
                for g in range(8):
                    a = j * 4 * D + g * P
                    TR(o[:, g * P:(g + 1) * P], q16[:, a:a + P], ident16[:])
                    ins = TR(o[:, 1024 + g * P:1024 + (g + 1) * P], k16[:, a:a + P], ident16[:])
                ins.then_inc(S["qkT_done"], 1)

            def head(j, half, c, r):
                a = j * 1024 + (4 * half + c) * P
                return slice(64 * r, 64 * r + 64), slice(a, a + P)

            def a_s(t, i):
                j, half = i // 2, i % 2
                if i == 0:
                    pe.wait_ge(S["KT_done"], 2 * t + 2)
                    pe.wait_ge(S["QT_done"], 2 * t + 2)
                if j == 1:
                    pe.wait_ge(S["max_done"], 4 * t + i - 1)
                for c in range(4):
                    for r in range(2):
                        rows, cc = head(j, half, c, r)
                        ins = MM(W[half][:, r * 512 + c * P:r * 512 + (c + 1) * P], QT[rows, cc], KT[rows, cc],
                                 start=True, stop=True, skip_group_check=True)
                ins.then_inc(S["s_done"], 1)

            def a_mT(t, j):
                n = 2 * t + j + 1
                pe.wait_ge(S["nm_done"], n)
                if j == 1:
                    pe.wait_ge(S["mT_done"], n - 1)
                TR(M[:, 0:P // 2].bitcast(f16), nm16[:, j * P:(j + 1) * P], ident16[:]).then_inc(S["mT_ps"], 1)

            def a_st(t, i):
                j, half = i // 2, i % 2
                if half == 0:
                    pe.wait_ge(S["mT_done"], 2 * t + j + 1)
                if j == 0:
                    pe.wait_ge(S["max_done"], 4 * t + i + 3)
                else:
                    pe.wait_ge(S["PT_done"], 4 * t + i - 1)
                for c in range(4):
                    for r in range(2):
                        rows, cc = head(j, half, c, r)
                        o = W[half][:, r * 512 + c * P:r * 512 + (c + 1) * P]
                        MM(o, KT[rows, cc], QT[rows, cc], start=True, stop=False, skip_group_check=True)
                        h = 4 * half + c
                        ins = MM(o, pick_row[rows, h * P:(h + 1) * P], mT[rows, j * P:(j + 1) * P], start=False, stop=True,
                                 skip_group_check=True)
                ins.then_inc(S["st_done"], 1)

            def a_pv(t, j):
                pe.wait_ge(S["PT_done"], 4 * t + 2 * j + 2)
                if j == 1:
                    pe.wait_ge(S["po_done"], 2 * t + 1)
                for h in range(NH):
                    half, c, r = h // 8, h % 8 // 2, h % 2
                    g, ch = h % 4, h // 4
                    a = (j * NH + h) * HP
                    ins = MM(M[HP * g:HP * (g + 1), ch * P:(ch + 1) * P], v_aug[:, a:a + HP], PT[half][:, (r * 4 + c) * P:(r * 4 + c + 1) * P],
                             start=True, stop=True, skip_group_check=True)
                ins.then_inc(S["pv_done"], 1)

            def a_oT(t, j):
                pe.wait_ge(S["po_done"], 2 * t + j + 1)
                pe.wait_ge(S["PT_done"], 4 * t + 3 + j)
                for ch in range(4):
                    ins = TR(W[j][:, ch * P:(ch + 1) * P], po[:, j * 512 + ch * P:j * 512 + (ch + 1) * P], ident[:])
                ins.then_inc(S["oTok_done"], 1)

            def a_aT(t, _):
                pe.wait_ge(S["attn_done"], 2 * t + 2)
                pe.wait_ge(S["po_done"], 2 * t + 2)
                transpose_pair(attn).then_inc(S["oT_ps"], 1)

            def a_o(t, _):
                pe.wait_ge(S["oT_lo_done"], t + 1)
                for j in range(2):
                    ins = split_mm(M[:, j * D:(j + 1) * D], [(cols(oT_hi, oT_lo, kc * T2 + j * P, P), cols(whi_a, wlo_a, NQ + NKV + kc * D, D))
                                                             for kc in range(KC)])
                ins.then_inc(S["o_done"], 1)

            def f_T(t, _):
                pe.wait_ge(S["f_xn"], 2 * t + 2)
                pe.wait_ge(S["x1_done"], t + 1)
                if not isinstance(t, int):
                    pe.wait_ge(S["a_lo"], t + 2)
                transpose_pair(xn_f).then_inc(S["f_T"], 1)

            def f_up(t, c):
                if c == 0:
                    pe.wait_ge(S["f_lo"], t + 1)
                    pe.wait_ge(S["piece_split"], 2 * EARLY)
                if c >= 2:
                    pe.wait_ge(S["hf_done"], NC * t + c - 1)
                for u in range(2):
                    ins = split_mm(G[c % 2][:, u * T2:(u + 1) * T2],
                                   [(cols(wgu_hi, wgu_lo, (kc * 2 + u) * INTER + c * P, P), cols(fT_hi, fT_lo, kc * T2, T2)) for kc in range(KC)])
                ins.then_inc(S["gu_done"], 1)

            def down(hi_sem, whi, wlo, off, part):
                def step(t, c):
                    pe.wait_ge(S[hi_sem], NC * t + c + 1)
                    b = c % HB * T2
                    for j in range(2):
                        ins = split_mm(DN[:, j * D:(j + 1) * D], [(cols(h_hi, h_lo, b + j * P, P), cols(whi, wlo, off + c * D, D))],
                                       first=c == 0 and j == 0, last=c == NC - 1)
                    ins.then_inc(S[part], 1)
                return step

            def l_T(t, j):
                pe.wait_ge(S["l_xn"], 2 * t + j + 1)
                for kc in range(KC):
                    ins = TR(G[j][:, kc * P:(kc + 1) * P], xn_l[:, j * D + kc * P:j * D + (kc + 1) * P], ident[:])
                ins.then_inc(S["l_T"], 1)

            def l_sc(t, j):
                pe.wait_ge(S["lT_done"], 2 * t + j + 1)
                for kc in range(KC):
                    ins = MM(G[j][:, D:D + P], lT[:, j * D + kc * P:j * D + (kc + 1) * P], csT[:, bass.ds(t * PW + j * D + kc * P, P)],
                             start=kc == 0, stop=kc == KC - 1, skip_group_check=True)
                ins.then_inc(S["l_sc"], 1)

            def l_pT(t, j):
                n = 2 * t + j + 1
                pe.wait_ge(S["lp_done"], n)
                TR(G[j][:, 384:512], pl[:, j * P:(j + 1) * P], ident[:]).then_inc(S["plT_ps"], 1)

            def l_ro(t, j):
                pe.wait_ge(S["plT_done"], 2 * t + j + 1)
                pe.wait_ge(S["ctx_in"], 16)
                MM(G[j][:, 0:D], plT[:, j * P:(j + 1) * P], cs[:, bass.ds(t * PW + j * D, D)], start=True, stop=True,
                   skip_group_check=True).then_inc(S["ro_done"], 1)

            def l_end(t, _):
                pe.wait_ge(S["x3_done"], 2 * t + 2)

            def r_T(t, _):
                pe.wait_ge(S["b_xn"], 2 * t + 2)
                transpose_pair(xn_b).then_inc(S["b_T"], 1)

            def r_rt(t, _):
                pe.wait_ge(S["b_lo"], t + 1)
                if isinstance(t, int):
                    pe.wait_ge(S["piece_split"], 2 * EARLY)
                split_mm(W[0][:, 0:T2], [(cols(wr_hi, wr_lo, kc * P, P), (bT_hi[:, bass.ds(t * PW + kc * T2, T2)], bT_lo[:, bass.ds(t * PW + kc * T2, T2)]))
                                         for kc in range(KC)]).then_inc(S["rt_ps"], 1)

            def r_lT(t, _):
                wait_apart(pe, "lg_done", t + 1)
                for j in range(2):
                    ins = TR(W[0][:, 512 + HP * j:512 + HP * (j + 1)], lgT[:, j * P:(j + 1) * P], ident[0:HP, 0:HP])
                ins.then_inc(S["lgT_ps"], 1)

            def r_pT(t, _):
                pe.wait_ge(S["pen_done"], 2 * t + 2)
                for j in range(2):
                    ins = TR(W[1][:, j * P // 2:(j + 1) * P // 2].bitcast(bf16), pen[:, j * P:(j + 1) * P], identb[:])
                ins.then_inc(S["penT_ps"], 1)

            def b_up(t, c):
                if c == 0:
                    pe.wait_ge(S["penT_done"], t + 1)
                    pe.wait_ge(S["piece_split"], 2 * len(PIECES))
                if c >= 2:
                    pe.wait_ge(S["bf_done"], NC * t + c - 1)
                o = G[c % 2][:, 0:T2]
                split_mm(o, [(cols(w12_hi, w12_lo, kc * INTER + c * P, P),
                              (bT_hi[:, bass.ds(t * PW + kc * T2, T2)], bT_lo[:, bass.ds(t * PW + kc * T2, T2)])) for kc in range(KC)], last=False)
                MM(o, spread[:, c * P:(c + 1) * P], penT[:, pair(t, T2)], start=False, stop=True, skip_group_check=True).then_inc(S["up_done"], 1)

            run(pe, {"A.T": a_T, "A.qkv": a_qkv, "A.qkT": a_qkT, "A.s": a_s, "A.mT": a_mT, "A.st": a_st, "A.pv": a_pv, "A.oT": a_oT,
                     "A.aT": a_aT, "A.o": a_o, "F.T": f_T, "F.up": f_up, "F.dn": down("h_lo_done", wd_hi, wd_lo, 0, "dn_part"),
                     "L.T": l_T, "L.sc": l_sc, "L.pT": l_pT, "L.ro": l_ro, "L.end": l_end,
                     "R.T": r_T, "R.rt": r_rt, "R.lT": r_lT, "R.pT": r_pT, "B.up": b_up,
                     "B.dn": down("bh_lo", w12_hi, w12_lo, W2O, "bdn_part")})


def kernel(**inputs):
    import numpy as np
    import concourse.bacc as bacc
    from concourse.bass_utils import run_bass_kernel_spmd

    def arr(n):
        return np.asarray(inputs[n])

    def chunked(wT):
        k, n = wT.shape
        return wT.reshape(k // 128, 128, n).transpose(1, 0, 2).reshape(128, -1)

    x, c = arr("x"), arr("ctx_2048")
    wr, br = arr("L1_ffn_Wr").T, arr("L1_ffn_br").reshape(-1, 1)
    data = {
        "x": x, "ctx": c,
        "ctxT": c.reshape(8, 128, 2, 128).transpose(3, 0, 2, 1).reshape(128, -1),
        "mask": arr("mask_BxS2_bk0").reshape(-1).view(np.uint32),
        "gx": arr("g_xattn"), "gf": arr("g_ffn"),
        "wq": chunked(arr("L0_xattn_q_w").T), "qb": arr("L0_xattn_q_b"),
        "wkv": chunked(np.concatenate([arr("L0_xattn_k_img_w").T, arr("L0_xattn_v_img_w").T], 1)),
        "kb": arr("L0_xattn_k_img_b"), "vb": arr("L0_xattn_v_img_b"),
        "wo": chunked(arr("L0_xattn_o_w").T), "ob": arr("L0_xattn_o_b"),
        "nq": arr("L0_xattn_norm_q_w"), "nk": arr("L0_xattn_norm_k_img_w"),
        "wgu": chunked(arr("L0_ffn_w_gate_up").T), "wd": chunked(arr("L0_ffn_w_down").T),
        "wr": chunked(np.concatenate([wr, np.zeros((wr.shape[0], 128 - wr.shape[1]), wr.dtype)], 1)),
        "br": np.concatenate([br, np.zeros((32 - br.shape[0], 1), br.dtype)]),
        "w1": chunked(arr("L1_ffn_W1").T), "w2": chunked(arr("L1_ffn_W2").T),
    }
    nc = bacc.Bacc("TRN2", target_bir_lowering=False, num_devices=1)
    arrays, args = {}, {}
    for n, a in data.items():
        a = np.ascontiguousarray(a)
        arrays["in_" + n] = a
        args[n] = nc.dram_tensor("in_" + n, a.shape, mybir.dt.from_np(a.dtype), kind="ExternalInput").ap()
    out = nc.dram_tensor("out_x", x.shape, mybir.dt.float32, kind="ExternalOutput").ap()
    a = args
    build(nc, a["x"], a["ctx"], a["ctxT"], a["mask"], a["gx"], a["gf"], a["wq"], a["qb"], a["wkv"], a["kb"], a["vb"],
          a["wo"], a["ob"], a["nq"], a["nk"], a["wgu"], a["wd"], a["wr"], a["br"], a["w1"], a["w2"], out)
    r = run_bass_kernel_spmd(nc, [arrays], core_ids=[0])
    return r.results[0]["out_x"]
```

```python
import concourse.bass as bass
from concourse import mybir
from contextlib import ExitStack


def build(nc, x_d, ctx_d, ctxT_d, mask_d, rows_d, wq_d, wkv_d, wo_d, wgu_d, wd_d, wr_d, br_d, w1_d, w2_d, out_d):
    f32, f32r, f16, bf16, u8 = (mybir.dt.float32, mybir.dt.float32r, mybir.dt.float16,
                                mybir.dt.bfloat16, mybir.dt.uint8)
    ALU, ACT, AX = mybir.AluOpType, mybir.ActivationFunctionType, mybir.AxisListType

    P = 128
    NT = x_d.shape[0]
    D = x_d.shape[2]
    KC = D // P
    NP = NT // 2
    PW = 2 * D
    T2 = 2 * P
    NH, HD = 16, 16
    HP = 32
    INTER = wd_d.shape[1] // D * P
    NC = INTER // P
    NB, TOPK, BLK = 16, 4, 64
    MASKED = -1e30 * D ** 0.5
    UNPICKED = -1e30
    EXP_LOW = -87.3365
    PAD = -1e30

    ctx = ExitStack()
    with ctx:
        def sb(name, shape, dt=f32):
            return ctx.enter_context(nc.sbuf_tensor(name, shape, dt))

        def sem(name):
            return ctx.enter_context(nc.semaphore(name))

        xs = sb("xs", [P, NT * D])
        cs = sb("cs", [P, NT * D])
        csT = sb("csT", [P, NT * D])
        NQ, NKV = KC * D, KC * 2 * D
        W2O = KC * INTER
        WEIGHTS = [("wa", KC * 4 * D), ("wgu", KC * 2 * INTER), ("wd", NC * D), ("wr", KC * P), ("w12", W2O + NC * D)]
        with ExitStack() as arriving:
            wa_raw, wgu_raw, wd_raw, wr_raw, w12_raw = [arriving.enter_context(nc.sbuf_tensor(f"{n}_raw", [P, c], f32)) for n, c in WEIGHTS]
        wlo_a, wgu_lo, wd_lo, wr_lo, w12_lo = [sb(f"{n}_lo", [P, c], f32r) for n, c in WEIGHTS]
        wgu_hi, wd_hi, wr_hi, w12_hi = [sb(f"{n}_hi", [P, c], f32r) for n, c in WEIGHTS[1:]]
        rows = sb("rows", [P, 6 * D + 4])
        qb, kb, vb, ob, nqw, nkw = [rows[:, i * D:(i + 1) * D] for i in range(6)]
        graw = rows[:, 6 * D:]
        gob = sb("gob", [P, D])
        wn = sb("wn", [P, D])
        wn_max, wn_inv, sc_exp = sb("wn_max", [P, 1]), sb("wn_inv", [P, 1]), sb("sc_exp", [P, 1])
        br_col = sb("br_col", [HP, 1])
        gate = sb("gate", [P, 4])
        gf0_half = sb("gf0_half", [P, 1])
        mask_words = sb("mask_words", [P, NT * P // 4], mybir.dt.uint32)
        mask_all = mask_words[:].bitcast(u8)
        valid = sb("valid", [P, NT])
        neg_half = sb("neg_half", [P, 4])
        ident = sb("ident", [P, P])
        ident16, identb = sb("ident16", [P, P], f16), sb("identb", [P, P], bf16)
        pick_row = sb("pick_row", [P, 8 * P], f16)
        spread = sb("spread", [P, NC * P], bf16)

        bn_a, var_a, vare_a, rstd_a = sb("bn_a", [P, 12]), sb("var_a", [P, 4]), sb("vare_a", [P, 2]), sb("rstd_a", [P, 2])
        ssq, msq, rms = sb("ssq", [P, 4]), sb("msq", [P, 4]), sb("rms", [P, 4])
        mx = sb("mx", [P, 2 * NH])
        nm16 = sb("nm16", [P, 2 * P], f16)
        mT = sb("mT", [P, 2 * P], f16)
        rden = sb("rden", [P, 2 * NH])
        bn_f, var_f, vare_f, rstd_f = sb("bn_f", [P, 12]), sb("var_f", [P, 4]), sb("vare_f", [P, 2]), sb("rstd_f", [P, 2])
        xn_f = sb("xn_f", [P, PW])
        fT_hi, fT_lo = sb("fT_hi", [P, PW], f32r), sb("fT_lo", [P, PW], f32r)
        HB = 4
        hf = sb("hf", [P, HB * T2])
        h_hi, h_lo = sb("h_hi", [P, HB * T2], f32r), sb("h_lo", [P, HB * T2], f32r)
        bn_l, var_l, vare_l, rstd_l = sb("bn_l", [P, 12]), sb("var_l", [P, 4]), sb("vare_l", [P, 2]), sb("rstd_l", [P, 2])
        xn_l = sb("xn_l", [P, PW])
        lT = sb("lT", [P, 2 * KC * P])
        mask2 = sb("mask2", [P, T2], u8)
        sc = sb("sc", [P, T2])
        nmx, nmx_s, den = sb("nmx", [P, 2]), sb("nmx_s", [P, 2]), sb("den", [P, 2])
        pl, plT = sb("pl", [P, T2]), sb("plT", [P, T2])
        rec, coef = sb("rec", [P, 2]), sb("coef", [P, 2])
        bn_b, var_b, vare_b, rstd_b = sb("bn_b", [P, 12]), sb("var_b", [P, 4]), sb("vare_b", [P, 2]), sb("rstd_b", [P, 2])
        t8, rep = sb("t8", [P, 16]), sb("rep", [P, 16])
        lgv, mr = sb("lgv", [P, 2 * 24]), sb("mr", [P, 2 * 24])
        pen = sb("pen", [P, T2], bf16)
        with ExitStack() as place:
            def sa(name, shape, dt=f32):
                return place.enter_context(nc.sbuf_tensor(name, shape, dt))
            whi_a = sa("whi_a", [P, KC * 4 * D], f32r)
            xn_a = sa("xn_a", [P, PW])
            aT_hi, aT_lo = sa("aT_hi", [P, PW], f32r), sa("aT_lo", [P, PW], f32r)
            c_hi, c_lo = sa("c_hi", [P, PW], f32r), sa("c_lo", [P, PW], f32r)
            qk_pre = sa("qk_pre", [P, 2 * D])
            q_pre, k_pre = qk_pre[:, 0:D], qk_pre[:, D:]
            junk = sa("junk", [P, D], bf16)
            v_aug = sa("v_aug", [P, 2 * NH * HP])
            q16, k16 = sa("q16", [P, 4 * D], f16), sa("k16", [P, 4 * D], f16)
            QT, KT = sa("QT", [P, 2 * 8 * P], f16), sa("KT", [P, 2 * 8 * P], f16)
            PTs = sa("PTs", [P, 2 * 8 * P])
            PT = [PTs[:, 0:8 * P], PTs[:, 8 * P:]]
            po = sa("po", [P, 4 * P])
            attn = sa("attn", [P, D])
            oT_hi, oT_lo = sa("oT_hi", [P, D], f32r), sa("oT_lo", [P, D], f32r)
        with ExitStack() as place:
            xn_b = sa("xn_b", [P, PW])
            bT_hi, bT_lo = sa("bT_hi", [P, NP * PW], f32r), sa("bT_lo", [P, NP * PW], f32r)
            lgT = sa("lgT", [HP, T2])
            penT = sa("penT", [P, NP * T2], bf16)

        def bank(name, cols=512):
            return ctx.enter_context(nc.psum_tensor(name, [P, cols], f32))
        G = [bank("G0"), bank("G1")]
        DN = bank("DN")
        W = [bank("W0", 1024), bank("W1", 1024)]
        M = bank("M")

        S = {n: sem(n) for n in """
            x0_in x_in ctxT0_in ctxT_in ctx_in qkv_in o_in rows_in mask_in stores
            consts rows_ready gates_ready ident_ready patterns_ready wqkv_hi wqkv_split wo_split piece_split
            a_stats a_var a_vare a_rstd a_xn a_T a_hi a_lo c_hi_done c_split gob_added
            qkv_done q_pre_done k_pre_done v_done ss_done msq_done rms_done qn_done kn_done q16_hi k16_hi q16_lo k16_lo
            qkT_done QT_done KT_done s_done max_done nm_hi nm_done mT_ps mT_done st_done PT_done pv_done po_done
            oTok_done rden_done attn_done oT_ps oT_hi_done oT_lo_done o_done x1_done
            f_stats f_var f_vare f_rstd f_xn f_T f_hi f_lo gu_done th_done uu_done hf_done h_hi_done h_lo_done dn_part x2_done
            l_stats l_var l_vare l_rstd l_xn l_T lT_done l_sc mask_sel sc_filled l_sel l_max l_maxs lp_done rec_done coef_done plT_ps plT_done ro_done x3_done
            b_stats b_var b_vare b_rstd b_xn b_T b_hi b_lo rt_ps lg_done lgT_ps t8_done lgv_done rep_done mr_done pen_done penT_ps penT_done
            up_done bf_done bh_hi bh_lo bdn_part x4_done wn_mul wn_abs wn_rec""".split()}

        LOAD, PIECE = 1024, 512
        LOADS = [(wgu_d, i, wgu_raw, wgu_hi, wgu_lo, i, LOAD) for i in range(0, KC * 2 * INTER, LOAD)]
        LOADS += [(wd_d, i, wd_raw, wd_hi, wd_lo, i, LOAD) for i in range(0, NC * D, LOAD)]
        LOADS += [(wr_d, 0, wr_raw, wr_hi, wr_lo, 0, KC * P)]
        EARLY_LOADS = len(LOADS)
        LOADS += [(w1_d, i, w12_raw, w12_hi, w12_lo, i, LOAD) for i in range(0, W2O, LOAD)]
        LOADS += [(w2_d, i, w12_raw, w12_hi, w12_lo, W2O + i, LOAD) for i in range(0, NC * D, LOAD)]
        loaded = [sem(f"loaded{i}") for i in range(len(LOADS))]
        PIECES = [(n, raw, hi, lo, col + i, min(PIECE, cols)) for n, (_, _, raw, hi, lo, col, cols) in enumerate(LOADS)
                  for i in range(0, cols, PIECE)]
        EARLY = sum(n < EARLY_LOADS for n, *_ in PIECES)

        block = ctx.enter_context(nc.Block())

        BODY = {
            "tensor": """
                E.dn2 E.up4 E.up5 C.st0 E.up6 C.st1 E.up7 C.pv0 A.T0 C.oT0 A.qkv0 C.aT0 C.o0 E.dn3 E.dn4 E.dn5 E.dn6 E.dn7
                A.qkT0 F.T0 A.s0 F.up0 A.s1 F.up1 A.mT0 A.qkv1 D.st0 L.T0 F.up2 F.dn0 D.st1 L.sc0 F.up3 A.qkT1 D.pv0 A.s2 L.pT0
                D.oT0 D.aT0 A.s3 F.dn1 L.ro0 D.o0 A.mT1""",
            "vector": """
                E.up4 E.up5 A.ln0 A.xn0 E.up6 E.up7 A.T0 C.oT0 A.qkv0 C.aT0 A.msq0 C.o0 A.nrm0 F.ln0 A.lo0 F.xn0 E.dn7 A.qkT0
                F.T0 A.s0 A.s1 L.ln0 F.up0 L.xn0 A.qkv1 F.up1 A.msq1 A.nrm1 A.lo1 L.sc0 F.up2 A.qkT1 A.s2 L.pT0 D.oT0 F.up3
                D.aT0 A.s3 D.o0 L.ro0""",
            "scalar": """
                E.up4 E.up5 A.ln0 C.st0 E.hi4 E.hi5 C.st1 E.up6 E.up7 C.pv0 A.T0 C.aT0 A.qkv0 E.hi6 E.hi7 A.nrm0 A.qkT0 F.T0
                F.up0 F.up1 A.mT0 F.hi0 A.qkv1 L.T0 D.st0 A.nrm1 F.hi1 F.up2 D.st1 L.sc0 A.qkT1 F.up3 D.pv0 D.aT0 F.hi2 L.pT0
                A.mT1 F.hi3""",
            "gpsimd": """
                A.ln0 A.T0 E.hi4 E.hi5 A.msq0 E.hi6 E.hi7 A.lo0 F.ln0 L.ln0 F.hi0 A.msq1 A.lo1 F.hi1 F.hi2 F.hi3""",
        }
        TAIL = {
            "tensor": """
                E.up4 C.st0 E.up5 C.st1 E.up6 C.pv0 E.up7 C.oT0 E.dn2 E.dn3 C.aT0 C.o0 E.dn4 E.dn5 E.dn6 E.dn7 F.T0 F.up0 F.up1
                L.T0 L.sc0 F.up2 F.up3 L.pT0 L.ro0 F.dn0 F.dn1 R.T0 R.rt0""",
            "vector": """
                E.up4 E.up5 C.oT0 E.up6 E.up7 C.aT0 C.o0 F.ln0 E.dn7 L.ln0 F.xn0 L.xn0 F.T0 F.up0 F.up1 L.sc0 L.pT0 F.up2 F.up3
                L.ro0 R.ln0 R.xn0 R.T0 R.rt0""",
            "scalar": """
                E.up4 C.st0 E.up5 C.st1 E.hi4 C.pv0 E.up6 E.up7 E.hi5 E.hi6 C.aT0 E.hi7 F.T0 F.up0 F.up1 L.T0 L.sc0 F.up2 F.up3
                L.pT0 F.hi0 F.hi1 F.hi2 F.hi3 R.T0""",
            "gpsimd": """
                E.hi4 E.hi5 E.hi6 E.hi7 F.ln0 L.ln0 F.hi0 F.hi1 F.hi2 F.hi3 R.ln0""",
        }
        JOIN = {
            "tensor": """
                E.up4 E.up5 E.dn2 R.lT0 E.up6 E.up7 E.dn3 E.dn4 R.pT0 E.dn5 E.dn6 E.dn7 B.up0 B.up1 B.up2 L.T0 B.up3 L.sc0 B.dn0
                L.pT0 B.dn1 L.ro0 B.up4 B.up5 B.up6 B.up7 Q.T0 B.dn2 B.dn3 Q.rt0 B.dn4 Q.lT0 B.dn5 B.dn6 Q.pT0 B.dn7""",
            "vector": """
                E.up4 E.up5 R.lT0 E.up6 E.up7 R.pT0 E.dn7 L.ln0 B.up0 B.up1 L.xn0 L.sc0 L.pT0 L.ro0 Q.ln0 B.up2 B.up3 B.up4
                Q.xn0 B.up5 Q.T0 B.up6 B.up7 Q.rt0 Q.lT0 Q.pT0 B.dn7""",
            "scalar": """
                E.up4 E.up5 E.hi4 E.hi5 E.up6 E.up7 E.hi6 E.hi7 B.up0 B.up1 L.T0 L.sc0 L.pT0 B.up2 B.up3 B.up4 B.up5 Q.T0 B.up6
                B.up7""",
            "gpsimd": """
                E.hi4 E.hi5 E.hi6 E.hi7 L.ln0 B.up0 B.up1 Q.ln0 B.up2 B.up3 B.up4 B.up5 B.up6 B.up7""",
        }
        MIX = {
            "tensor": """
                B.up0 B.up1 B.up2 B.up3 B.up4 R.T0 B.up5 B.up6 R.rt0 B.dn0 B.dn1 R.lT0 B.dn2 B.dn3 B.up7 B.dn4 B.dn5 R.pT0 B.dn6
                B.dn7""",
            "vector": """
                R.ln0 B.up0 R.xn0 B.up1 R.T0 B.up2 R.rt0 B.up3 B.up4 R.lT0 B.up5 B.up6 B.up7 R.pT0 B.dn7""",
            "scalar": """
                B.up0 B.up1 B.up2 B.up3 B.up4 R.T0 B.up5 B.up6 B.up7""",
            "gpsimd": """
                R.ln0 B.up0 B.up1 B.up2 B.up3 B.up4 B.up5 B.up6 B.up7""",
        }

        def run(eng, kind, steps):
            def go(order, **pair_of):
                for word in order[kind].split():
                    name, i = word[:-1], int(word[-1])
                    if name[0] in pair_of:
                        step = {"E": "F", "Q": "R", "C": "D"}.get(name[0], name[0]) + name[1:]
                        if step in steps:
                            steps[step](pair_of[name[0]], *((int(name[0] == "C"), i) if step[0] == "D" else (i,)))

            go(BODY, A=0, D=0)
            go(BODY, A=1, D=1, C=0, F=0)
            with eng.Fori(2, NP) as p:
                go(BODY, A=p, D=p, C=p - 1, F=p - 1, E=p - 2, L=p - 2)
            go(TAIL, C=NP - 1, F=NP - 1, E=NP - 2, L=NP - 2, R=0)
            go(JOIN, E=NP - 1, L=NP - 1, R=0, Q=1, B=0)
            with eng.Fori(1, NP - 1) as r:
                go(MIX, B=r, R=r + 1)
            go(MIX, B=NP - 1)

        def wait_late(eng, name, count):
            if not isinstance(count, int) or count > 0:
                eng.wait_ge(S[name], count)

        def wait_apart(eng, name, value):
            v = value if isinstance(value, int) else eng.snap(value)
            eng.wait_ge(S["consts"], 1)
            eng.wait_ge(S[name], v)

        def parts(which, s):
            v = (q16, k16)[which][:].rearrange("p (h a b c) -> p h a b c", a=2, b=2, c=HD)
            return v[:, :, :, s, :] if which else v[:, :, s, :, :]

        def twice(src):
            return src.rearrange("p (h c) -> p h c", c=HD).unsqueeze(2).to_broadcast([P, NH, 2, HD])

        def pair(t, w=PW):
            return bass.ds(t * w, w)

        @block.sync
        def _(sp):
            x_rows = xs[:].rearrange("p (t d) -> p t d", t=NT)
            sp.dma_start(x_rows[:, 0:2], x_d[0:2].rearrange("t p d -> p t d")).then_inc(S["x0_in"], 16)
            sp.dma_start(wa_raw[:, 0:NQ], wq_d).then_inc(S["qkv_in"], 16)
            sp.dma_start(wa_raw[:, NQ:NQ + NKV], wkv_d).then_inc(S["qkv_in"], 16)
            sp.dma_start(wa_raw[:, NQ + NKV:], wo_d).then_inc(S["o_in"], 16)
            sp.dma_start(x_rows[:, 2:], x_d[2:].rearrange("t p d -> p t d")).then_inc(S["x_in"], 16)
            sp.dma_start(csT[:, PW:], ctxT_d[:, PW:]).then_inc(S["ctxT_in"], 16)
            for n, (src, at, raw, _, _, col, cols) in enumerate(LOADS):
                sp.dma_start(raw[:, col:col + cols], src[:, at:at + cols]).then_inc(loaded[n], 16)
            sp.dma_start(cs[:].rearrange("p (t d) -> p t d", t=NT), ctx_d.rearrange("t p d -> p t d")).then_inc(S["ctx_in"], 16)
            with sp.Fori(0, NP) as r:
                sp.wait_ge(S["x4_done"], r + 1)
                sp.dma_start(out_d[bass.ds(r * 2, 2), :, :].rearrange("t p d -> p t d"),
                             xs[:, pair(r)].rearrange("p (t d) -> p t d", t=2)).then_inc(S["stores"], 16)
            sp.wait_ge(S["stores"], 16 * NP)

        @block.gpsimd
        def _(pool):
            def patterns():
                nc.gpsimd.memset(v_aug[:], 0.0).then_inc(S["consts"], 1)
                nc.gpsimd.memset(nm16[:], 0.0).then_inc(S["consts"], 1)
                nc.gpsimd.memset(pen[:], 0.0).then_inc(S["consts"], 1)
                nc.gpsimd.memset(rep[:], PAD).then_inc(S["consts"], 1)
                nc.gpsimd.memset(lgv[:], PAD).then_inc(S["consts"], 1)
                for m in (ident16, identb, pick_row, spread):
                    nc.gpsimd.memset(m[:], 0.0).then_inc(S["consts"], 1)
                pool.wait_ge(S["consts"], 11)
                nc.gpsimd.memset(v_aug[:].rearrange("p (h c) -> p h c", c=HP)[:, :, HD:HD + 1], 1.0).then_inc(S["patterns_ready"], 1)
                for m in (ident16, identb):
                    nc.gpsimd.affine_select(out=m[:], in_=m[:], compare_op=ALU.not_equal, fill=1.0, base=0,
                                            pattern=[[-1, P]], channel_multiplier=1).then_inc(S["patterns_ready"], 1)
                done = 3
                for base in (0, 8, 64, 72):
                    pool.wait_ge(S["patterns_ready"], done)
                    v = pick_row[:].rearrange("p (i k) -> p i k", k=P)
                    nc.gpsimd.affine_select(out=v, in_=v, compare_op=ALU.not_equal, fill=1.0, base=-base,
                                            pattern=[[-1, 8], [0, P]], channel_multiplier=1).then_inc(S["patterns_ready"], 1)
                    done += 1
                v = spread[:].rearrange("p (c b m) -> p (c b) m", b=2, m=BLK)
                nc.gpsimd.affine_select(out=v, in_=v, compare_op=ALU.not_equal, fill=1.0, base=0,
                                        pattern=[[-1, NB], [0, BLK]], channel_multiplier=1).then_inc(S["patterns_ready"], 1)

            def split(raw, hi, lo, done, before):
                nc.gpsimd.tensor_scalar(hi, raw, 1.0, 0.0, ALU.mult, ALU.add).then_inc(S[done], 1)
                pool.wait_ge(S[done], before + 1)
                nc.gpsimd.tensor_tensor(lo, raw, hi.bitcast(f32), ALU.subtract).then_inc(S[done], 1)

            def split_piece(n):
                load, raw, hi, lo, col, cols = PIECES[n]
                at = slice(col, col + cols)
                pool.wait_ge(loaded[load], 16)
                split(raw[:, at], hi[:, at], lo[:, at], "piece_split", 2 * n)

            def ln(kind, vare, out):
                def step(t, _):
                    pool.wait_ge(S[f"{kind}_vare"], t + 1)
                    nc.gpsimd.tensor_tensor(out[:], vare[:], neg_half[:, 0:2], ALU.pow).then_inc(S[f"{kind}_rstd"], 1)
                    if kind == "a":
                        pool.wait_ge(S["c_hi_done"], t + 1)
                        nc.gpsimd.tensor_tensor(c_lo[:], csT[:, pair(t)], c_hi[:].bitcast(f32), ALU.subtract).then_inc(S["c_split"], 1)
                        if isinstance(t, int) and t == 0:
                            patterns()
                return step

            def a_T(t, _):
                if isinstance(t, int) and t == 0:
                    pool.wait_ge(S["rows_ready"], 5)
                pool.wait_ge(S["a_xn"], 2 * t + 2)
                nc.gpsimd.tensor_tensor(xs[:, pair(t)].rearrange("p (j d) -> p j d", d=D), xs[:, pair(t)].rearrange("p (j d) -> p j d", d=D),
                                        gob[:].unsqueeze(1).to_broadcast([P, 2, D]), ALU.add).then_inc(S["gob_added"], 1)

            def a_msq(t, j):
                pool.wait_ge(S["msq_done"], 2 * t + j + 1)
                nc.gpsimd.tensor_tensor(rms[:, 2 * j:2 * j + 2], msq[:, 2 * j:2 * j + 2], neg_half[:, 0:2], ALU.pow).then_inc(S["rms_done"], 1)

            def a_lo(t, j):
                pool.wait_ge(S["k16_hi"], 2 * t + j + 1)
                nc.gpsimd.tensor_tensor(parts(1, 1), twice(k_pre), parts(1, 0), ALU.subtract).then_inc(S["k16_lo"], 1)
                if isinstance(t, int) and t == 0 and j == 0:
                    pool.wait_ge(S["o_in"], 16)
                    split(wa_raw[:, NQ + NKV:], whi_a[:, NQ + NKV:], wlo_a[:, NQ + NKV:], "wo_split", 0)
                if isinstance(t, int) and t == 0:
                    for n in (range(0, 4), range(4, EARLY))[j]:
                        split_piece(n)

            def low_of_hidden(hi_done, lo_done):
                def step(t, c):
                    pool.wait_ge(S[hi_done], NC * t + c + 1)
                    b = c % HB * T2
                    nc.gpsimd.tensor_tensor(h_lo[:, b:b + T2], hf[:, b:b + T2], h_hi[:, b:b + T2].bitcast(f32),
                                            ALU.subtract).then_inc(S[lo_done], 1)
                return step

            def f_hi(t, c):
                low_of_hidden("h_hi_done", "h_lo_done")(t, c)
                if isinstance(t, int) and t == 0:
                    for n in range(EARLY + 2 * c, min(EARLY + 2 * c + 2, len(PIECES))):
                        split_piece(n)

            def l_ln(t, _):
                pool.wait_ge(S["mask_in"], 16)
                wait_late(pool, "lp_done", 2 * t)
                nc.gpsimd.tensor_copy(mask2[:], mask_all[:, pair(t, T2)]).then_inc(S["mask_sel"], 1)
                nc.gpsimd.memset(sc[:], MASKED).then_inc(S["sc_filled"], 1)
                ln("l", vare_l, rstd_l)(t, 0)

            nc.gpsimd.memset(neg_half[:], -0.5).then_inc(S["consts"], 1)
            nc.gpsimd.memset(ident[:], 0.0).then_inc(S["consts"], 1)
            pool.wait_ge(S["consts"], 2)
            nc.gpsimd.affine_select(out=ident[:], in_=ident[:], compare_op=ALU.not_equal, fill=1.0, base=0,
                                    pattern=[[-1, P]], channel_multiplier=1).then_inc(S["ident_ready"], 1)
            run(pool, "gpsimd", {"A.ln": ln("a", vare_a, rstd_a), "A.T": a_T, "A.msq": a_msq, "A.lo": a_lo, "F.ln": ln("f", vare_f, rstd_f),
                       "F.hi": f_hi, "L.ln": l_ln, "R.ln": ln("b", vare_b, rstd_b), "B.up": low_of_hidden("bh_hi", "bh_lo")})

        @block.scalar
        def _(act):
            act.dma_start(csT[:, 0:PW], ctxT_d[:, 0:PW]).then_inc(S["ctxT0_in"], 16)
            act.dma_start(rows[:], rows_d.partition_broadcast(P)).then_inc(S["rows_in"], 16)
            act.dma_start(br_col[:], br_d).then_inc(S["rows_in"], 16)
            act.dma_start(mask_words[:], mask_d.partition_broadcast(P)).then_inc(S["mask_in"], 16)
            def copy(out, in_, s):
                nc.scalar.activation(out, in_, ACT.Copy).then_inc(S[s], 1)

            def a_ln(t, _):
                if isinstance(t, int):
                    act.wait_ge(S["ctxT_in" if t else "ctxT0_in"], 16)
                wait_late(act, "qkv_done", 2 * t)
                copy(c_hi[:], csT[:, pair(t)], "c_hi_done")
                if isinstance(t, int) and t == 0:
                    act.wait_ge(S["qkv_in"], 32)
                    copy(whi_a[:, 0:NQ + NKV], wa_raw[:, 0:NQ + NKV], "wqkv_hi")
                    act.wait_ge(S["rows_in"], 32)
                    nc.scalar.activation(gate[:], graw, ACT.Tanh).then_inc(S["gates_ready"], 1)

            def a_T(t, _):
                act.wait_ge(S["a_T"], t + 1)
                copy(aT_hi[:], W[0][:, 0:PW], "a_hi")

            def a_qkv(t, j):
                n = 2 * t + j + 1
                for i, (s, src) in enumerate((("q_pre_done", q_pre), ("k_pre_done", k_pre))):
                    act.wait_ge(S[s], n)
                    wait_late(act, "ss_done", 2 * (n - 1) + i)
                    nc.scalar.activation(junk[:], src, ACT.Square, scale=D ** -0.5,
                                         accum_out=ssq[:, 2 * j + i:2 * j + i + 1]).then_inc(S["ss_done"], 1)

            def a_nrm(t, j):
                n = 2 * t + j + 1
                act.wait_ge(S["kn_done"], n)
                copy(parts(1, 0), twice(k_pre), "k16_hi")
                act.wait_ge(S["qn_done"], n)
                copy(parts(0, 0), twice(q_pre), "q16_hi")

            def a_qkT(t, j):
                act.wait_ge(S["qkT_done"], 2 * t + j + 1)
                copy(QT[:, j * 1024:(j + 1) * 1024], W[0][:, 0:512].bitcast(f16), "QT_done")

            def a_mT(t, j):
                act.wait_ge(S["mT_ps"], 2 * t + j + 1)
                copy(mT[:, j * P:(j + 1) * P], W[0][:, 0:P // 2].bitcast(f16), "mT_done")

            def d_st(t, j, half):
                act.wait_ge(S["st_done"], 2 * (2 * t + j) + half + 1)
                wait_late(act, "pv_done", 2 * t + j)
                nc.scalar.activation(PT[half], W[1][:], ACT.Exp, scale=sc_exp[:]).then_inc(S["PT_done"], 1)

            def d_pv(t, j, _):
                act.wait_ge(S["pv_done"], 2 * t + j + 1)
                copy(po[:], W[1][:, 0:512], "po_done")

            def d_aT(t, j, _):
                act.wait_ge(S["oT_ps"], 2 * t + j + 1)
                copy(oT_hi[:], W[1][:, 0:D], "oT_hi_done")

            def f_T(t, _):
                act.wait_ge(S["f_T"], t + 1)
                copy(fT_hi[:], M[:], "f_hi")

            def f_up(t, c):
                k, b = NC * t + c + 1, c % HB * T2
                act.wait_ge(S["gu_done"], k)
                wait_late(act, "h_lo_done", k - HB)
                nc.scalar.activation(hf[:, b:b + T2], G[c % 2][:, 0:T2], ACT.Tanh, scale=0.5).then_inc(S["th_done"], 1)

            def f_hi(t, c):
                k, b = NC * t + c + 1, c % HB * T2
                act.wait_ge(S["hf_done"], k)
                wait_late(act, "dn_part", k - HB)
                copy(h_hi[:, b:b + T2], hf[:, b:b + T2], "h_hi_done")

            def l_T(t, _):
                act.wait_ge(S["l_T"], t + 1)
                copy(lT[:], M[:], "lT_done")

            def l_sc(t, _):
                act.wait_ge(S["l_maxs"], t + 1)
                for j in range(2):
                    nc.scalar.activation(pl[:, j * P:(j + 1) * P], sc[:, j * P:(j + 1) * P], ACT.Exp, scale=D ** -0.5,
                                         bias=nmx_s[:, j:j + 1], accum_out=den[:, j:j + 1]).then_inc(S["lp_done"], 1)

            def l_pT(t, _):
                act.wait_ge(S["plT_ps"], t + 1)
                copy(plT[:], M[:, 0:T2], "plT_done")

            def r_T(t, _):
                act.wait_ge(S["b_T"], t + 1)
                copy(bT_hi[:, pair(t)], M[:], "b_hi")

            def b_up(t, c):
                k, b = NC * t + c + 1, c % HB * T2
                act.wait_ge(S["up_done"], k)
                if isinstance(t, int) and k <= HB:
                    act.wait_ge(S["h_lo_done"], NC * NP)
                wait_late(act, "bh_lo", k - HB)
                nc.scalar.activation(hf[:, b:b + T2], G[c % 2][:, 0:T2], ACT.Gelu).then_inc(S["bf_done"], 1)

            run(act, "scalar", {"A.ln": a_ln, "A.T": a_T, "A.qkv": a_qkv, "A.nrm": a_nrm, "A.qkT": a_qkT, "A.mT": a_mT, "D.st": d_st, "D.pv": d_pv,
                      "D.aT": d_aT, "F.T": f_T, "F.up": f_up, "F.hi": f_hi, "L.T": l_T, "L.sc": l_sc, "L.pT": l_pT, "R.T": r_T, "B.up": b_up})

        @block.vector
        def _(dve):
            V = nc.vector
            def constants():
                dve.wait_ge(S["rows_in"], 32)
                V.tensor_tensor(wn[:], nqw, nkw, ALU.mult).then_inc(S["wn_mul"], 1)
                dve.wait_ge(S["wn_mul"], 1)
                V.tensor_reduce(wn_max[:], wn[:], AX.X, ALU.max, apply_absolute_value=True).then_inc(S["wn_abs"], 1)
                dve.wait_ge(S["wn_abs"], 1)
                V.tensor_scalar(wn_max[:], wn_max[:], 1e-30, None, ALU.max).then_inc(S["wn_abs"], 1)
                dve.wait_ge(S["wn_abs"], 2)
                V.reciprocal(wn_inv[:], wn_max[:]).then_inc(S["wn_rec"], 1)
                V.tensor_scalar(sc_exp[:], wn_max[:], HD ** -0.5, None, ALU.mult).then_inc(S["rows_ready"], 1)
                dve.wait_ge(S["wn_rec"], 1)
                V.tensor_scalar(wn[:], wn[:], wn_inv[:], None, ALU.mult).then_inc(S["rows_ready"], 1)
                dve.wait_ge(S["gates_ready"], 1)
                V.tensor_scalar(gf0_half[:], gate[:, 2:3], 0.5, None, ALU.mult).then_inc(S["rows_ready"], 1)
                V.tensor_scalar(gob[:], ob, gate[:, 0:1], None, ALU.mult).then_inc(S["rows_ready"], 1)
                dve.wait_ge(S["mask_in"], 16)
                V.tensor_reduce(valid[:], mask_all.rearrange("p (t k) -> p t k", k=P), AX.X, ALU.max).then_inc(S["rows_ready"], 1)
                dve.wait_ge(S["rows_ready"], 5)

            def ln(t, kind, src, bn, var, vare):
                for j in range(2):
                    V.bn_stats(bn[:, 6 * j:6 * j + 6], src(j)).then_inc(S[f"{kind}_stats"], 1)
                dve.wait_ge(S[f"{kind}_stats"], 2 * t + 2)
                V.memset(vare[:], 1e-5).then_inc(S[f"{kind}_var"], 1)
                for j in range(2):
                    V.bn_aggr(var[:, 2 * j:2 * j + 2], bn[:, 6 * j:6 * j + 6]).then_inc(S[f"{kind}_var"], 1)
                dve.wait_ge(S[f"{kind}_var"], 3 * t + 3)
                V.tensor_tensor(vare[:], var[:].rearrange("p (j s) -> p j s", s=2)[:, :, 1], vare[:], ALU.add).then_inc(S[f"{kind}_vare"], 1)

            def norm(t, kind, src, var, rs, xn):
                dve.wait_ge(S[f"{kind}_rstd"], t + 1)
                for j in range(2):
                    V.tensor_scalar(xn[:, j * D:(j + 1) * D], src(j), var[:, 2 * j:2 * j + 1], rs[:, j:j + 1],
                                    ALU.subtract, ALU.mult).then_inc(S[f"{kind}_xn"], 1)

            def tile_rows(t):
                return lambda j: xs[:, bass.ds(t * PW + j * D, D)]

            def xn(kind, var, rs, out):
                return lambda t, _: norm(t, kind, tile_rows(t), var, rs, out)

            def low(out, ps, hi, s):
                V.tensor_tensor(out, ps, hi.bitcast(f32), ALU.subtract).then_inc(S[s], 1)

            def a_ln(t, _):
                if isinstance(t, int):
                    dve.wait_ge(S["x_in" if t else "x0_in"], 16)
                ln(t, "a", tile_rows(t), bn_a, var_a, vare_a)

            def a_T(t, _):
                if isinstance(t, int) and t == 0:
                    dve.wait_ge(S["wqkv_hi"], 1)
                    w = slice(0, NQ + NKV)
                    V.tensor_tensor(wlo_a[:, w], wa_raw[:, w], whi_a[:, w].bitcast(f32), ALU.subtract).then_inc(S["wqkv_split"], 1)
                dve.wait_ge(S["a_hi"], t + 1)
                low(aT_lo[:], W[0][:, 0:PW], aT_hi[:], "a_lo")
                if isinstance(t, int) and t == 0:
                    constants()

            def a_qkv(t, j):
                n = 2 * t + j + 1
                dve.wait_ge(S["qkv_done"], n)
                wait_late(dve, "k16_lo", n - 1)
                V.tensor_tensor(q_pre, W[0][:, 512:512 + D], qb, ALU.add).then_inc(S["q_pre_done"], 1)
                V.tensor_tensor(k_pre, W[0][:, 0:D], kb, ALU.add).then_inc(S["k_pre_done"], 1)
                v = v_aug[:, j * NH * HP:(j + 1) * NH * HP].rearrange("p (h c) -> p h c", c=HP)
                if isinstance(t, int) and t == 0:
                    dve.wait_ge(S["patterns_ready"], 8)
                V.tensor_tensor(v[:, :, 0:HD], W[0][:, D:2 * D].rearrange("p (h c) -> p h c", c=HD),
                                vb.rearrange("p (h c) -> p h c", c=HD), ALU.add).then_inc(S["v_done"], 1)

            def a_msq(t, j):
                dve.wait_ge(S["ss_done"], 4 * t + 2 * j + 2)
                V.tensor_scalar(msq[:, 2 * j:2 * j + 2], ssq[:, 2 * j:2 * j + 2], 1e-6, None, ALU.add).then_inc(S["msq_done"], 1)

            def a_nrm(t, j):
                n = 2 * t + j + 1
                dve.wait_ge(S["rms_done"], n)
                V.tensor_scalar(k_pre, k_pre, rms[:, 2 * j + 1:2 * j + 2], None, ALU.mult).then_inc(S["kn_done"], 1)
                V.scalar_tensor_tensor(q_pre, q_pre, rms[:, 2 * j:2 * j + 1], wn[:], ALU.mult, ALU.mult).then_inc(S["qn_done"], 1)

            def a_lo(t, j):
                dve.wait_ge(S["q16_hi"], 2 * t + j + 1)
                V.tensor_tensor(parts(0, 1), twice(q_pre), parts(0, 0), ALU.subtract).then_inc(S["q16_lo"], 1)

            def a_qkT(t, j):
                dve.wait_ge(S["qkT_done"], 2 * t + j + 1)
                V.tensor_copy(KT[:, j * 1024:(j + 1) * 1024], W[0][:, 512:1024].bitcast(f16)).then_inc(S["KT_done"], 1)

            def a_s(t, i):
                j, half = i // 2, i % 2
                dve.wait_ge(S["s_done"], 4 * t + i + 1)
                o = mx[:, j * NH:(j + 1) * NH].rearrange("p (r i) -> p r i", r=2)[:, :, 4 * half:4 * half + 4]
                V.tensor_reduce(o, W[0][:].rearrange("p (r i k) -> p r i k", r=2, k=P), AX.X, ALU.max).then_inc(S["max_done"], 1)
                if half == 1:
                    n = 2 * t + j + 1
                    dve.wait_ge(S["max_done"], 2 * n)
                    m = mx[:, j * NH:(j + 1) * NH].rearrange("p (r i) -> p r i", r=2)
                    o = nm16[:, j * P:(j + 1) * P].rearrange("p (r s) -> p r s", r=2)
                    V.tensor_scalar(o[:, :, 0:8], m, -1.0, None, ALU.mult).then_inc(S["nm_hi"], 1)
                    dve.wait_ge(S["nm_hi"], n)
                    V.scalar_tensor_tensor(o[:, :, 8:16], m, -1.0, o[:, :, 0:8], ALU.mult, ALU.subtract).then_inc(S["nm_done"], 1)

            def d_oT(t, j, _):
                n = 2 * t + j + 1
                dve.wait_ge(S["oTok_done"], n)
                o = W[1][:, 512:].rearrange("p (h c) -> p h c", c=HP)
                V.reciprocal(rden[:, j * NH:(j + 1) * NH], o[:, :, HD]).then_inc(S["rden_done"], 1)
                dve.wait_ge(S["rden_done"], n)
                V.tensor_tensor(attn[:].rearrange("p (h c) -> p h c", c=HD), o[:, :, 0:HD],
                                rden[:, j * NH:(j + 1) * NH].unsqueeze(2).to_broadcast([P, NH, HD]),
                                ALU.mult).then_inc(S["attn_done"], 1)

            def d_aT(t, j, _):
                dve.wait_ge(S["oT_hi_done"], 2 * t + j + 1)
                low(oT_lo[:], W[1][:, 0:D], oT_hi[:], "oT_lo_done")

            def d_o(t, j, _):
                dve.wait_ge(S["o_done"], 2 * t + j + 1)
                dve.wait_ge(S["gob_added"], t + 1)
                x = xs[:, bass.ds(t * PW + j * D, D)]
                V.scalar_tensor_tensor(x, W[1][:, 512:512 + D], gate[:, 0:1], x, ALU.mult, ALU.add).then_inc(S["x1_done"], 1)

            def f_ln(t, _):
                wait_apart(dve, "x1_done", 2 * t + 2)
                ln(t, "f", tile_rows(t), bn_f, var_f, vare_f)

            def f_T(t, _):
                dve.wait_ge(S["f_hi"], t + 1)
                low(fT_lo[:], M[:], fT_hi[:], "f_lo")

            def f_up(t, c):
                k, b = NC * t + c + 1, c % HB * T2
                dve.wait_ge(S["th_done"], k)
                V.scalar_tensor_tensor(hf[:, b:b + T2], hf[:, b:b + T2], 1.0, G[c % 2][:, 0:T2], ALU.add, ALU.mult).then_inc(S["uu_done"], 1)
                dve.wait_ge(S["uu_done"], k)
                V.tensor_tensor(hf[:, b:b + T2], G[c % 2][:, T2:2 * T2], hf[:, b:b + T2], ALU.mult).then_inc(S["hf_done"], 1)

            def f_dn(t, c):
                if c == NC - 1:
                    dve.wait_ge(S["dn_part"], NC * t + NC)
                    V.scalar_tensor_tensor(xs[:, pair(t)], DN[:], gf0_half[:], xs[:, pair(t)], ALU.mult, ALU.add).then_inc(S["x2_done"], 1)

            def l_ln(t, _):
                wait_apart(dve, "x2_done", t + 1)
                ln(t, "l", tile_rows(t), bn_l, var_l, vare_l)

            def l_sc(t, _):
                wait_apart(dve, "l_sc", t + 1)
                dve.wait_ge(S["mask_sel"], t + 1)
                dve.wait_ge(S["sc_filled"], t + 1)
                V.copy_predicated(sc[:], mask2[:], M[:, 0:T2]).then_inc(S["l_sel"], 1)
                dve.wait_ge(S["l_sel"], t + 1)
                V.reduce_max(nmx[:], sc[:].rearrange("p (j k) -> p j k", k=P), AX.X).then_inc(S["l_max"], 1)
                dve.wait_ge(S["l_max"], t + 1)
                V.tensor_scalar(nmx_s[:], nmx[:], -(D ** -0.5), None, ALU.mult).then_inc(S["l_maxs"], 1)

            def l_pT(t, _):
                dve.wait_ge(S["lp_done"], 2 * t + 2)
                V.reciprocal(rec[:], den[:]).then_inc(S["rec_done"], 1)
                dve.wait_ge(S["rec_done"], t + 1)
                V.scalar_tensor_tensor(coef[:], rec[:], gate[:, 1:2], valid[:, bass.ds(t * 2, 2)], ALU.mult, ALU.mult).then_inc(S["coef_done"], 1)

            def l_ro(t, _):
                dve.wait_ge(S["ro_done"], t + 1)
                dve.wait_ge(S["coef_done"], t + 1)
                for j in range(2):
                    V.scalar_tensor_tensor(xs[:, bass.ds(t * PW + j * D, D)], M[:, j * D:(j + 1) * D], coef[:, j:j + 1],
                                           xs[:, bass.ds(t * PW + j * D, D)], ALU.mult, ALU.add).then_inc(S["x3_done"], 1)

            def r_ln(t, _):
                wait_apart(dve, "x3_done", 2 * t + 2)
                ln(t, "b", tile_rows(t), bn_b, var_b, vare_b)

            def r_T(t, _):
                dve.wait_ge(S["b_hi"], t + 1)
                low(bT_lo[:, pair(t)], M[:], bT_hi[:, pair(t)], "b_lo")

            def r_rt(t, _):
                dve.wait_ge(S["rt_ps"], t + 1)
                V.tensor_scalar(lgT[:], W[0][0:HP, 0:T2], br_col[:], None, ALU.add).then_inc(S["lg_done"], 1)

            def r_lT(t, _):
                wait_apart(dve, "lgT_ps", t + 1)
                for j in range(2):
                    V.max(t8[:, 8 * j:8 * j + 8], W[0][:, 512 + HP * j:512 + HP * j + NB]).then_inc(S["t8_done"], 1)
                for j in range(2):
                    dve.wait_ge(S["t8_done"], 2 * t + j + 1)
                    V.tensor_scalar(lgv[:, 24 * j:24 * j + NB], W[0][:, 512 + HP * j:512 + HP * j + NB], t8[:, 8 * j:8 * j + 1], EXP_LOW,
                                    ALU.subtract, ALU.max).then_inc(S["lgv_done"], 1)
                    V.tensor_scalar(rep[:, 8 * j:8 * j + TOPK], t8[:, 8 * j:8 * j + TOPK], t8[:, 8 * j:8 * j + 1], EXP_LOW,
                                    ALU.subtract, ALU.max).then_inc(S["rep_done"], 1)
                for j in range(2):
                    wait_apart(dve, "lgv_done", 2 * t + j + 1)
                    dve.wait_ge(S["rep_done"], 2 * t + j + 1)
                    V.match_replace(mr[:, 24 * j:24 * j + 24], rep[:, 8 * j:8 * j + 8], lgv[:, 24 * j:24 * j + 24], 1.0).then_inc(S["mr_done"], 1)
                for j in range(2):
                    dve.wait_ge(S["mr_done"], 2 * t + j + 1)
                    V.tensor_scalar(pen[:, j * P:j * P + NB], mr[:, 24 * j:24 * j + NB], 0.5, UNPICKED, ALU.is_lt, ALU.mult).then_inc(S["pen_done"], 1)

            def r_pT(t, _):
                dve.wait_ge(S["penT_ps"], t + 1)
                V.tensor_copy(penT[:, pair(t, T2)], W[1][:, 0:P].bitcast(bf16)).then_inc(S["penT_done"], 1)

            def b_up(t, c):
                k, b = NC * t + c + 1, c % HB * T2
                dve.wait_ge(S["bf_done"], k)
                if isinstance(t, int) and k <= HB:
                    dve.wait_ge(S["dn_part"], NC * NP)
                wait_late(dve, "bdn_part", k - HB)
                V.tensor_copy(h_hi[:, b:b + T2], hf[:, b:b + T2]).then_inc(S["bh_hi"], 1)

            def b_dn(t, c):
                if c == NC - 1:
                    dve.wait_ge(S["bdn_part"], NC * t + NC)
                    V.scalar_tensor_tensor(xs[:, pair(t)], DN[:], gate[:, 3:4], xs[:, pair(t)], ALU.mult, ALU.add).then_inc(S["x4_done"], 1)

            run(dve, "vector", {"A.ln": a_ln, "A.T": a_T, "A.qkv": a_qkv, "A.msq": a_msq, "A.nrm": a_nrm, "A.lo": a_lo, "A.qkT": a_qkT, "A.s": a_s,
                      "A.xn": xn("a", var_a, rstd_a, xn_a), "F.xn": xn("f", var_f, rstd_f, xn_f), "L.xn": xn("l", var_l, rstd_l, xn_l),
                      "R.xn": xn("b", var_b, rstd_b, xn_b), "D.oT": d_oT,
                      "D.aT": d_aT, "D.o": d_o, "F.ln": f_ln, "F.T": f_T, "F.up": f_up, "F.dn": f_dn, "L.ln": l_ln, "L.sc": l_sc, "L.pT": l_pT, "L.ro": l_ro,
                      "R.ln": r_ln, "R.T": r_T, "R.rt": r_rt, "R.lT": r_lT, "R.pT": r_pT, "B.up": b_up, "B.dn": b_dn})

        @block.tensor
        def _(pe):
            MM, TR = nc.tensor.matmul, nc.tensor.transpose

            def split_mm(out, terms, first=True, last=True):
                n = 3 * len(terms)
                i = 0
                for (lh, ll), (rh, rl) in terms:
                    for a, b in ((lh, rh), (lh, rl), (ll, rh)):
                        ins = MM(out, a, b, start=first and i == 0, stop=last and i == n - 1, skip_group_check=True)
                        i += 1
                return ins

            def transpose_pair(src, to=M):
                for j in range(2):
                    for kc in range(KC):
                        ins = TR(to[:, kc * T2 + j * P:kc * T2 + (j + 1) * P], src[:, j * D + kc * P:j * D + (kc + 1) * P], ident[:])
                return ins

            def cols(hi, lo, a, n):
                return hi[:, a:a + n], lo[:, a:a + n]

            def a_T(t, _):
                if isinstance(t, int):
                    pe.wait_ge(S["ident_ready"], 1)
                wait_late(pe, "mT_done", 2 * t)
                pe.wait_ge(S["a_xn"], 2 * t + 2)
                transpose_pair(xn_a, W[0]).then_inc(S["a_T"], 1)

            def a_qkv(t, j):
                if j == 0:
                    pe.wait_ge(S["a_lo"], t + 1)
                    pe.wait_ge(S["c_split"], t + 1)
                    if isinstance(t, int):
                        pe.wait_ge(S["wqkv_split"], 1)
                else:
                    pe.wait_ge(S["mT_done"], 2 * t + 1)
                split_mm(W[0][:, 0:512], [(cols(c_hi, c_lo, j * D + kc * P, P), cols(whi_a, wlo_a, NQ + kc * 2 * D, 2 * D))
                                          for kc in range(KC)])
                split_mm(W[0][:, 512:512 + D], [(cols(aT_hi, aT_lo, kc * T2 + j * P, P), cols(whi_a, wlo_a, kc * D, D))
                                                for kc in range(KC)]).then_inc(S["qkv_done"], 1)

            def a_qkT(t, j):
                n = 2 * t + j + 1
                if isinstance(t, int) and t == 0:
                    pe.wait_ge(S["patterns_ready"], 8)
                pe.wait_ge(S["q16_lo"], n)
                pe.wait_ge(S["k16_lo"], n)
                pe.wait_ge(S["v_done"], n)
                o = W[0][:].bitcast(f16)
                for g in range(8):
                    TR(o[:, g * P:(g + 1) * P], q16[:, g * P:(g + 1) * P], ident16[:])
                    ins = TR(o[:, 1024 + g * P:1024 + (g + 1) * P], k16[:, g * P:(g + 1) * P], ident16[:])
                ins.then_inc(S["qkT_done"], 1)

            def head(j, half, c, r):
                a = j * 1024 + (4 * half + c) * P
                return slice(64 * r, 64 * r + 64), slice(a, a + P)

            def a_s(t, i):
                j, half = i // 2, i % 2
                if half == 0:
                    pe.wait_ge(S["KT_done"], 2 * t + j + 1)
                    pe.wait_ge(S["QT_done"], 2 * t + j + 1)
                else:
                    pe.wait_ge(S["max_done"], 4 * t + i)
                for c in range(4):
                    for r in range(2):
                        rows, cc = head(j, half, c, r)
                        ins = MM(W[0][:, r * 512 + c * P:r * 512 + (c + 1) * P], QT[rows, cc], KT[rows, cc],
                                 start=True, stop=True, skip_group_check=True)
                ins.then_inc(S["s_done"], 1)

            def a_mT(t, j):
                pe.wait_ge(S["nm_done"], 2 * t + j + 1)
                TR(W[0][:, 0:P // 2].bitcast(f16), nm16[:, j * P:(j + 1) * P], ident16[:]).then_inc(S["mT_ps"], 1)

            def d_st(t, j, half):
                n = 2 * t + j + 1
                if half == 0:
                    pe.wait_ge(S["mT_done"], n)
                    wait_late(pe, "x1_done", n - 1)
                else:
                    pe.wait_ge(S["PT_done"], 2 * n - 1)
                for c in range(4):
                    for r in range(2):
                        rows, cc = head(j, half, c, r)
                        o = W[1][:, r * 512 + c * P:r * 512 + (c + 1) * P]
                        MM(o, KT[rows, cc], QT[rows, cc], start=True, stop=False, skip_group_check=True)
                        h = 4 * half + c
                        ins = MM(o, pick_row[rows, h * P:(h + 1) * P], mT[rows, j * P:(j + 1) * P], start=False, stop=True,
                                 skip_group_check=True)
                ins.then_inc(S["st_done"], 1)

            def d_pv(t, j, _):
                n = 2 * t + j + 1
                pe.wait_ge(S["PT_done"], 2 * n)
                for h in range(NH):
                    half, c, r = h // 8, h % 8 // 2, h % 2
                    g, ch = h % 4, h // 4
                    a = (j * NH + h) * HP
                    ins = MM(W[1][HP * g:HP * (g + 1), ch * P:(ch + 1) * P], v_aug[:, a:a + HP], PT[half][:, (r * 4 + c) * P:(r * 4 + c + 1) * P],
                             start=True, stop=True, skip_group_check=True)
                ins.then_inc(S["pv_done"], 1)

            def d_oT(t, j, _):
                pe.wait_ge(S["po_done"], 2 * t + j + 1)
                for ch in range(4):
                    ins = TR(W[1][:, 512 + ch * P:512 + (ch + 1) * P], po[:, ch * P:(ch + 1) * P], ident[:])
                ins.then_inc(S["oTok_done"], 1)

            def d_aT(t, j, _):
                pe.wait_ge(S["attn_done"], 2 * t + j + 1)
                for kc in range(KC):
                    ins = TR(W[1][:, kc * P:(kc + 1) * P], attn[:, kc * P:(kc + 1) * P], ident[:])
                ins.then_inc(S["oT_ps"], 1)

            def d_o(t, j, _):
                pe.wait_ge(S["oT_lo_done"], 2 * t + j + 1)
                if isinstance(t, int):
                    pe.wait_ge(S["wo_split"], 2)
                split_mm(W[1][:, 512:512 + D], [(cols(oT_hi, oT_lo, kc * P, P), cols(whi_a, wlo_a, NQ + NKV + kc * D, D))
                                                for kc in range(KC)]).then_inc(S["o_done"], 1)

            def f_T(t, _):
                pe.wait_ge(S["f_xn"], 2 * t + 2)
                transpose_pair(xn_f).then_inc(S["f_T"], 1)

            def f_up(t, c):
                if c == 0:
                    pe.wait_ge(S["f_lo"], t + 1)
                    if isinstance(t, int):
                        pe.wait_ge(S["piece_split"], 2 * EARLY)
                wait_late(pe, "hf_done", NC * t + c - 1)
                for u in range(2):
                    ins = split_mm(G[c % 2][:, u * T2:(u + 1) * T2],
                                   [(cols(wgu_hi, wgu_lo, (kc * 2 + u) * INTER + c * P, P), cols(fT_hi, fT_lo, kc * T2, T2)) for kc in range(KC)])
                ins.then_inc(S["gu_done"], 1)

            def down(hi_sem, whi, wlo, off, part, taken):
                def step(t, c):
                    if c == 0:
                        if part == "bdn_part" and isinstance(t, int):
                            pe.wait_ge(S["x2_done"], NP)
                        wait_late(pe, taken, t)
                    pe.wait_ge(S[hi_sem], NC * t + c + 1)
                    b = c % HB * T2
                    for j in range(2):
                        ins = split_mm(DN[:, j * D:(j + 1) * D], [(cols(h_hi, h_lo, b + j * P, P), cols(whi, wlo, off + c * D, D))],
                                       first=c == 0 and j == 0, last=c == NC - 1)
                    ins.then_inc(S[part], 1)
                return step

            def l_T(t, _):
                pe.wait_ge(S["l_xn"], 2 * t + 2)
                if isinstance(t, int) and t == NP - 1:
                    pe.wait_ge(S["b_lo"], 1)
                else:
                    pe.wait_ge(S["f_lo"], t + 2)
                transpose_pair(xn_l).then_inc(S["l_T"], 1)

            def l_sc(t, _):
                pe.wait_ge(S["lT_done"], t + 1)
                for j in range(2):
                    for kc in range(KC):
                        ins = MM(M[:, j * P:(j + 1) * P], lT[:, kc * T2 + j * P:kc * T2 + (j + 1) * P],
                                 csT[:, bass.ds(t * PW + j * D + kc * P, P)], start=kc == 0, stop=kc == KC - 1, skip_group_check=True)
                ins.then_inc(S["l_sc"], 1)

            def l_pT(t, _):
                pe.wait_ge(S["lp_done"], 2 * t + 2)
                for j in range(2):
                    ins = TR(M[:, j * P:(j + 1) * P], pl[:, j * P:(j + 1) * P], ident[:])
                ins.then_inc(S["plT_ps"], 1)

            def l_ro(t, _):
                pe.wait_ge(S["plT_done"], t + 1)
                pe.wait_ge(S["ctx_in"], 16)
                for j in range(2):
                    ins = MM(M[:, j * D:(j + 1) * D], plT[:, j * P:(j + 1) * P], cs[:, bass.ds(t * PW + j * D, D)], start=True, stop=True,
                             skip_group_check=True)
                ins.then_inc(S["ro_done"], 1)

            def r_T(t, _):
                pe.wait_ge(S["b_xn"], 2 * t + 2)
                if isinstance(t, int):
                    pe.wait_ge(S["x3_done"], 2 * (NP - 1 + t))
                else:
                    pe.wait_ge(S["b_lo"], t)
                transpose_pair(xn_b).then_inc(S["b_T"], 1)

            def r_rt(t, _):
                pe.wait_ge(S["b_lo"], t + 1)
                if isinstance(t, int):
                    pe.wait_ge(S["piece_split"], 2 * EARLY)
                split_mm(W[0][:, 0:T2], [(cols(wr_hi, wr_lo, kc * P, P), (bT_hi[:, bass.ds(t * PW + kc * T2, T2)], bT_lo[:, bass.ds(t * PW + kc * T2, T2)]))
                                         for kc in range(KC)]).then_inc(S["rt_ps"], 1)

            def r_lT(t, _):
                wait_apart(pe, "lg_done", t + 1)
                for j in range(2):
                    ins = TR(W[0][:, 512 + HP * j:512 + HP * (j + 1)], lgT[:, j * P:(j + 1) * P], ident[0:HP, 0:HP])
                ins.then_inc(S["lgT_ps"], 1)

            def r_pT(t, _):
                pe.wait_ge(S["pen_done"], 2 * t + 2)
                for j in range(2):
                    ins = TR(W[1][:, j * P // 2:(j + 1) * P // 2].bitcast(bf16), pen[:, j * P:(j + 1) * P], identb[:])
                ins.then_inc(S["penT_ps"], 1)

            def b_up(t, c):
                if c == 0:
                    pe.wait_ge(S["penT_done"], t + 1)
                    pe.wait_ge(S["piece_split"], 2 * len(PIECES))
                if isinstance(t, int) and t == 0 and c < 2:
                    pe.wait_ge(S["hf_done"], NC * NP)
                wait_late(pe, "bf_done", NC * t + c - 1)
                o = G[c % 2][:, 0:T2]
                split_mm(o, [(cols(w12_hi, w12_lo, kc * INTER + c * P, P),
                              (bT_hi[:, bass.ds(t * PW + kc * T2, T2)], bT_lo[:, bass.ds(t * PW + kc * T2, T2)])) for kc in range(KC)], last=False)
                MM(o, spread[:, c * P:(c + 1) * P], penT[:, pair(t, T2)], start=False, stop=True, skip_group_check=True).then_inc(S["up_done"], 1)

            run(pe, "tensor", {"A.T": a_T, "A.qkv": a_qkv, "A.qkT": a_qkT, "A.s": a_s, "A.mT": a_mT, "D.st": d_st, "D.pv": d_pv, "D.oT": d_oT,
                     "D.aT": d_aT, "D.o": d_o, "F.T": f_T, "F.up": f_up, "F.dn": down("h_lo_done", wd_hi, wd_lo, 0, "dn_part", "x2_done"),
                     "L.T": l_T, "L.sc": l_sc, "L.pT": l_pT, "L.ro": l_ro,
                     "R.T": r_T, "R.rt": r_rt, "R.lT": r_lT, "R.pT": r_pT, "B.up": b_up,
                     "B.dn": down("bh_lo", w12_hi, w12_lo, W2O, "bdn_part", "x4_done")})


def kernel(**inputs):
    import numpy as np
    import concourse.bacc as bacc
    from concourse.bass_utils import run_bass_kernel_spmd

    def arr(n):
        return np.asarray(inputs[n])

    def chunked(wT):
        k, n = wT.shape
        return wT.reshape(k // 128, 128, n).transpose(1, 0, 2).reshape(128, -1)

    x, c = arr("x"), arr("ctx_2048")
    wr, br = arr("L1_ffn_Wr").T, arr("L1_ffn_br").reshape(-1, 1)
    data = {
        "x": x, "ctx": c,
        "ctxT": c.reshape(8, 128, 2, 128).transpose(3, 0, 2, 1).reshape(128, -1),
        "mask": arr("mask_BxS2_bk0").reshape(-1).view(np.uint32),
        "rows": np.concatenate([arr(n).reshape(-1) for n in (
            "L0_xattn_q_b", "L0_xattn_k_img_b", "L0_xattn_v_img_b", "L0_xattn_o_b", "L0_xattn_norm_q_w", "L0_xattn_norm_k_img_w",
            "g_xattn", "g_ffn")]),
        "wq": chunked(arr("L0_xattn_q_w").T),
        "wkv": chunked(np.concatenate([arr("L0_xattn_k_img_w").T, arr("L0_xattn_v_img_w").T], 1)),
        "wo": chunked(arr("L0_xattn_o_w").T),
        "wgu": chunked(arr("L0_ffn_w_gate_up").T), "wd": chunked(arr("L0_ffn_w_down").T),
        "wr": chunked(np.concatenate([wr, np.zeros((wr.shape[0], 128 - wr.shape[1]), wr.dtype)], 1)),
        "br": np.concatenate([br, np.zeros((32 - br.shape[0], 1), br.dtype)]),
        "w1": chunked(arr("L1_ffn_W1").T), "w2": chunked(arr("L1_ffn_W2").T),
    }
    nc = bacc.Bacc("TRN2", target_bir_lowering=False, num_devices=1)
    arrays, args = {}, {}
    for n, a in data.items():
        a = np.ascontiguousarray(a)
        arrays["in_" + n] = a
        args[n] = nc.dram_tensor("in_" + n, a.shape, mybir.dt.from_np(a.dtype), kind="ExternalInput").ap()
    out = nc.dram_tensor("out_x", x.shape, mybir.dt.float32, kind="ExternalOutput").ap()
    a = args
    build(nc, a["x"], a["ctx"], a["ctxT"], a["mask"], a["rows"], a["wq"], a["wkv"], a["wo"], a["wgu"], a["wd"], a["wr"], a["br"],
          a["w1"], a["w2"], out)
    r = run_bass_kernel_spmd(nc, [arrays], core_ids=[0])
    return r.results[0]["out_x"]
```

```python
import concourse.bass as bass
from concourse import mybir
from contextlib import ExitStack


def build(nc, x_d, ctx_d, ctxT_d, mask_d, rows_d, wq_d, wkv_d, wo_d, wgu_d, wd_d, wr_d, br_d, w1_d, w2_d, out_d):
    f32, f32r, f16, bf16, u8 = (mybir.dt.float32, mybir.dt.float32r, mybir.dt.float16,
                                mybir.dt.bfloat16, mybir.dt.uint8)
    ALU, ACT, AX = mybir.AluOpType, mybir.ActivationFunctionType, mybir.AxisListType

    P = 128
    NT = x_d.shape[0]
    D = x_d.shape[2]
    KC = D // P
    NP = NT // 2
    PW = 2 * D
    T2 = 2 * P
    NH, HD = 16, 16
    HP = 32
    INTER = wd_d.shape[1] // D * P
    NC = INTER // P
    NB, TOPK, BLK = 16, 4, 64
    MASKED = -1e30 * D ** 0.5
    UNPICKED = -1e30
    EXP_LOW = -87.3365
    PAD = -1e30

    ctx = ExitStack()
    with ctx:
        def sb(name, shape, dt=f32):
            return ctx.enter_context(nc.sbuf_tensor(name, shape, dt))

        def sem(name):
            return ctx.enter_context(nc.semaphore(name))

        xs = sb("xs", [P, NT * D])
        cs = sb("cs", [P, NT * D])
        csT = sb("csT", [P, NT * D])
        NQ, NKV = KC * D, KC * 2 * D
        W2O = KC * INTER
        WEIGHTS = [("wa", KC * 4 * D), ("wgu", KC * 2 * INTER), ("wd", NC * D), ("wr", KC * P), ("w12", W2O + NC * D)]
        with ExitStack() as arriving:
            wa_raw, wgu_raw, wd_raw, wr_raw, w12_raw = [arriving.enter_context(nc.sbuf_tensor(f"{n}_raw", [P, c], f32)) for n, c in WEIGHTS]
        wlo_a, wgu_lo, wd_lo, wr_lo, w12_lo = [sb(f"{n}_lo", [P, c], f32r) for n, c in WEIGHTS]
        wgu_hi, wd_hi, wr_hi, w12_hi = [sb(f"{n}_hi", [P, c], f32r) for n, c in WEIGHTS[1:]]
        rows = sb("rows", [P, 6 * D + 4])
        qb, kb, vb, ob, nqw, nkw = [rows[:, i * D:(i + 1) * D] for i in range(6)]
        graw = rows[:, 6 * D:]
        gob = sb("gob", [P, D])
        wn = sb("wn", [P, D])
        wn_max, wn_inv, sc_exp = sb("wn_max", [P, 1]), sb("wn_inv", [P, 1]), sb("sc_exp", [P, 1])
        br_col = sb("br_col", [HP, 1])
        gate = sb("gate", [P, 4])
        gf0_half = sb("gf0_half", [P, 1])
        mask_words = sb("mask_words", [P, NT * P // 4], mybir.dt.uint32)
        mask_all = mask_words[:].bitcast(u8)
        valid = sb("valid", [P, NT])
        neg_half = sb("neg_half", [P, 4])
        ident = sb("ident", [P, P])
        ident16, identb = sb("ident16", [P, P], f16), sb("identb", [P, P], bf16)
        pick_row = sb("pick_row", [P, 8 * P], f16)
        spread = sb("spread", [P, NC * P], bf16)

        bn_a, var_a, vare_a, rstd_a = sb("bn_a", [P, 12]), sb("var_a", [P, 4]), sb("vare_a", [P, 2]), sb("rstd_a", [P, 2])
        ssq, msq, rms = sb("ssq", [P, 4]), sb("msq", [P, 4]), sb("rms", [P, 4])
        mx = sb("mx", [P, 2 * NH])
        nm16 = sb("nm16", [P, 2 * P], f16)
        mT = sb("mT", [P, 2 * P], f16)
        rden = sb("rden", [P, 2 * NH])
        bn_f, var_f, vare_f, rstd_f = sb("bn_f", [P, 12]), sb("var_f", [P, 4]), sb("vare_f", [P, 2]), sb("rstd_f", [P, 2])
        xn_f = sb("xn_f", [P, PW])
        fT_hi, fT_lo = sb("fT_hi", [P, PW], f32r), sb("fT_lo", [P, PW], f32r)
        HB = 4
        hf = sb("hf", [P, HB * T2])
        h_hi, h_lo = sb("h_hi", [P, HB * T2], f32r), sb("h_lo", [P, HB * T2], f32r)
        bn_l, var_l, vare_l, rstd_l = sb("bn_l", [P, 12]), sb("var_l", [P, 4]), sb("vare_l", [P, 2]), sb("rstd_l", [P, 2])
        xn_l = sb("xn_l", [P, PW])
        lT = sb("lT", [P, 2 * KC * P])
        mask2 = sb("mask2", [P, T2], u8)
        sc = sb("sc", [P, T2])
        nmx, nmx_s, den = sb("nmx", [P, 2]), sb("nmx_s", [P, 2]), sb("den", [P, 2])
        pl, plT = sb("pl", [P, T2]), sb("plT", [P, T2])
        rec, coef = sb("rec", [P, 2]), sb("coef", [P, 2])
        bn_b, var_b, vare_b, rstd_b = sb("bn_b", [P, 12]), sb("var_b", [P, 4]), sb("vare_b", [P, 2]), sb("rstd_b", [P, 2])
        t8, rep = sb("t8", [P, 16]), sb("rep", [P, 16])
        lgv, mr = sb("lgv", [P, 2 * 24]), sb("mr", [P, 2 * 24])
        pen = sb("pen", [P, T2], bf16)
        with ExitStack() as place:
            def sa(name, shape, dt=f32):
                return place.enter_context(nc.sbuf_tensor(name, shape, dt))
            xn_a = sa("xn_a", [P, PW])
            aT_hi, aT_lo = sa("aT_hi", [P, PW], f32r), sa("aT_lo", [P, PW], f32r)
            c_hi, c_lo = sa("c_hi", [P, PW], f32r), sa("c_lo", [P, PW], f32r)
            qk_pre = sa("qk_pre", [P, 2 * D])
            q_pre, k_pre = qk_pre[:, 0:D], qk_pre[:, D:]
            junk = sa("junk", [P, D], bf16)
            q16, k16 = sa("q16", [P, 4 * D], f16), sa("k16", [P, 4 * D], f16)
            whi_a = sa("whi_a", [P, KC * 4 * D], f32r)
            v_aug = sa("v_aug", [P, 2 * NH * HP])
            QT, KT = sa("QT", [P, 2 * 8 * P], f16), sa("KT", [P, 2 * 8 * P], f16)
            PTs = sa("PTs", [P, 2 * 8 * P])
            PT = [PTs[:, 0:8 * P], PTs[:, 8 * P:]]
            po = sa("po", [P, 4 * P])
            attn = sa("attn", [P, D])
            oT_hi, oT_lo = sa("oT_hi", [P, D], f32r), sa("oT_lo", [P, D], f32r)
        with ExitStack() as place:
            xn_b = sa("xn_b", [P, PW])
            bT_hi, bT_lo = sa("bT_hi", [P, NP * PW], f32r), sa("bT_lo", [P, NP * PW], f32r)
            lgT = sa("lgT", [HP, T2])
            penT = sa("penT", [P, NP * T2], bf16)
            hb = sa("hb", [P, HB * T2])
            hb_hi, hb_lo = sa("hb_hi", [P, HB * T2], f32r), sa("hb_lo", [P, HB * T2], f32r)

        def bank(name, cols=512):
            return ctx.enter_context(nc.psum_tensor(name, [P, cols], f32))
        G = [bank("G0"), bank("G1")]
        DN = bank("DN")
        W = [bank("W0", 1024), bank("W1", 1024)]
        M = bank("M")
        BG, BDN, BR = [W[0][:, 0:512], W[0][:, 512:]], W[1][:, 0:512], W[1][:, 512:]

        S = {n: sem(n) for n in """
            x0_in x_in ctxT0_in ctxT_in ctx_in qkv_in o_in rows_in mask_in stores
            consts rows_ready gates_ready ident_ready patterns_ready wqkv_hi wqkv_split wo_split pool_split vec_split
            a_stats a_var a_vare a_rstd a_xn a_T a_hi a_lo c_hi_done c_split gob_added
            qkv_done q_pre_done k_pre_done v_done ss_done msq_done rms_done qn_done kn_done q16_hi k16_hi q16_lo k16_lo
            qkT_done QT_done KT_done s_done max_done nm_hi nm_done mT_ps mT_done st_done PT_done pv_done po_done
            oTok_done rden_done attn_done oT_ps oT_hi_done oT_lo_done o_done x1_done
            f_stats f_var f_vare f_rstd f_xn f_T f_hi f_lo gu_done th_done uu_done hf_done h_hi_done h_lo_done dn_part x2_done
            l_stats l_var l_vare l_rstd l_xn l_T lT_done l_sc mask_sel sc_filled l_sel l_max l_maxs lp_done rec_done coef_done plT_ps plT_done ro_done x3_done
            b_stats b_var b_vare b_rstd b_xn b_T b_hi b_lo rt_ps lg_done lgT_ps t8_done lgv_done rep_done mr_done pen_done penT_ps penT_done
            up_done bf_done bh_hi bh_lo bdn_part x4_done wn_mul wn_abs wn_rec""".split()}

        LOAD, PIECE = 1024, 512
        LOADS = [(wgu_d, i, wgu_raw, wgu_hi, wgu_lo, i, LOAD) for i in range(0, KC * 2 * INTER, LOAD)]
        LOADS += [(wd_d, i, wd_raw, wd_hi, wd_lo, i, LOAD) for i in range(0, NC * D, LOAD)]
        LOADS += [(wr_d, 0, wr_raw, wr_hi, wr_lo, 0, KC * P)]
        EARLY_LOADS = len(LOADS)
        LOADS += [(w1_d, i, w12_raw, w12_hi, w12_lo, i, LOAD) for i in range(0, W2O, LOAD)]
        LOADS += [(w2_d, i, w12_raw, w12_hi, w12_lo, W2O + i, LOAD) for i in range(0, NC * D, LOAD)]
        loaded = [sem(f"loaded{i}") for i in range(len(LOADS))]
        PIECES = [(n, raw, hi, lo, col + i, min(PIECE, cols)) for n, (_, _, raw, hi, lo, col, cols) in enumerate(LOADS)
                  for i in range(0, cols, PIECE)]
        EARLY = sum(n < EARLY_LOADS for n, *_ in PIECES)
        EARLY_POOL, LATE_POOL, LATE_VEC = 6, 4, len(PIECES) - EARLY - 4
        OF_POOL = [*range(EARLY_POOL), *range(EARLY, EARLY + LATE_POOL)]
        OF_VEC = [*range(EARLY_POOL, EARLY), *range(EARLY + LATE_POOL, len(PIECES))]

        block = ctx.enter_context(nc.Block())

        FIRST = {
            "tensor": """
                E.dn2 C.st0 A.T0 C.st1 C.pv0 E.dn3 A.qkv0 C.oT0 E.up4 C.aT0 A.qkT0 A.s0 E.up5 E.up6 A.s1 A.mT0 C.o0 D.st0 E.dn4
                E.up7 F.T0 E.dn5 E.dn6 F.up0 F.up1 F.up2 A.qkv1 E.dn7 L.T0 D.st1 D.pv0 D.oT0 A.qkT1 L.sc0 L.pT0 D.aT0 A.s2 L.ro0
                D.o0 F.up3 A.s3 F.dn0 F.dn1 A.mT1""",
            "vector": """
                E.up4 E.up5 E.up6 A.ln0 E.up7 C.oT0 F.ln0 F.xn0 F.T0 F.up0 A.xn0 A.T0 A.qkv0 F.up1 F.up2 A.msq0 A.nrm0 A.lo0
                V.s0 C.aT0 F.up3 V.s1 A.qkT0 V.s2 V.s3 A.s0 A.s1 V.s4 V.s5 E.dn7 L.ln0 A.qkv1 A.msq1 A.nrm1 V.s6 C.o0 A.lo1
                D.oT0 A.qkT1 D.aT0 A.s2 A.s3 D.o0 L.xn0 L.sc0 L.pT0 L.ro0""",
            "scalar": """
                A.ln0 E.up4 E.hi4 E.up5 E.up6 E.hi5 C.st0 C.st1 C.pv0 C.aT0 E.up7 E.hi6 E.hi7 F.T0 A.T0 A.qkv0 A.nrm0 F.up0
                F.up1 F.up2 A.qkT0 A.mT0 D.st0 L.T0 A.qkv1 D.st1 A.nrm1 D.pv0 A.qkT1 F.hi0 F.up3 D.aT0 F.hi1 L.sc0 L.pT0 A.mT1
                F.hi2 F.hi3""",
            "gpsimd": """
                E.hi4 A.ln0 A.T0 A.msq0 F.ln0 A.lo0 W.p0 W.o0 W.s0 L.ln0 E.hi5 E.hi6 W.s1 W.s2 E.hi7 A.msq1 F.hi0 A.lo1 W.s3
                W.s4 W.s5 F.hi1 F.hi2 F.hi3""",
        }
        SECOND = {
            "tensor": """
                E.up4 E.up5 E.up6 C.st0 E.dn2 C.st1 E.dn3 A.T0 E.up7 E.dn4 E.dn5 C.pv0 C.oT0 A.qkv0 C.aT0 C.o0 F.T0 E.dn6 A.qkT0
                F.up0 A.s0 A.s1 F.up1 E.dn7 A.mT0 D.st0 A.qkv1 D.st1 F.up2 F.up3 D.pv0 A.qkT1 D.oT0 A.s2 D.aT0 L.T0 F.dn0 L.sc0
                L.pT0 L.ro0 A.s3 D.o0 F.dn1 A.mT1""",
            "vector": """
                E.up4 A.ln0 V.t0 E.up5 A.xn0 E.up6 A.T0 C.oT0 C.aT0 E.up7 A.qkv0 C.o0 E.dn7 A.msq0 F.ln0 A.nrm0 F.xn0 A.lo0 F.T0
                L.ln0 V.t1 L.xn0 A.qkT0 V.t2 A.s0 A.s1 V.t3 F.up0 F.up1 A.qkv1 A.msq1 A.nrm1 F.up2 A.lo1 L.sc0 F.up3 A.qkT1
                D.oT0 A.s2 D.aT0 A.s3 L.pT0 L.ro0 D.o0""",
            "scalar": """
                E.up4 E.hi4 C.st0 C.st1 A.ln0 E.up5 A.T0 E.up6 E.hi5 C.pv0 C.aT0 A.qkv0 A.nrm0 E.hi6 E.up7 E.hi7 F.T0 A.qkT0
                A.mT0 F.up0 F.up1 D.st0 A.qkv1 D.st1 F.up2 A.nrm1 F.up3 F.hi0 F.hi1 D.pv0 F.hi2 L.T0 A.qkT1 L.sc0 F.hi3 L.pT0
                D.aT0 A.mT1""",
            "gpsimd": """
                E.hi4 L.ln0 A.ln0 E.hi5 A.T0 A.msq0 F.ln0 A.lo0 E.hi6 E.hi7 W.s6 W.s7 A.msq1 A.lo1 W.s8 F.hi0 F.hi1 W.s9 F.hi2
                F.hi3""",
        }
        BODY = {
            "tensor": """
                E.up4 C.st0 E.up5 A.T0 C.st1 E.dn2 A.qkv0 E.up6 C.pv0 C.oT0 E.up7 C.aT0 A.qkT0 E.dn3 A.s0 E.dn4 C.o0 A.s1 E.dn5
                E.dn6 E.dn7 A.mT0 D.st0 A.qkv1 F.T0 D.st1 F.up0 F.up1 D.pv0 L.T0 A.qkT1 D.oT0 L.sc0 A.s2 F.up2 F.dn0 A.s3 D.aT0
                F.dn1 F.up3 L.pT0 D.o0 A.mT1 L.ro0""",
            "vector": """
                A.ln0 A.xn0 A.T0 E.up4 A.qkv0 A.msq0 E.up5 A.nrm0 C.oT0 A.lo0 E.up6 C.aT0 A.qkT0 E.up7 A.s0 C.o0 A.s1 F.ln0
                E.dn7 F.xn0 A.qkv1 F.T0 A.msq1 L.ln0 A.nrm1 F.up0 L.xn0 A.lo1 F.up1 A.qkT1 D.oT0 A.s2 L.sc0 A.s3 D.aT0 L.pT0
                F.up2 D.o0 F.up3 L.ro0""",
            "scalar": """
                C.st0 A.ln0 A.T0 E.up4 E.up5 E.hi4 C.st1 A.qkv0 C.pv0 E.up6 A.nrm0 E.up7 C.aT0 A.qkT0 E.hi5 E.hi6 E.hi7 A.mT0
                D.st0 F.T0 A.qkv1 D.st1 F.up0 A.nrm1 D.pv0 F.up1 L.T0 A.qkT1 F.hi0 F.hi1 D.aT0 F.up2 L.sc0 F.up3 L.pT0 A.mT1
                F.hi2 F.hi3""",
            "gpsimd": """
                A.ln0 A.T0 E.hi4 A.msq0 A.lo0 E.hi5 E.hi6 E.hi7 F.ln0 A.msq1 L.ln0 A.lo1 F.hi0 F.hi1 F.hi2 F.hi3""",
        }
        TAIL = {
            "tensor": """
                C.st0 E.up4 C.st1 E.up5 C.pv0 E.dn2 C.oT0 E.dn3 C.aT0 E.up6 C.o0 E.up7 R.T0 E.dn4 E.dn5 R.rt0 R.lT0 E.dn6 E.dn7
                R.pT0 B.up0 F.T0 B.up1 B.up2 B.up3 Q.T0 B.up4 B.up5 B.up6 B.up7 B.dn0 F.up0 L.T0 F.up1 B.dn1 L.sc0 F.dn0 Q.rt0
                B.dn2 B.dn3 Q.lT0 F.up2 F.up3 L.pT0 Q.pT0 B.dn4 B.dn5 F.dn1 L.ro0 B.dn6 B.dn7""",
            "vector": """
                R.ln0 E.up4 R.xn0 C.oT0 C.aT0 E.up5 E.up6 C.o0 F.ln0 R.T0 E.up7 R.rt0 R.lT0 R.pT0 F.xn0 Q.ln0 B.up0 B.up1 Q.xn0
                E.dn7 L.ln0 L.xn0 F.T0 B.up2 B.up3 Q.T0 F.up0 F.up1 L.sc0 B.up4 B.up5 Q.rt0 B.up6 B.up7 Q.lT0 F.up2 F.up3 L.pT0
                Q.pT0 L.ro0 B.dn7""",
            "scalar": """
                C.st0 C.st1 E.up4 C.pv0 C.aT0 E.up5 E.up6 E.hi4 E.hi5 E.up7 R.T0 E.hi6 E.hi7 B.up0 B.up1 B.up2 B.up3 F.T0 Q.T0
                B.up4 B.up5 F.up0 L.T0 F.hi0 F.up1 F.hi1 B.up6 B.up7 L.sc0 F.up2 F.up3 L.pT0 F.hi2 F.hi3""",
            "gpsimd": """
                R.ln0 E.hi4 E.hi5 E.hi6 E.hi7 F.ln0 Q.ln0 B.up0 B.up1 L.ln0 F.hi0 B.up2 B.up3 F.hi1 B.up4 B.up5 B.up6 B.up7
                F.hi2 F.hi3""",
        }
        JOIN = {
            "tensor": """
                E.up4 E.up5 E.up6 E.up7 E.dn2 E.dn3 E.dn4 E.dn5 E.dn6 E.dn7 R.T0 B.up0 B.up1 B.up2 L.T0 B.up3 L.sc0 R.rt0 B.up4
                R.lT0 B.up5 L.pT0 R.pT0 L.ro0 B.dn0 B.dn1 B.dn2 B.dn3 B.up6 B.up7 Q.T0 B.dn4 B.dn5 Q.rt0 Q.lT0 B.dn6 B.dn7 Q.pT0""",
            "vector": """
                E.up4 E.up5 R.ln0 E.up6 E.up7 R.xn0 E.dn7 L.ln0 L.xn0 R.T0 L.sc0 R.rt0 B.up0 B.up1 B.up2 R.lT0 B.up3 L.pT0 R.pT0
                L.ro0 Q.ln0 B.up4 Q.xn0 B.up5 B.up6 Q.T0 B.up7 Q.rt0 Q.lT0 Q.pT0 B.dn7""",
            "scalar": """
                E.up4 E.up5 E.hi4 E.up6 E.up7 E.hi5 E.hi6 E.hi7 B.up0 B.up1 R.T0 B.up2 L.T0 B.up3 L.sc0 B.up4 L.pT0 B.up5 B.up6
                B.up7 Q.T0""",
            "gpsimd": """
                E.hi4 R.ln0 E.hi5 E.hi6 E.hi7 L.ln0 B.up0 B.up1 B.up2 B.up3 Q.ln0 B.up4 B.up5 B.up6 B.up7""",
        }
        LAST = {
            "tensor": """
                B.up0 B.up1 B.up2 B.up3 B.up4 B.up5 B.up6 B.up7 B.dn0 B.dn1 B.dn2 B.dn3 B.dn4 B.dn5 B.dn6 B.dn7""",
            "vector": """
                B.up0 B.up1 B.up2 B.up3 B.up4 B.up5 B.up6 B.up7 B.dn7""",
            "scalar": """
                B.up0 B.up1 B.up2 B.up3 B.up4 B.up5 B.up6 B.up7""",
            "gpsimd": """
                B.up0 B.up1 B.up2 B.up3 B.up4 B.up5 B.up6 B.up7""",
        }

        def run(eng, kind, steps):
            def go(order, **pair_of):
                for word in order[kind].split():
                    name, i = word[:-1], int(word[-1])
                    if name[0] in pair_of:
                        step = {"E": "F", "Q": "R", "C": "D"}.get(name[0], name[0]) + name[1:]
                        if step in steps:
                            steps[step](pair_of[name[0]], *((int(name[0] == "C"), i) if step[0] == "D" else (i,)))

            go(FIRST, A=0, D=0, W=0, V=0)
            go(SECOND, A=1, D=1, C=0, F=0, W=0, V=0)
            with eng.Fori(2, NP) as p:
                go(BODY, A=p, D=p, C=p - 1, F=p - 1, E=p - 2, L=p - 2)
            go(TAIL, C=NP - 1, F=NP - 1, E=NP - 2, L=NP - 2, R=0, Q=1, B=0)
            go(JOIN, E=NP - 1, L=NP - 1, R=2, Q=3, B=1)
            with eng.Fori(2, NP) as r:
                go(LAST, B=r)

        def wait_late(eng, name, count):
            if not isinstance(count, int) or count > 0:
                eng.wait_ge(S[name], count)

        def wait_apart(eng, name, value):
            v = value if isinstance(value, int) else eng.snap(value)
            eng.wait_ge(S["consts"], 1)
            eng.wait_ge(S[name], v)

        def parts(which, s):
            v = (q16, k16)[which][:].rearrange("p (h a b c) -> p h a b c", a=2, b=2, c=HD)
            return v[:, :, :, s, :] if which else v[:, :, s, :, :]

        def twice(src):
            return src.rearrange("p (h c) -> p h c", c=HD).unsqueeze(2).to_broadcast([P, NH, 2, HD])

        def pair(t, w=PW):
            return bass.ds(t * w, w)

        @block.sync
        def _(sp):
            x_rows = xs[:].rearrange("p (t d) -> p t d", t=NT)
            sp.dma_start(x_rows[:, 0:2], x_d[0:2].rearrange("t p d -> p t d")).then_inc(S["x0_in"], 16)
            sp.dma_start(wa_raw[:, 0:NQ], wq_d).then_inc(S["qkv_in"], 16)
            sp.dma_start(wa_raw[:, NQ:NQ + NKV], wkv_d).then_inc(S["qkv_in"], 16)
            sp.dma_start(wa_raw[:, NQ + NKV:], wo_d).then_inc(S["o_in"], 16)
            sp.dma_start(x_rows[:, 2:], x_d[2:].rearrange("t p d -> p t d")).then_inc(S["x_in"], 16)
            sp.dma_start(csT[:, PW:], ctxT_d[:, PW:]).then_inc(S["ctxT_in"], 16)
            for n, (src, at, raw, _, _, col, cols) in enumerate(LOADS):
                sp.dma_start(raw[:, col:col + cols], src[:, at:at + cols]).then_inc(loaded[n], 16)
            sp.dma_start(cs[:].rearrange("p (t d) -> p t d", t=NT), ctx_d.rearrange("t p d -> p t d")).then_inc(S["ctx_in"], 16)
            with sp.Fori(0, NP) as r:
                sp.wait_ge(S["x4_done"], r + 1)
                sp.dma_start(out_d[bass.ds(r * 2, 2), :, :].rearrange("t p d -> p t d"),
                             xs[:, pair(r)].rearrange("p (t d) -> p t d", t=2)).then_inc(S["stores"], 16)
            sp.wait_ge(S["stores"], 16 * NP)

        @block.gpsimd
        def _(pool):
            def patterns():
                nc.gpsimd.memset(v_aug[:], 0.0).then_inc(S["consts"], 1)
                nc.gpsimd.memset(nm16[:], 0.0).then_inc(S["consts"], 1)
                nc.gpsimd.memset(pen[:], 0.0).then_inc(S["consts"], 1)
                nc.gpsimd.memset(rep[:], PAD).then_inc(S["consts"], 1)
                nc.gpsimd.memset(lgv[:], PAD).then_inc(S["consts"], 1)
                for m in (ident16, identb, pick_row, spread):
                    nc.gpsimd.memset(m[:], 0.0).then_inc(S["consts"], 1)
                pool.wait_ge(S["consts"], 11)
                nc.gpsimd.memset(v_aug[:].rearrange("p (h c) -> p h c", c=HP)[:, :, HD:HD + 1], 1.0).then_inc(S["patterns_ready"], 1)
                for m in (ident16, identb):
                    nc.gpsimd.affine_select(out=m[:], in_=m[:], compare_op=ALU.not_equal, fill=1.0, base=0,
                                            pattern=[[-1, P]], channel_multiplier=1).then_inc(S["patterns_ready"], 1)

            def pick_patterns():
                done = 3
                for base in (0, 8, 64, 72):
                    pool.wait_ge(S["patterns_ready"], done)
                    v = pick_row[:].rearrange("p (i k) -> p i k", k=P)
                    nc.gpsimd.affine_select(out=v, in_=v, compare_op=ALU.not_equal, fill=1.0, base=-base,
                                            pattern=[[-1, 8], [0, P]], channel_multiplier=1).then_inc(S["patterns_ready"], 1)
                    done += 1
                v = spread[:].rearrange("p (c b m) -> p (c b) m", b=2, m=BLK)
                nc.gpsimd.affine_select(out=v, in_=v, compare_op=ALU.not_equal, fill=1.0, base=0,
                                        pattern=[[-1, NB], [0, BLK]], channel_multiplier=1).then_inc(S["patterns_ready"], 1)

            def split(raw, hi, lo, done, before):
                nc.gpsimd.tensor_scalar(hi, raw, 1.0, 0.0, ALU.mult, ALU.add).then_inc(S[done], 1)
                pool.wait_ge(S[done], before + 1)
                nc.gpsimd.tensor_tensor(lo, raw, hi.bitcast(f32), ALU.subtract).then_inc(S[done], 1)

            def w_patterns(_, i):
                pick_patterns()

            def w_out(_, i):
                pool.wait_ge(S["o_in"], 16)
                split(wa_raw[:, NQ + NKV:], whi_a[:, NQ + NKV:], wlo_a[:, NQ + NKV:], "wo_split", 0)

            def w_split(_, i):
                load, raw, hi, lo, col, cols = PIECES[OF_POOL[i]]
                at = slice(col, col + cols)
                pool.wait_ge(loaded[load], 16)
                split(raw[:, at], hi[:, at], lo[:, at], "pool_split", 2 * i)

            def ln(kind, vare, out):
                def step(t, _):
                    pool.wait_ge(S[f"{kind}_vare"], t + 1)
                    nc.gpsimd.tensor_tensor(out[:], vare[:], neg_half[:, 0:2], ALU.pow).then_inc(S[f"{kind}_rstd"], 1)
                    if kind == "a":
                        pool.wait_ge(S["c_hi_done"], t + 1)
                        nc.gpsimd.tensor_tensor(c_lo[:], csT[:, pair(t)], c_hi[:].bitcast(f32), ALU.subtract).then_inc(S["c_split"], 1)
                        if isinstance(t, int) and t == 0:
                            patterns()
                return step

            def a_T(t, _):
                if isinstance(t, int) and t == 0:
                    pool.wait_ge(S["rows_ready"], 5)
                pool.wait_ge(S["a_xn"], 2 * t + 2)
                nc.gpsimd.tensor_tensor(xs[:, pair(t)].rearrange("p (j d) -> p j d", d=D), xs[:, pair(t)].rearrange("p (j d) -> p j d", d=D),
                                        gob[:].unsqueeze(1).to_broadcast([P, 2, D]), ALU.add).then_inc(S["gob_added"], 1)

            def a_msq(t, j):
                pool.wait_ge(S["msq_done"], 2 * t + j + 1)
                nc.gpsimd.tensor_tensor(rms[:, 2 * j:2 * j + 2], msq[:, 2 * j:2 * j + 2], neg_half[:, 0:2], ALU.pow).then_inc(S["rms_done"], 1)

            def a_lo(t, j):
                pool.wait_ge(S["k16_hi"], 2 * t + j + 1)
                nc.gpsimd.tensor_tensor(parts(1, 1), twice(k_pre), parts(1, 0), ALU.subtract).then_inc(S["k16_lo"], 1)

            def low_of_hidden(h, hi, lo, hi_done, lo_done):
                def step(t, c):
                    pool.wait_ge(S[hi_done], NC * t + c + 1)
                    b = c % HB * T2
                    nc.gpsimd.tensor_tensor(lo[:, b:b + T2], h[:, b:b + T2], hi[:, b:b + T2].bitcast(f32),
                                            ALU.subtract).then_inc(S[lo_done], 1)
                return step

            def l_ln(t, _):
                pool.wait_ge(S["mask_in"], 16)
                wait_late(pool, "lp_done", 2 * t)
                nc.gpsimd.tensor_copy(mask2[:], mask_all[:, pair(t, T2)]).then_inc(S["mask_sel"], 1)
                nc.gpsimd.memset(sc[:], MASKED).then_inc(S["sc_filled"], 1)
                ln("l", vare_l, rstd_l)(t, 0)

            nc.gpsimd.memset(neg_half[:], -0.5).then_inc(S["consts"], 1)
            nc.gpsimd.memset(ident[:], 0.0).then_inc(S["consts"], 1)
            pool.wait_ge(S["consts"], 2)
            nc.gpsimd.affine_select(out=ident[:], in_=ident[:], compare_op=ALU.not_equal, fill=1.0, base=0,
                                    pattern=[[-1, P]], channel_multiplier=1).then_inc(S["ident_ready"], 1)
            run(pool, "gpsimd", {"A.ln": ln("a", vare_a, rstd_a), "A.T": a_T, "A.msq": a_msq, "A.lo": a_lo, "F.ln": ln("f", vare_f, rstd_f),
                       "F.hi": low_of_hidden(hf, h_hi, h_lo, "h_hi_done", "h_lo_done"), "L.ln": l_ln,
                       "W.p": w_patterns, "W.o": w_out, "W.s": w_split, "R.ln": ln("b", vare_b, rstd_b), "B.up": low_of_hidden(hb, hb_hi, hb_lo, "bh_hi", "bh_lo")})

        @block.scalar
        def _(act):
            act.dma_start(csT[:, 0:PW], ctxT_d[:, 0:PW]).then_inc(S["ctxT0_in"], 16)
            act.dma_start(rows[:], rows_d.partition_broadcast(P)).then_inc(S["rows_in"], 16)
            act.dma_start(br_col[:], br_d).then_inc(S["rows_in"], 16)
            act.dma_start(mask_words[:], mask_d.partition_broadcast(P)).then_inc(S["mask_in"], 16)
            def copy(out, in_, s):
                nc.scalar.activation(out, in_, ACT.Copy).then_inc(S[s], 1)

            def a_ln(t, _):
                if isinstance(t, int):
                    act.wait_ge(S["ctxT_in" if t else "ctxT0_in"], 16)
                wait_late(act, "qkv_done", 2 * t)
                copy(c_hi[:], csT[:, pair(t)], "c_hi_done")
                if isinstance(t, int) and t == 0:
                    act.wait_ge(S["qkv_in"], 32)
                    copy(whi_a[:, 0:NQ + NKV], wa_raw[:, 0:NQ + NKV], "wqkv_hi")
                    act.wait_ge(S["rows_in"], 32)
                    nc.scalar.activation(gate[:], graw, ACT.Tanh).then_inc(S["gates_ready"], 1)

            def a_T(t, _):
                act.wait_ge(S["a_T"], t + 1)
                copy(aT_hi[:], W[0][:, 0:PW], "a_hi")

            def a_qkv(t, j):
                n = 2 * t + j + 1
                for i, (s, src) in enumerate((("q_pre_done", q_pre), ("k_pre_done", k_pre))):
                    act.wait_ge(S[s], n)
                    wait_late(act, "ss_done", 2 * (n - 1) + i)
                    nc.scalar.activation(junk[:], src, ACT.Square, scale=D ** -0.5,
                                         accum_out=ssq[:, 2 * j + i:2 * j + i + 1]).then_inc(S["ss_done"], 1)

            def a_nrm(t, j):
                n = 2 * t + j + 1
                act.wait_ge(S["kn_done"], n)
                copy(parts(1, 0), twice(k_pre), "k16_hi")
                act.wait_ge(S["qn_done"], n)
                copy(parts(0, 0), twice(q_pre), "q16_hi")

            def a_qkT(t, j):
                act.wait_ge(S["qkT_done"], 2 * t + j + 1)
                copy(QT[:, j * 1024:(j + 1) * 1024], W[0][:, 0:512].bitcast(f16), "QT_done")

            def a_mT(t, j):
                act.wait_ge(S["mT_ps"], 2 * t + j + 1)
                copy(mT[:, j * P:(j + 1) * P], W[0][:, 0:P // 2].bitcast(f16), "mT_done")

            def d_st(t, j, half):
                act.wait_ge(S["st_done"], 2 * (2 * t + j) + half + 1)
                wait_late(act, "pv_done", 2 * t + j)
                nc.scalar.activation(PT[half], W[1][:], ACT.Exp, scale=sc_exp[:]).then_inc(S["PT_done"], 1)

            def d_pv(t, j, _):
                act.wait_ge(S["pv_done"], 2 * t + j + 1)
                copy(po[:], W[1][:, 0:512], "po_done")

            def d_aT(t, j, _):
                act.wait_ge(S["oT_ps"], 2 * t + j + 1)
                copy(oT_hi[:], W[1][:, 0:D], "oT_hi_done")

            def f_T(t, _):
                act.wait_ge(S["f_T"], t + 1)
                copy(fT_hi[:], M[:], "f_hi")

            def f_up(t, c):
                k, b = NC * t + c + 1, c % HB * T2
                act.wait_ge(S["gu_done"], k)
                wait_late(act, "h_lo_done", k - HB)
                nc.scalar.activation(hf[:, b:b + T2], G[c % 2][:, 0:T2], ACT.Tanh, scale=0.5).then_inc(S["th_done"], 1)

            def f_hi(t, c):
                k, b = NC * t + c + 1, c % HB * T2
                act.wait_ge(S["hf_done"], k)
                wait_late(act, "dn_part", k - HB)
                copy(h_hi[:, b:b + T2], hf[:, b:b + T2], "h_hi_done")

            def l_T(t, _):
                act.wait_ge(S["l_T"], t + 1)
                copy(lT[:], M[:], "lT_done")

            def l_sc(t, _):
                act.wait_ge(S["l_maxs"], t + 1)
                for j in range(2):
                    nc.scalar.activation(pl[:, j * P:(j + 1) * P], sc[:, j * P:(j + 1) * P], ACT.Exp, scale=D ** -0.5,
                                         bias=nmx_s[:, j:j + 1], accum_out=den[:, j:j + 1]).then_inc(S["lp_done"], 1)

            def l_pT(t, _):
                act.wait_ge(S["plT_ps"], t + 1)
                copy(plT[:], M[:, 0:T2], "plT_done")

            def r_T(t, _):
                act.wait_ge(S["b_T"], t + 1)
                copy(bT_hi[:, pair(t)], BR, "b_hi")

            def b_up(t, c):
                k, b = NC * t + c + 1, c % HB * T2
                act.wait_ge(S["up_done"], k)
                wait_late(act, "bh_lo", k - HB)
                nc.scalar.activation(hb[:, b:b + T2], BG[c % 2][:, 0:T2], ACT.Gelu).then_inc(S["bf_done"], 1)

            run(act, "scalar", {"A.ln": a_ln, "A.T": a_T, "A.qkv": a_qkv, "A.nrm": a_nrm, "A.qkT": a_qkT, "A.mT": a_mT, "D.st": d_st, "D.pv": d_pv,
                      "D.aT": d_aT, "F.T": f_T, "F.up": f_up, "F.hi": f_hi, "L.T": l_T, "L.sc": l_sc, "L.pT": l_pT, "R.T": r_T, "B.up": b_up})

        @block.vector
        def _(dve):
            V = nc.vector
            def constants():
                dve.wait_ge(S["rows_in"], 32)
                V.tensor_tensor(wn[:], nqw, nkw, ALU.mult).then_inc(S["wn_mul"], 1)
                dve.wait_ge(S["wn_mul"], 1)
                V.tensor_reduce(wn_max[:], wn[:], AX.X, ALU.max, apply_absolute_value=True).then_inc(S["wn_abs"], 1)
                dve.wait_ge(S["wn_abs"], 1)
                V.tensor_scalar(wn_max[:], wn_max[:], 1e-30, None, ALU.max).then_inc(S["wn_abs"], 1)
                dve.wait_ge(S["wn_abs"], 2)
                V.reciprocal(wn_inv[:], wn_max[:]).then_inc(S["wn_rec"], 1)
                V.tensor_scalar(sc_exp[:], wn_max[:], HD ** -0.5, None, ALU.mult).then_inc(S["rows_ready"], 1)
                dve.wait_ge(S["wn_rec"], 1)
                V.tensor_scalar(wn[:], wn[:], wn_inv[:], None, ALU.mult).then_inc(S["rows_ready"], 1)
                dve.wait_ge(S["gates_ready"], 1)
                V.tensor_scalar(gf0_half[:], gate[:, 2:3], 0.5, None, ALU.mult).then_inc(S["rows_ready"], 1)
                V.tensor_scalar(gob[:], ob, gate[:, 0:1], None, ALU.mult).then_inc(S["rows_ready"], 1)
                dve.wait_ge(S["mask_in"], 16)
                V.tensor_reduce(valid[:], mask_all.rearrange("p (t k) -> p t k", k=P), AX.X, ALU.max).then_inc(S["rows_ready"], 1)
                dve.wait_ge(S["rows_ready"], 5)

            def ln(t, kind, src, bn, var, vare):
                for j in range(2):
                    V.bn_stats(bn[:, 6 * j:6 * j + 6], src(j)).then_inc(S[f"{kind}_stats"], 1)
                dve.wait_ge(S[f"{kind}_stats"], 2 * t + 2)
                V.memset(vare[:], 1e-5).then_inc(S[f"{kind}_var"], 1)
                for j in range(2):
                    V.bn_aggr(var[:, 2 * j:2 * j + 2], bn[:, 6 * j:6 * j + 6]).then_inc(S[f"{kind}_var"], 1)
                dve.wait_ge(S[f"{kind}_var"], 3 * t + 3)
                V.tensor_tensor(vare[:], var[:].rearrange("p (j s) -> p j s", s=2)[:, :, 1], vare[:], ALU.add).then_inc(S[f"{kind}_vare"], 1)

            def v_split(_, i):
                load, raw, hi, lo, col, cols = PIECES[OF_VEC[i]]
                at = slice(col, col + cols)
                dve.wait_ge(loaded[load], 16)
                V.tensor_copy(hi[:, at], raw[:, at]).then_inc(S["vec_split"], 1)
                dve.wait_ge(S["vec_split"], 2 * i + 1)
                V.tensor_tensor(lo[:, at], raw[:, at], hi[:, at].bitcast(f32), ALU.subtract).then_inc(S["vec_split"], 1)

            def norm(t, kind, src, var, rs, xn):
                dve.wait_ge(S[f"{kind}_rstd"], t + 1)
                for j in range(2):
                    V.tensor_scalar(xn[:, j * D:(j + 1) * D], src(j), var[:, 2 * j:2 * j + 1], rs[:, j:j + 1],
                                    ALU.subtract, ALU.mult).then_inc(S[f"{kind}_xn"], 1)

            def tile_rows(t):
                return lambda j: xs[:, bass.ds(t * PW + j * D, D)]

            def xn(kind, var, rs, out):
                return lambda t, _: norm(t, kind, tile_rows(t), var, rs, out)

            def low(out, ps, hi, s):
                V.tensor_tensor(out, ps, hi.bitcast(f32), ALU.subtract).then_inc(S[s], 1)

            def a_ln(t, _):
                if isinstance(t, int):
                    dve.wait_ge(S["x_in" if t else "x0_in"], 16)
                ln(t, "a", tile_rows(t), bn_a, var_a, vare_a)

            def a_T(t, _):
                if isinstance(t, int) and t == 0:
                    dve.wait_ge(S["wqkv_hi"], 1)
                    w = slice(0, NQ + NKV)
                    V.tensor_tensor(wlo_a[:, w], wa_raw[:, w], whi_a[:, w].bitcast(f32), ALU.subtract).then_inc(S["wqkv_split"], 1)
                dve.wait_ge(S["a_hi"], t + 1)
                low(aT_lo[:], W[0][:, 0:PW], aT_hi[:], "a_lo")
                if isinstance(t, int) and t == 0:
                    constants()

            def a_qkv(t, j):
                n = 2 * t + j + 1
                dve.wait_ge(S["qkv_done"], n)
                wait_late(dve, "k16_lo", n - 1)
                V.tensor_tensor(q_pre, W[0][:, 512:512 + D], qb, ALU.add).then_inc(S["q_pre_done"], 1)
                V.tensor_tensor(k_pre, W[0][:, 0:D], kb, ALU.add).then_inc(S["k_pre_done"], 1)
                v = v_aug[:, j * NH * HP:(j + 1) * NH * HP].rearrange("p (h c) -> p h c", c=HP)
                if isinstance(t, int) and t == 0:
                    dve.wait_ge(S["patterns_ready"], 3)
                V.tensor_tensor(v[:, :, 0:HD], W[0][:, D:2 * D].rearrange("p (h c) -> p h c", c=HD),
                                vb.rearrange("p (h c) -> p h c", c=HD), ALU.add).then_inc(S["v_done"], 1)

            def a_msq(t, j):
                dve.wait_ge(S["ss_done"], 4 * t + 2 * j + 2)
                V.tensor_scalar(msq[:, 2 * j:2 * j + 2], ssq[:, 2 * j:2 * j + 2], 1e-6, None, ALU.add).then_inc(S["msq_done"], 1)

            def a_nrm(t, j):
                n = 2 * t + j + 1
                dve.wait_ge(S["rms_done"], n)
                V.tensor_scalar(k_pre, k_pre, rms[:, 2 * j + 1:2 * j + 2], None, ALU.mult).then_inc(S["kn_done"], 1)
                V.scalar_tensor_tensor(q_pre, q_pre, rms[:, 2 * j:2 * j + 1], wn[:], ALU.mult, ALU.mult).then_inc(S["qn_done"], 1)

            def a_lo(t, j):
                dve.wait_ge(S["q16_hi"], 2 * t + j + 1)
                V.tensor_tensor(parts(0, 1), twice(q_pre), parts(0, 0), ALU.subtract).then_inc(S["q16_lo"], 1)

            def a_qkT(t, j):
                dve.wait_ge(S["qkT_done"], 2 * t + j + 1)
                V.tensor_copy(KT[:, j * 1024:(j + 1) * 1024], W[0][:, 512:1024].bitcast(f16)).then_inc(S["KT_done"], 1)

            def a_s(t, i):
                j, half = i // 2, i % 2
                dve.wait_ge(S["s_done"], 4 * t + i + 1)
                o = mx[:, j * NH:(j + 1) * NH].rearrange("p (r i) -> p r i", r=2)[:, :, 4 * half:4 * half + 4]
                V.tensor_reduce(o, W[0][:].rearrange("p (r i k) -> p r i k", r=2, k=P), AX.X, ALU.max).then_inc(S["max_done"], 1)
                if half == 1:
                    n = 2 * t + j + 1
                    dve.wait_ge(S["max_done"], 2 * n)
                    m = mx[:, j * NH:(j + 1) * NH].rearrange("p (r i) -> p r i", r=2)
                    o = nm16[:, j * P:(j + 1) * P].rearrange("p (r s) -> p r s", r=2)
                    V.tensor_scalar(o[:, :, 0:8], m, -1.0, None, ALU.mult).then_inc(S["nm_hi"], 1)
                    dve.wait_ge(S["nm_hi"], n)
                    V.scalar_tensor_tensor(o[:, :, 8:16], m, -1.0, o[:, :, 0:8], ALU.mult, ALU.subtract).then_inc(S["nm_done"], 1)

            def d_oT(t, j, _):
                n = 2 * t + j + 1
                dve.wait_ge(S["oTok_done"], n)
                o = W[1][:, 512:].rearrange("p (h c) -> p h c", c=HP)
                V.reciprocal(rden[:, j * NH:(j + 1) * NH], o[:, :, HD]).then_inc(S["rden_done"], 1)
                dve.wait_ge(S["rden_done"], n)
                V.tensor_tensor(attn[:].rearrange("p (h c) -> p h c", c=HD), o[:, :, 0:HD],
                                rden[:, j * NH:(j + 1) * NH].unsqueeze(2).to_broadcast([P, NH, HD]),
                                ALU.mult).then_inc(S["attn_done"], 1)

            def d_aT(t, j, _):
                dve.wait_ge(S["oT_hi_done"], 2 * t + j + 1)
                low(oT_lo[:], W[1][:, 0:D], oT_hi[:], "oT_lo_done")

            def d_o(t, j, _):
                dve.wait_ge(S["o_done"], 2 * t + j + 1)
                dve.wait_ge(S["gob_added"], t + 1)
                x = xs[:, bass.ds(t * PW + j * D, D)]
                V.scalar_tensor_tensor(x, W[1][:, 512:512 + D], gate[:, 0:1], x, ALU.mult, ALU.add).then_inc(S["x1_done"], 1)

            def f_ln(t, _):
                wait_apart(dve, "x1_done", 2 * t + 2)
                ln(t, "f", tile_rows(t), bn_f, var_f, vare_f)

            def f_T(t, _):
                dve.wait_ge(S["f_hi"], t + 1)
                low(fT_lo[:], M[:], fT_hi[:], "f_lo")

            def f_up(t, c):
                k, b = NC * t + c + 1, c % HB * T2
                dve.wait_ge(S["th_done"], k)
                V.scalar_tensor_tensor(hf[:, b:b + T2], hf[:, b:b + T2], 1.0, G[c % 2][:, 0:T2], ALU.add, ALU.mult).then_inc(S["uu_done"], 1)
                dve.wait_ge(S["uu_done"], k)
                V.tensor_tensor(hf[:, b:b + T2], G[c % 2][:, T2:2 * T2], hf[:, b:b + T2], ALU.mult).then_inc(S["hf_done"], 1)

            def f_dn(t, c):
                if c == NC - 1:
                    dve.wait_ge(S["dn_part"], NC * t + NC)
                    V.scalar_tensor_tensor(xs[:, pair(t)], DN[:], gf0_half[:], xs[:, pair(t)], ALU.mult, ALU.add).then_inc(S["x2_done"], 1)

            def l_ln(t, _):
                wait_apart(dve, "x2_done", t + 1)
                ln(t, "l", tile_rows(t), bn_l, var_l, vare_l)

            def l_sc(t, _):
                wait_apart(dve, "l_sc", t + 1)
                dve.wait_ge(S["mask_sel"], t + 1)
                dve.wait_ge(S["sc_filled"], t + 1)
                V.copy_predicated(sc[:], mask2[:], M[:, 0:T2]).then_inc(S["l_sel"], 1)
                dve.wait_ge(S["l_sel"], t + 1)
                V.reduce_max(nmx[:], sc[:].rearrange("p (j k) -> p j k", k=P), AX.X).then_inc(S["l_max"], 1)
                dve.wait_ge(S["l_max"], t + 1)
                V.tensor_scalar(nmx_s[:], nmx[:], -(D ** -0.5), None, ALU.mult).then_inc(S["l_maxs"], 1)

            def l_pT(t, _):
                dve.wait_ge(S["lp_done"], 2 * t + 2)
                V.reciprocal(rec[:], den[:]).then_inc(S["rec_done"], 1)
                dve.wait_ge(S["rec_done"], t + 1)
                V.scalar_tensor_tensor(coef[:], rec[:], gate[:, 1:2], valid[:, bass.ds(t * 2, 2)], ALU.mult, ALU.mult).then_inc(S["coef_done"], 1)

            def l_ro(t, _):
                dve.wait_ge(S["ro_done"], t + 1)
                dve.wait_ge(S["coef_done"], t + 1)
                for j in range(2):
                    V.scalar_tensor_tensor(xs[:, bass.ds(t * PW + j * D, D)], M[:, j * D:(j + 1) * D], coef[:, j:j + 1],
                                           xs[:, bass.ds(t * PW + j * D, D)], ALU.mult, ALU.add).then_inc(S["x3_done"], 1)

            def r_ln(t, _):
                wait_apart(dve, "x3_done", 2 * t + 2)
                ln(t, "b", tile_rows(t), bn_b, var_b, vare_b)

            def r_T(t, _):
                dve.wait_ge(S["b_hi"], t + 1)
                low(bT_lo[:, pair(t)], BR, bT_hi[:, pair(t)], "b_lo")

            def r_rt(t, _):
                dve.wait_ge(S["rt_ps"], t + 1)
                V.tensor_scalar(lgT[:], BR[0:HP, 0:T2], br_col[:], None, ALU.add).then_inc(S["lg_done"], 1)

            def r_lT(t, _):
                wait_apart(dve, "lgT_ps", t + 1)
                for j in range(2):
                    V.max(t8[:, 8 * j:8 * j + 8], BR[:, T2 + HP * j:T2 + HP * j + NB]).then_inc(S["t8_done"], 1)
                for j in range(2):
                    dve.wait_ge(S["t8_done"], 2 * t + j + 1)
                    V.tensor_scalar(lgv[:, 24 * j:24 * j + NB], BR[:, T2 + HP * j:T2 + HP * j + NB], t8[:, 8 * j:8 * j + 1], EXP_LOW,
                                    ALU.subtract, ALU.max).then_inc(S["lgv_done"], 1)
                    V.tensor_scalar(rep[:, 8 * j:8 * j + TOPK], t8[:, 8 * j:8 * j + TOPK], t8[:, 8 * j:8 * j + 1], EXP_LOW,
                                    ALU.subtract, ALU.max).then_inc(S["rep_done"], 1)
                for j in range(2):
                    wait_apart(dve, "lgv_done", 2 * t + j + 1)
                    dve.wait_ge(S["rep_done"], 2 * t + j + 1)
                    V.match_replace(mr[:, 24 * j:24 * j + 24], rep[:, 8 * j:8 * j + 8], lgv[:, 24 * j:24 * j + 24], 1.0).then_inc(S["mr_done"], 1)
                for j in range(2):
                    dve.wait_ge(S["mr_done"], 2 * t + j + 1)
                    V.tensor_scalar(pen[:, j * P:j * P + NB], mr[:, 24 * j:24 * j + NB], 0.5, UNPICKED, ALU.is_lt, ALU.mult).then_inc(S["pen_done"], 1)

            def r_pT(t, _):
                dve.wait_ge(S["penT_ps"], t + 1)
                V.tensor_copy(penT[:, pair(t, T2)], BR[:, 0:P].bitcast(bf16)).then_inc(S["penT_done"], 1)

            def b_up(t, c):
                k, b = NC * t + c + 1, c % HB * T2
                dve.wait_ge(S["bf_done"], k)
                wait_late(dve, "bdn_part", k - HB)
                V.tensor_copy(hb_hi[:, b:b + T2], hb[:, b:b + T2]).then_inc(S["bh_hi"], 1)

            def b_dn(t, c):
                if c == NC - 1:
                    dve.wait_ge(S["bdn_part"], NC * t + NC)
                    V.scalar_tensor_tensor(xs[:, pair(t)], BDN, gate[:, 3:4], xs[:, pair(t)], ALU.mult, ALU.add).then_inc(S["x4_done"], 1)

            run(dve, "vector", {"V.s": v_split, "V.t": lambda _, i: v_split(_, EARLY - EARLY_POOL + i),
                      "A.ln": a_ln, "A.T": a_T, "A.qkv": a_qkv, "A.msq": a_msq, "A.nrm": a_nrm, "A.lo": a_lo, "A.qkT": a_qkT, "A.s": a_s,
                      "A.xn": xn("a", var_a, rstd_a, xn_a), "F.xn": xn("f", var_f, rstd_f, xn_f), "L.xn": xn("l", var_l, rstd_l, xn_l),
                      "R.xn": xn("b", var_b, rstd_b, xn_b), "D.oT": d_oT,
                      "D.aT": d_aT, "D.o": d_o, "F.ln": f_ln, "F.T": f_T, "F.up": f_up, "F.dn": f_dn, "L.ln": l_ln, "L.sc": l_sc, "L.pT": l_pT, "L.ro": l_ro,
                      "R.ln": r_ln, "R.T": r_T, "R.rt": r_rt, "R.lT": r_lT, "R.pT": r_pT, "B.up": b_up, "B.dn": b_dn})

        @block.tensor
        def _(pe):
            MM, TR = nc.tensor.matmul, nc.tensor.transpose

            def split_mm(out, terms, first=True, last=True):
                n = 3 * len(terms)
                i = 0
                for (lh, ll), (rh, rl) in terms:
                    for a, b in ((lh, rh), (lh, rl), (ll, rh)):
                        ins = MM(out, a, b, start=first and i == 0, stop=last and i == n - 1, skip_group_check=True)
                        i += 1
                return ins

            def transpose_pair(src, to=M):
                for j in range(2):
                    for kc in range(KC):
                        ins = TR(to[:, kc * T2 + j * P:kc * T2 + (j + 1) * P], src[:, j * D + kc * P:j * D + (kc + 1) * P], ident[:])
                return ins

            def cols(hi, lo, a, n):
                return hi[:, a:a + n], lo[:, a:a + n]

            def a_T(t, _):
                if isinstance(t, int):
                    pe.wait_ge(S["ident_ready"], 1)
                wait_late(pe, "mT_done", 2 * t)
                pe.wait_ge(S["a_xn"], 2 * t + 2)
                transpose_pair(xn_a, W[0]).then_inc(S["a_T"], 1)

            def a_qkv(t, j):
                if j == 0:
                    pe.wait_ge(S["a_lo"], t + 1)
                    pe.wait_ge(S["c_split"], t + 1)
                    if isinstance(t, int):
                        pe.wait_ge(S["wqkv_split"], 1)
                else:
                    pe.wait_ge(S["mT_done"], 2 * t + 1)
                split_mm(W[0][:, 0:512], [(cols(c_hi, c_lo, j * D + kc * P, P), cols(whi_a, wlo_a, NQ + kc * 2 * D, 2 * D))
                                          for kc in range(KC)])
                split_mm(W[0][:, 512:512 + D], [(cols(aT_hi, aT_lo, kc * T2 + j * P, P), cols(whi_a, wlo_a, kc * D, D))
                                                for kc in range(KC)]).then_inc(S["qkv_done"], 1)

            def a_qkT(t, j):
                n = 2 * t + j + 1
                if isinstance(t, int) and t == 0:
                    pe.wait_ge(S["patterns_ready"], 3)
                pe.wait_ge(S["q16_lo"], n)
                pe.wait_ge(S["k16_lo"], n)
                pe.wait_ge(S["v_done"], n)
                o = W[0][:].bitcast(f16)
                for g in range(8):
                    TR(o[:, g * P:(g + 1) * P], q16[:, g * P:(g + 1) * P], ident16[:])
                    ins = TR(o[:, 1024 + g * P:1024 + (g + 1) * P], k16[:, g * P:(g + 1) * P], ident16[:])
                ins.then_inc(S["qkT_done"], 1)

            def head(j, half, c, r):
                a = j * 1024 + (4 * half + c) * P
                return slice(64 * r, 64 * r + 64), slice(a, a + P)

            def a_s(t, i):
                j, half = i // 2, i % 2
                if half == 0:
                    pe.wait_ge(S["KT_done"], 2 * t + j + 1)
                    pe.wait_ge(S["QT_done"], 2 * t + j + 1)
                else:
                    pe.wait_ge(S["max_done"], 4 * t + i)
                for c in range(4):
                    for r in range(2):
                        rows, cc = head(j, half, c, r)
                        ins = MM(W[0][:, r * 512 + c * P:r * 512 + (c + 1) * P], QT[rows, cc], KT[rows, cc],
                                 start=True, stop=True, skip_group_check=True)
                ins.then_inc(S["s_done"], 1)

            def a_mT(t, j):
                pe.wait_ge(S["nm_done"], 2 * t + j + 1)
                TR(W[0][:, 0:P // 2].bitcast(f16), nm16[:, j * P:(j + 1) * P], ident16[:]).then_inc(S["mT_ps"], 1)

            def d_st(t, j, half):
                n = 2 * t + j + 1
                if half == 0:
                    pe.wait_ge(S["mT_done"], n)
                    if isinstance(t, int) and t == 0:
                        pe.wait_ge(S["patterns_ready"], 8)
                    wait_late(pe, "x1_done", n - 1)
                else:
                    pe.wait_ge(S["PT_done"], 2 * n - 1)
                for c in range(4):
                    for r in range(2):
                        rows, cc = head(j, half, c, r)
                        o = W[1][:, r * 512 + c * P:r * 512 + (c + 1) * P]
                        MM(o, KT[rows, cc], QT[rows, cc], start=True, stop=False, skip_group_check=True)
                        h = 4 * half + c
                        ins = MM(o, pick_row[rows, h * P:(h + 1) * P], mT[rows, j * P:(j + 1) * P], start=False, stop=True,
                                 skip_group_check=True)
                ins.then_inc(S["st_done"], 1)

            def d_pv(t, j, _):
                n = 2 * t + j + 1
                pe.wait_ge(S["PT_done"], 2 * n)
                for h in range(NH):
                    half, c, r = h // 8, h % 8 // 2, h % 2
                    g, ch = h % 4, h // 4
                    a = (j * NH + h) * HP
                    ins = MM(W[1][HP * g:HP * (g + 1), ch * P:(ch + 1) * P], v_aug[:, a:a + HP], PT[half][:, (r * 4 + c) * P:(r * 4 + c + 1) * P],
                             start=True, stop=True, skip_group_check=True)
                ins.then_inc(S["pv_done"], 1)

            def d_oT(t, j, _):
                pe.wait_ge(S["po_done"], 2 * t + j + 1)
                for ch in range(4):
                    ins = TR(W[1][:, 512 + ch * P:512 + (ch + 1) * P], po[:, ch * P:(ch + 1) * P], ident[:])
                ins.then_inc(S["oTok_done"], 1)

            def d_aT(t, j, _):
                pe.wait_ge(S["attn_done"], 2 * t + j + 1)
                for kc in range(KC):
                    ins = TR(W[1][:, kc * P:(kc + 1) * P], attn[:, kc * P:(kc + 1) * P], ident[:])
                ins.then_inc(S["oT_ps"], 1)

            def d_o(t, j, _):
                pe.wait_ge(S["oT_lo_done"], 2 * t + j + 1)
                if isinstance(t, int):
                    pe.wait_ge(S["wo_split"], 2)
                split_mm(W[1][:, 512:512 + D], [(cols(oT_hi, oT_lo, kc * P, P), cols(whi_a, wlo_a, NQ + NKV + kc * D, D))
                                                for kc in range(KC)]).then_inc(S["o_done"], 1)

            def f_T(t, _):
                pe.wait_ge(S["f_xn"], 2 * t + 2)
                transpose_pair(xn_f).then_inc(S["f_T"], 1)

            def f_up(t, c):
                if c == 0:
                    pe.wait_ge(S["f_lo"], t + 1)
                    if isinstance(t, int):
                        pe.wait_ge(S["pool_split"], 2 * EARLY_POOL)
                        pe.wait_ge(S["vec_split"], 2 * (EARLY - EARLY_POOL))
                wait_late(pe, "hf_done", NC * t + c - 1)
                for u in range(2):
                    ins = split_mm(G[c % 2][:, u * T2:(u + 1) * T2],
                                   [(cols(wgu_hi, wgu_lo, (kc * 2 + u) * INTER + c * P, P), cols(fT_hi, fT_lo, kc * T2, T2)) for kc in range(KC)])
                ins.then_inc(S["gu_done"], 1)

            def down(h, hi_sem, w, off, to, part, taken):
                def step(t, c):
                    if c == 0:
                        if to is BDN and isinstance(t, int):
                            pe.wait_ge(S["x1_done"], 2 * NP)
                        wait_late(pe, taken, t)
                    pe.wait_ge(S[hi_sem], NC * t + c + 1)
                    b = c % HB * T2
                    for j in range(2):
                        ins = split_mm(to[:, j * D:(j + 1) * D], [(cols(*h, b + j * P, P), cols(*w, off + c * D, D))],
                                       first=c == 0 and j == 0, last=c == NC - 1)
                    ins.then_inc(S[part], 1)
                return step

            def l_T(t, _):
                pe.wait_ge(S["l_xn"], 2 * t + 2)
                pe.wait_ge(S["f_lo"], min(t + 2, NP) if isinstance(t, int) else t + 2)
                transpose_pair(xn_l).then_inc(S["l_T"], 1)

            def l_sc(t, _):
                pe.wait_ge(S["lT_done"], t + 1)
                for j in range(2):
                    for kc in range(KC):
                        ins = MM(M[:, j * P:(j + 1) * P], lT[:, kc * T2 + j * P:kc * T2 + (j + 1) * P],
                                 csT[:, bass.ds(t * PW + j * D + kc * P, P)], start=kc == 0, stop=kc == KC - 1, skip_group_check=True)
                ins.then_inc(S["l_sc"], 1)

            def l_pT(t, _):
                pe.wait_ge(S["lp_done"], 2 * t + 2)
                for j in range(2):
                    ins = TR(M[:, j * P:(j + 1) * P], pl[:, j * P:(j + 1) * P], ident[:])
                ins.then_inc(S["plT_ps"], 1)

            def l_ro(t, _):
                pe.wait_ge(S["plT_done"], t + 1)
                pe.wait_ge(S["ctx_in"], 16)
                for j in range(2):
                    ins = MM(M[:, j * D:(j + 1) * D], plT[:, j * P:(j + 1) * P], cs[:, bass.ds(t * PW + j * D, D)], start=True, stop=True,
                             skip_group_check=True)
                ins.then_inc(S["ro_done"], 1)

            def r_T(t, _):
                pe.wait_ge(S["b_xn"], 2 * t + 2)
                if t == 0:
                    pe.wait_ge(S["x1_done"], 2 * NP)
                wait_late(pe, "penT_done", t)
                transpose_pair(xn_b, BR).then_inc(S["b_T"], 1)

            def r_rt(t, _):
                pe.wait_ge(S["b_lo"], t + 1)
                if isinstance(t, int):
                    pe.wait_ge(S["vec_split"], 2 * (EARLY - EARLY_POOL))
                split_mm(BR[:, 0:T2], [(cols(wr_hi, wr_lo, kc * P, P), (bT_hi[:, bass.ds(t * PW + kc * T2, T2)], bT_lo[:, bass.ds(t * PW + kc * T2, T2)]))
                                         for kc in range(KC)]).then_inc(S["rt_ps"], 1)

            def r_lT(t, _):
                wait_apart(pe, "lg_done", t + 1)
                for j in range(2):
                    ins = TR(BR[:, T2 + HP * j:T2 + HP * (j + 1)], lgT[:, j * P:(j + 1) * P], ident[0:HP, 0:HP])
                ins.then_inc(S["lgT_ps"], 1)

            def r_pT(t, _):
                pe.wait_ge(S["pen_done"], 2 * t + 2)
                for j in range(2):
                    ins = TR(BR[:, j * P // 2:(j + 1) * P // 2].bitcast(bf16), pen[:, j * P:(j + 1) * P], identb[:])
                ins.then_inc(S["penT_ps"], 1)

            def b_up(t, c):
                if c == 0:
                    pe.wait_ge(S["penT_done"], t + 1)
                    pe.wait_ge(S["pool_split"], 2 * len(OF_POOL))
                    pe.wait_ge(S["vec_split"], 2 * len(OF_VEC))
                wait_late(pe, "bf_done", NC * t + c - 1)
                o = BG[c % 2][:, 0:T2]
                split_mm(o, [(cols(w12_hi, w12_lo, kc * INTER + c * P, P),
                              (bT_hi[:, bass.ds(t * PW + kc * T2, T2)], bT_lo[:, bass.ds(t * PW + kc * T2, T2)])) for kc in range(KC)], last=False)
                MM(o, spread[:, c * P:(c + 1) * P], penT[:, pair(t, T2)], start=False, stop=True, skip_group_check=True).then_inc(S["up_done"], 1)

            run(pe, "tensor", {"A.T": a_T, "A.qkv": a_qkv, "A.qkT": a_qkT, "A.s": a_s, "A.mT": a_mT, "D.st": d_st, "D.pv": d_pv, "D.oT": d_oT,
                     "D.aT": d_aT, "D.o": d_o, "F.T": f_T, "F.up": f_up, "F.dn": down((h_hi, h_lo), "h_lo_done", (wd_hi, wd_lo), 0, DN, "dn_part", "x2_done"),
                     "L.T": l_T, "L.sc": l_sc, "L.pT": l_pT, "L.ro": l_ro,
                     "R.T": r_T, "R.rt": r_rt, "R.lT": r_lT, "R.pT": r_pT, "B.up": b_up,
                     "B.dn": down((hb_hi, hb_lo), "bh_lo", (w12_hi, w12_lo), W2O, BDN, "bdn_part", "x4_done")})


def kernel(**inputs):
    import numpy as np
    import concourse.bacc as bacc
    from concourse.bass_utils import run_bass_kernel_spmd

    def arr(n):
        return np.asarray(inputs[n])

    def chunked(wT):
        k, n = wT.shape
        return wT.reshape(k // 128, 128, n).transpose(1, 0, 2).reshape(128, -1)

    x, c = arr("x"), arr("ctx_2048")
    wr, br = arr("L1_ffn_Wr").T, arr("L1_ffn_br").reshape(-1, 1)
    data = {
        "x": x, "ctx": c,
        "ctxT": c.reshape(8, 128, 2, 128).transpose(3, 0, 2, 1).reshape(128, -1),
        "mask": arr("mask_BxS2_bk0").reshape(-1).view(np.uint32),
        "rows": np.concatenate([arr(n).reshape(-1) for n in (
            "L0_xattn_q_b", "L0_xattn_k_img_b", "L0_xattn_v_img_b", "L0_xattn_o_b", "L0_xattn_norm_q_w", "L0_xattn_norm_k_img_w",
            "g_xattn", "g_ffn")]),
        "wq": chunked(arr("L0_xattn_q_w").T),
        "wkv": chunked(np.concatenate([arr("L0_xattn_k_img_w").T, arr("L0_xattn_v_img_w").T], 1)),
        "wo": chunked(arr("L0_xattn_o_w").T),
        "wgu": chunked(arr("L0_ffn_w_gate_up").T), "wd": chunked(arr("L0_ffn_w_down").T),
        "wr": chunked(np.concatenate([wr, np.zeros((wr.shape[0], 128 - wr.shape[1]), wr.dtype)], 1)),
        "br": np.concatenate([br, np.zeros((32 - br.shape[0], 1), br.dtype)]),
        "w1": chunked(arr("L1_ffn_W1").T), "w2": chunked(arr("L1_ffn_W2").T),
    }
    nc = bacc.Bacc("TRN2", target_bir_lowering=False, num_devices=1)
    arrays, args = {}, {}
    for n, a in data.items():
        a = np.ascontiguousarray(a)
        arrays["in_" + n] = a
        args[n] = nc.dram_tensor("in_" + n, a.shape, mybir.dt.from_np(a.dtype), kind="ExternalInput").ap()
    out = nc.dram_tensor("out_x", x.shape, mybir.dt.float32, kind="ExternalOutput").ap()
    a = args
    build(nc, a["x"], a["ctx"], a["ctxT"], a["mask"], a["rows"], a["wq"], a["wkv"], a["wo"], a["wgu"], a["wd"], a["wr"], a["br"],
          a["w1"], a["w2"], out)
    r = run_bass_kernel_spmd(nc, [arrays], core_ids=[0])
    return r.results[0]["out_x"]
```
